# Optimizing a Trainium2 kernel written in Bass

```python
import numpy as np
import jax
import jax.numpy as jnp

def _softmax(x, axis=-1):
    return jax.nn.softmax(x, axis=axis)

def _gelu(x):
    return jax.nn.gelu(x, approximate=True)

def _silu(x):
    return jax.nn.silu(x)

def _sigmoid(x):
    return jax.nn.sigmoid(x)

def _layernorm(x, axis=-1, eps=1e-05):
    m = jnp.mean(x, axis=axis, keepdims=True)
    v = jnp.var(x, axis=axis, keepdims=True)
    return (x - m) / jnp.sqrt(v + eps)

def _scatter_add(tgt, idx, src, axis=0):
    return tgt.at[idx].add(src)

def _segment_sum(src, seg, n):
    return jax.ops.segment_sum(src, seg, n)
kernel_name = 'mk_recurrent_d1_jaxref_r4_06ed44'

def setup_inputs(seed: int=0):
    np.random.seed(seed)
    _w = jnp.asarray

    def _L0_attn_setup():
        import jax, jax.numpy as jnp
        import numpy as np
        import math
        B, Q, D = (2, 512, 256)
        H, R = (16, 12)
        DH = D // H
        RHO = 2.0
        MAX_OFFSET = 6.0

        def _split_heads(y):
            b, q, d = y.shape
            return y.reshape(b, q, H, DH).transpose(0, 2, 1, 3)

        def _sample(seq, pos):
            b, h, q, dh = seq.shape
            low = jnp.clip(jnp.floor(pos), 0, q - 1).astype(jnp.int32)
            high = jnp.clip(jnp.ceil(pos), 0, q - 1).astype(jnp.int32)
            frac = (pos - low.astype(pos.dtype))[..., None]
            bi = jnp.arange(b)[:, None, None, None]
            hi = jnp.arange(h)[None, :, None, None]
            gl = seq[bi, hi, low]
            gh = seq[bi, hi, high]
            return gl * (1.0 - frac) + gh * frac
        key = jax.random.key(seed)
        ks = jax.random.split(key, 16)
        s = 0.02
        inp = {'x': jax.random.normal(ks[0], (B, Q, D), dtype=jnp.float32), 'wq': jax.random.normal(ks[1], (D, D), dtype=jnp.float32) * s, 'bq': jnp.zeros((D,), jnp.float32), 'wk': jax.random.normal(ks[2], (D, D), dtype=jnp.float32) * s, 'bk': jnp.zeros((D,), jnp.float32), 'wv': jax.random.normal(ks[3], (D, D), dtype=jnp.float32) * s, 'bv': jnp.zeros((D,), jnp.float32), 'wo': jax.random.normal(ks[4], (D, D), dtype=jnp.float32) * s, 'bo': jnp.zeros((D,), jnp.float32), 'dw_w': jax.random.normal(ks[5], (D, 1, 3), dtype=jnp.float32) * s, 'dw_b': jnp.zeros((D,), jnp.float32), 'pw_w': jax.random.normal(ks[6], (H * R, D), dtype=jnp.float32) * s, 'pw_b': jnp.zeros((H * R,), jnp.float32), 'rel_scale': jnp.asarray(0.1, jnp.float32)}
        return inp
    _L0_attn_in = _L0_attn_setup()

    def _L0_ffn_setup():
        import jax, jax.numpy as jnp
        import numpy as np
        D, H, N, K = (256, 512, 8, 2)
        B, S = (4, 512)
        key = jax.random.key(seed)
        ks = jax.random.split(key, 4)
        x = jax.random.normal(ks[0], (B, S, D), dtype=jnp.float32)
        Wr = jax.random.normal(ks[1], (N, D), dtype=jnp.float32) / np.sqrt(D)
        br = jnp.zeros((N,), jnp.float32)
        Wl1 = jax.random.normal(ks[2], (N, D, 2 * H), dtype=jnp.float32) / np.sqrt(D)
        bl1 = jnp.zeros((N, 2 * H), jnp.float32)
        Wl2 = jax.random.normal(ks[3], (N, H, D), dtype=jnp.float32) / np.sqrt(H)
        bl2 = jnp.zeros((N, D), jnp.float32)
        biases_N = jnp.zeros((N,), jnp.float32)
        return {'x': x, 'Wr': Wr, 'br': br, 'Wl1': Wl1, 'bl1': bl1, 'Wl2': Wl2, 'bl2': bl2, 'biases_N': biases_N}
    _L0_ffn_in = _L0_ffn_setup()
    _d = {'L0_attn_x': _L0_attn_in['x'], 'L0_attn_wq': _L0_attn_in['wq'], 'L0_attn_bq': _L0_attn_in['bq'], 'L0_attn_wk': _L0_attn_in['wk'], 'L0_attn_bk': _L0_attn_in['bk'], 'L0_attn_wv': _L0_attn_in['wv'], 'L0_attn_bv': _L0_attn_in['bv'], 'L0_attn_wo': _L0_attn_in['wo'], 'L0_attn_bo': _L0_attn_in['bo'], 'L0_attn_dw_w': _L0_attn_in['dw_w'], 'L0_attn_dw_b': _L0_attn_in['dw_b'], 'L0_attn_pw_w': _L0_attn_in['pw_w'], 'L0_attn_pw_b': _L0_attn_in['pw_b'], 'L0_attn_rel_scale': _L0_attn_in['rel_scale'], 'L0_ffn_Wr': _L0_ffn_in['Wr'], 'L0_ffn_br': _L0_ffn_in['br'], 'L0_ffn_Wl1': _L0_ffn_in['Wl1'], 'L0_ffn_bl1': _L0_ffn_in['bl1'], 'L0_ffn_Wl2': _L0_ffn_in['Wl2'], 'L0_ffn_bl2': _L0_ffn_in['bl2'], 'L0_ffn_biases_N': _L0_ffn_in['biases_N']}
    _x0 = _d['L0_attn_x']
    _d['L0_attn_x'] = jax.random.normal(jax.random.fold_in(jax.random.key(seed), 1), (2, 4096, 256), dtype=_x0.dtype)
    del _x0
    return _d

def reference(L0_attn_x, L0_attn_wq, L0_attn_bq, L0_attn_wk, L0_attn_bk, L0_attn_wv, L0_attn_bv, L0_attn_wo, L0_attn_bo, L0_attn_dw_w, L0_attn_dw_b, L0_attn_pw_w, L0_attn_pw_b, L0_attn_rel_scale, L0_ffn_Wr, L0_ffn_br, L0_ffn_Wl1, L0_ffn_bl1, L0_ffn_Wl2, L0_ffn_bl2, L0_ffn_biases_N):

    def _L0_attn_ref(x, wq, bq, wk, bk, wv, bv, wo, bo, dw_w, dw_b, pw_w, pw_b, rel_scale):
        import jax, jax.numpy as jnp
        import numpy as np
        import math
        B, Q, D = (2, 512, 256)
        H, R = (16, 12)
        DH = D // H
        RHO = 2.0
        MAX_OFFSET = 6.0

        def _split_heads(y):
            b, q, d = y.shape
            return y.reshape(b, q, H, DH).transpose(0, 2, 1, 3)

        def _sample(seq, pos):
            b, h, q, dh = seq.shape
            low = jnp.clip(jnp.floor(pos), 0, q - 1).astype(jnp.int32)
            high = jnp.clip(jnp.ceil(pos), 0, q - 1).astype(jnp.int32)
            frac = (pos - low.astype(pos.dtype))[..., None]
            bi = jnp.arange(b)[:, None, None, None]
            hi = jnp.arange(h)[None, :, None, None]
            gl = seq[bi, hi, low]
            gh = seq[bi, hi, high]
            return gl * (1.0 - frac) + gh * frac
        b, q, d = x.shape
        q_lin = x @ wq.T + bq
        qh = _split_heads(q_lin)
        kh = _split_heads(x @ wk.T + bk)
        vh = _split_heads(x @ wv.T + bv)
        feat = q_lin.transpose(0, 2, 1)
        dw = jax.lax.conv_general_dilated(feat, dw_w, window_strides=(1,), padding=[(1, 1)], feature_group_count=D, dimension_numbers=('NCH', 'OIH', 'NCH'))
        dw = dw + dw_b[None, :, None]
        g = jax.nn.gelu(dw, approximate=False)
        off = jnp.einsum('od,bdq->boq', pw_w, g) + pw_b[None, :, None]
        off = off.transpose(0, 2, 1).reshape(b, q, H, R).transpose(0, 2, 1, 3)
        off = jnp.tanh(off) * MAX_OFFSET
        base = jnp.arange(q, dtype=x.dtype)[None, None, :, None]
        anchor = jnp.linspace(-RHO, RHO, R, dtype=x.dtype)[None, None, None, :]
        positions = jnp.clip(base + anchor + off, 0.0, q - 1.0)
        sk = _sample(kh, positions)
        sv = _sample(vh, positions)
        scores = jnp.einsum('bhqd,bhqrd->bhqr', qh, sk) / math.sqrt(DH)
        rel = positions - jnp.arange(q, dtype=x.dtype)[None, None, :, None]
        scores = scores - rel_scale * jnp.abs(rel)
        attn = jax.nn.softmax(scores, axis=-1)
        out = jnp.einsum('bhqr,bhqrd->bhqd', attn, sv)
        out = out.transpose(0, 2, 1, 3).reshape(b, q, d)
        return out @ wo.T + bo

    def _L0_ffn_ref(x, Wr, br, Wl1, bl1, Wl2, bl2, biases_N):
        import jax, jax.numpy as jnp
        import numpy as np
        D, H, N, K = (256, 512, 8, 2)
        B, S = (4, 512)
        Bb, Ss, Dd = x.shape
        scores_BSN = jnp.einsum('bsd,nd->bsn', x, Wr) + br
        w_BSN = jax.nn.softmax(scores_BSN, axis=-1)
        _, idx_BSK = jax.lax.top_k(scores_BSN + biases_N[None, None, :], K)
        val_BSK = jnp.take_along_axis(w_BSN, idx_BSK, axis=-1)
        val_BSK = val_BSK / jnp.sum(val_BSK, axis=-1, keepdims=True)
        M = Bb * Ss
        x_MD = x.reshape(M, Dd)
        idx_MK = idx_BSK.reshape(M, K)
        val_MK = val_BSK.reshape(M, K)
        h_NM2H = jnp.einsum('md,ndh->nmh', x_MD, Wl1) + bl1[:, None, :]
        a_NMH, b_NMH = (h_NM2H[..., :H], h_NM2H[..., H:])
        y_NMD = jnp.einsum('nmh,nhd->nmd', jax.nn.silu(a_NMH) * b_NMH, Wl2) + bl2[:, None, :]
        ew_MN = jnp.zeros((M, N), x.dtype)
        ew_MN = ew_MN.at[jnp.arange(M)[:, None], idx_MK].set(val_MK)
        y_MD = jnp.einsum('mn,nmd->md', ew_MN, y_NMD)
        return y_MD.reshape(Bb, Ss, Dd)
    x = L0_attn_x
    xn = _layernorm(x, axis=-1)
    s = _L0_attn_ref(xn, L0_attn_wq, L0_attn_bq, L0_attn_wk, L0_attn_bk, L0_attn_wv, L0_attn_bv, L0_attn_wo, L0_attn_bo, L0_attn_dw_w, L0_attn_dw_b, L0_attn_pw_w, L0_attn_pw_b, L0_attn_rel_scale)
    g = _silu(_L0_ffn_ref(xn, L0_ffn_Wr, L0_ffn_br, L0_ffn_Wl1, L0_ffn_bl1, L0_ffn_Wl2, L0_ffn_bl2, L0_ffn_biases_N))
    x = x + s * g
    return x

_drawn_inputs = setup_inputs


def setup_inputs(seed=0):
    import zlib

    import numpy as np

    out = dict(_drawn_inputs(seed))
    spreads = {'L0_attn_bq': (0.0, 0.8),
     'L0_attn_bk': (0.0, 0.8),
     'L0_attn_bv': (0.0, 0.8),
     'L0_attn_bo': (0.0, 0.342),
     'L0_attn_dw_b': (0.0, 0.8),
     'L0_attn_pw_b': (0.0, 0.8),
     'L0_ffn_br': (0.0, 0.8),
     'L0_ffn_bl1': (0.0, 0.8),
     'L0_ffn_bl2': (0.0, 0.8),
     'L0_ffn_biases_N': (0.0, 0.8)}
    factors = {'L0_attn_wq': 8.0,
     'L0_attn_wk': 8.0,
     'L0_attn_wv': 4.7,
     'L0_attn_wo': 3.979,
     'L0_attn_dw_w': 8.0,
     'L0_attn_pw_w': 8.0}
    for name, (base, spread) in spreads.items():
        noise = np.random.default_rng([zlib.crc32(name.encode()), seed]).standard_normal(out[name].shape)
        drawn = base * np.exp(spread * noise) if base else spread * noise
        out[name] = jnp.asarray(drawn.astype(out[name].dtype))
    for name, factor in factors.items():
        out[name] = (out[name] * factor).astype(out[name].dtype)
    return out
```

```python
from contextlib import ExitStack

import concourse.bass as bass
import numpy as np
from concourse import mybir

P = 128
F32 = mybir.dt.float32
BF16 = mybir.dt.bfloat16
I32 = mybir.dt.int32
U32 = mybir.dt.uint32
ACT = mybir.ActivationFunctionType
ALU = mybir.AluOpType
AX = mybir.AxisListType
ds = bass.ds

BATCH, SEQ, D = 2, 4096, 256
TOKENS = BATCH * SEQ
TILES = TOKENS // P
KC = D // P
HEADS, SAMPLES = 16, 12
DH = D // HEADS
HR = HEADS * SAMPLES
RHO, MAX_OFFSET = 2.0, 6.0
REACH = int(RHO + MAX_OFFSET)
LN_EPS = 1e-5

EXPERTS, HID, TOPK = 8, 512, 2
NB = 3
HC = HID // P
SLOT_TILES = TOKENS * TOPK // P + EXPERTS
SLOTS = SLOT_TILES * P

GROUP = 4
GTOK = GROUP * P
GROUPS_PER_SEQ = SEQ // GTOK

HG = 4
GH = HEADS // HG
GD = GH * DH
GR = GH * SAMPLES
RUN = TOKENS // P
IB = 16
NIB = RUN // IB
WIN = IB + 2 * REACH
TH = IB * GH
PAIRS = TH * SAMPLES
NJ = 2 * REACH + 1
KNOTS = 2 * REACH
STEPS = HG * NIB
SCALE = float(DH) ** -0.5
MOE_PER_STEP = SLOT_TILES // (STEPS + 1)
assert MOE_PER_STEP * (STEPS + 1) == SLOT_TILES


def anchors():
    step = np.arange(SAMPLES, dtype=np.float32) * np.float32(1.0 / (SAMPLES - 1))
    a = np.float32(-RHO) * (np.float32(1) - step) + np.float32(RHO) * step
    a[-1] = RHO
    return [float(v) for v in a]


class Chain:

    def __init__(self, eng, sem, base=0):
        self.eng, self.sem, self.base, self.n = eng, sem, base, 0

    def __call__(self, ins):
        self.n += 1
        ins.then_inc(self.sem, 1)
        self.eng.wait_ge(self.sem, self.base + self.n)


def project_block(nc, io, dram, keep):
    with ExitStack() as ctx:
        def sb(name, shape, dt=F32):
            return ctx.enter_context(nc.sbuf_tensor(name, shape, dt))

        def ps(name, shape, dt=F32):
            return ctx.enter_context(nc.psum_tensor(name, shape, dt))

        def sem(name):
            return ctx.enter_context(nc.semaphore(name))

        x_in = sb("x_in", [P, 2, GROUP, D])
        xn = sb("xn", [P, 2, GROUP, D])
        xnT = sb("xnT", [P, 2, KC, GTOK])
        wqkv = sb("wqkv", [P, KC, 3 * D])
        wr = sb("wr", [P, KC, EXPERTS])
        bqkv_bc = sb("bqkv_bc", [P, 3 * D])
        br_bc = sb("br_bc", [P, EXPERTS])
        bq_col = sb("bq_col", [P, KC])
        qkv = sb("qkv", [P, 2, GROUP, 3 * D])
        zeros = sb("zeros", [P, 4 * D])
        stats = sb("stats", [P, GROUP, 6])
        mv = sb("mv", [P, GROUP, 2])
        var = sb("var", [P, GROUP])
        std = sb("std", [P, GROUP])
        rstd = sb("rstd", [P, GROUP])

        pT = ps("pT", [P, KC, GTOK])
        pQ = ps("pQ", [P, KC, GTOK])
        pQK = ps("pQK", [P, 2, 512])
        pV = ps("pV", [P, 512])
        pR = ps("pR", [P, 512])

        weights_in = sem("weights_in")
        zeros_set = sem("zeros_set")
        ident_set = sem("ident_set")
        pads_set = sem("pads_set")
        x_loaded = [sem(f"x_loaded{u}") for u in range(2)]
        xn_ready = sem("xn_ready")
        xn_stored = [sem(f"xn_stored{u}") for u in range(2)]
        var_ready = sem("var_ready")
        std_ready = sem("std_ready")
        xT_done = sem("xT_done")
        xnT_ready = sem("xnT_ready")
        qT_done = sem("qT_done")
        r_done = sem("r_done")
        r_free = sem("r_free")
        qk_done = sem("qk_done")
        qk_free = sem("qk_free")
        v_done = sem("v_done")
        v_free = sem("v_free")
        qkv_stored = [sem(f"qkv_stored{u}") for u in range(2)]
        filled = sem("filled")
        go = sem("go1")
        ln_chain = sem("ln_chain")
        QKV_STORES = 3 * HG

        block = ctx.enter_context(nc.Block())

        @block.sync
        def _(sp):
            def load_x(t, u):
                sp.dma_start(x_in[:, u], io["x"][ds(u * SEQ + t * GTOK, GTOK), :].rearrange(
                    "(a p) c -> p a c", p=P)).then_inc(x_loaded[u], 16)

            def store_xn(t, u):
                sp.wait_ge(xn_ready, 2 * t + u + 1)
                sp.dma_start(dram["xn"][ds(u * SEQ + t * GTOK, GTOK), :].rearrange("(a p) c -> p a c", p=P),
                             xn[:, u]).then_inc(xn_stored[u], 16)

            def store_qkv(t, u):
                sp.wait_ge(v_free, (2 * t + u + 1) * GROUP + 1)
                for w, name, pad in ((0, "q", 0), (1, "k", REACH), (2, "v", REACH)):
                    for hg in range(HG):
                        dst = dram[name][hg, ds(pad + u * SEQ + t * GTOK, GTOK), :]
                        sp.dma_start(dst.rearrange("(a p) c -> p a c", p=P),
                                     qkv[:, u, :, w * D + hg * GD:w * D + (hg + 1) * GD]).then_inc(qkv_stored[u], 16)

            load_x(0, 0)
            load_x(0, 1)
            with sp.Fori(0, GROUPS_PER_SEQ - 1) as t:
                for u in range(2):
                    store_xn(t, u)
                    load_x(t + 1, u)
                for u in range(2):
                    store_qkv(t, u)
            for u in range(2):
                store_xn(GROUPS_PER_SEQ - 1, u)
            for u in range(2):
                store_qkv(GROUPS_PER_SEQ - 1, u)
            sp.wait_ge(pads_set, 16 * 4 * HG)
            sp.wait_ge(filled, 16 * (SLOTS // (4 * P)))
            for u in range(2):
                sp.wait_ge(xn_stored[u], 16 * GROUPS_PER_SEQ + 16)
                sp.wait_ge(qkv_stored[u], 16 * QKV_STORES * (GROUPS_PER_SEQ + 1))

        @block.gpsimd
        def _(pool):
            nc.gpsimd.memset(zeros[:], 0.0).then_inc(zeros_set, 1)
            nc.gpsimd.memset(keep["ident"][:], 0.0).then_inc(zeros_set, 1)
            pool.wait_ge(zeros_set, 2)
            nc.gpsimd.affine_select(out=keep["ident"][:], in_=keep["ident"][:], compare_op=ALU.not_equal, fill=1.0,
                                    base=0, pattern=[[-1, P]], channel_multiplier=1).then_inc(ident_set, 1)
            for name in ("k", "v"):
                for hg in range(HG):
                    for row in (0, REACH + TOKENS):
                        pool.dma_start(dram[name][hg, row:row + REACH, :], zeros[0:REACH, 0:GD]).then_inc(pads_set, 16)
            with pool.Fori(0, SLOTS // (4 * P)) as n:
                pool.dma_start(dram["xs"][ds(n * 4 * P, 4 * P), :].rearrange("(p a) c -> p (a c)", p=P),
                               zeros[:]).then_inc(filled, 16)

        @block.scalar
        def _(act):
            act.dma_start(wqkv[:], io["w_qkvT"].rearrange("(k p) n -> p k n", p=P)).then_inc(weights_in, 16)
            act.dma_start(wr[:], io["w_rT"].rearrange("(k p) n -> p k n", p=P)).then_inc(weights_in, 16)
            act.dma_start(bqkv_bc[:], io["b_qkv"].partition_broadcast(P)).then_inc(weights_in, 16)
            act.dma_start(br_bc[:], io["b_r"].partition_broadcast(P)).then_inc(weights_in, 16)
            act.dma_start(bq_col[:], io["b_qkv"][0:D].rearrange("(k p) -> p k", p=P),
                          allow_slow_non_contiguous=True).then_inc(weights_in, 16)
            act.wait_ge(weights_in, 80)

            def group(t, u):
                n = 2 * t + u
                act.wait_ge(xT_done, n + 1)
                nc.scalar.activation(xnT[:, u], pT[:], ACT.Identity).then_inc(xnT_ready, 1)
                act.wait_ge(qT_done, n + 1)
                for c in range(KC):
                    nc.scalar.activation(keep["qT"][:, c, ds(u * (SEQ + 2) + 1 + t * GTOK, GTOK)], pQ[:, c],
                                         ACT.Identity, bias=bq_col[:, c:c + 1])

            def root(t, u):
                act.wait_ge(var_ready, 2 * t + u + 1)
                nc.scalar.activation(std[:], var[:], ACT.Sqrt).then_inc(std_ready, 1)

            root(0, 0)
            with act.Fori(0, GROUPS_PER_SEQ - 1) as t:
                root(t, 1)
                group(t, 0)
                root(t + 1, 0)
                group(t, 1)
            last = GROUPS_PER_SEQ - 1
            root(last, 1)
            group(last, 0)
            group(last, 1)

        @block.tensor
        def _(pe):
            pe.wait_ge(weights_in, 80)
            pe.wait_ge(ident_set, 1)

            def group(t, u):
                n = 2 * t + u
                pe.wait_ge(xn_ready, n + 1)
                for a in range(GROUP):
                    for c in range(KC):
                        tr = nc.tensor.transpose(pT[:, c, a * P:(a + 1) * P], xn[:, u, a, c * P:(c + 1) * P],
                                                 keep["ident"][:])
                tr.then_inc(xT_done, 1)
                pe.wait_ge(xnT_ready, n + 1)
                for o in range(KC):
                    for c in range(KC):
                        mm = nc.tensor.matmul(pQ[:, o], wqkv[:, c, o * P:(o + 1) * P], xnT[:, u, c],
                                              start=(c == 0), stop=(c == KC - 1))
                mm.then_inc(qT_done, 1)
                pe.wait_ge(r_free, n + 1)
                for a in range(GROUP):
                    for c in range(KC):
                        mm = nc.tensor.matmul(pR[:, a * EXPERTS:(a + 1) * EXPERTS], xnT[:, u, c, a * P:(a + 1) * P],
                                              wr[:, c], start=(c == 0), stop=(c == KC - 1))
                mm.then_inc(r_done, 1)
                for a in range(GROUP):
                    m = n * GROUP + a
                    pe.wait_ge(qk_free, m + 1)
                    for c in range(KC):
                        mm = nc.tensor.matmul(pQK[:, a % 2], xnT[:, u, c, a * P:(a + 1) * P], wqkv[:, c, 0:2 * D],
                                              start=(c == 0), stop=(c == KC - 1))
                    mm.then_inc(qk_done, 1)
                    pe.wait_ge(v_free, m + 1)
                    for c in range(KC):
                        mm = nc.tensor.matmul(pV[:, 0:D], xnT[:, u, c, a * P:(a + 1) * P], wqkv[:, c, 2 * D:3 * D],
                                              start=(c == 0), stop=(c == KC - 1))
                    mm.then_inc(v_done, 1)

            with pe.Fori(0, GROUPS_PER_SEQ) as t:
                group(t, 0)
                group(t, 1)

        @block.vector
        def _(dve):
            for u in range(2):
                dve.sem_inc(xn_stored[u], 16)
                dve.sem_inc(qkv_stored[u], 16 * QKV_STORES)
            dve.sem_inc(r_free, 1)
            dve.sem_inc(qk_free, 2)
            dve.sem_inc(v_free, 1)
            for b in range(BATCH):
                for col in (b * (SEQ + 2), b * (SEQ + 2) + SEQ + 1):
                    nc.vector.memset(keep["qT"][:, :, col:col + 1], 0.0)
            dve.wait_ge(weights_in, 80)
            CHAIN = 7

            def layernorm(t, u):
                chain = Chain(dve, ln_chain, (2 * t + u) * CHAIN)
                dve.wait_ge(x_loaded[u], 16 * t + 16)
                dve.wait_ge(xn_stored[u], 16 * t + 16)
                for a in range(GROUP):
                    ins = nc.vector.bn_stats(stats[:, a], x_in[:, u, a])
                chain(ins)
                dve.sem_inc(go, 1)
                for a in range(GROUP):
                    ins = nc.vector.bn_aggr(mv[:, a], stats[:, a])
                chain(ins)
                V = nc.vector
                V.tensor_scalar(var[:], mv[:, :, 1], LN_EPS, None, ALU.add).then_inc(var_ready, 1)
                dve.wait_ge(std_ready, 2 * t + u + 1)
                chain(V.reciprocal(rstd[:], std[:]))
                chain(V.tensor_tensor(std[:], rstd[:], rstd[:], ALU.mult))
                chain(V.tensor_tensor(std[:], std[:], var[:], ALU.mult))
                chain(V.tensor_scalar(std[:], std[:], -0.5, 1.5, ALU.mult, ALU.add))
                chain(V.tensor_tensor(rstd[:], rstd[:], std[:], ALU.mult))
                for a in range(GROUP):
                    ins = nc.vector.tensor_scalar(xn[:, u, a], x_in[:, u, a], mv[:, a, 0:1], rstd[:, a:a + 1],
                                                  ALU.subtract, ALU.mult)
                ins.then_inc(xn_ready, 1)

            def evacuate(t, u):
                n = 2 * t + u
                dve.wait_ge(r_done, n + 1)
                nc.vector.tensor_tensor(
                    keep["scores"][:, ds((u * GROUPS_PER_SEQ + t) * GROUP, GROUP), :],
                    pR[:, 0:GROUP * EXPERTS].rearrange("p (a e) -> p a e", a=GROUP),
                    br_bc[:, None, :].broadcast_to([P, GROUP, EXPERTS]), ALU.add).then_inc(r_free, 1)
                dve.wait_ge(qkv_stored[u], 16 * QKV_STORES * t + 16 * QKV_STORES)
                for a in range(GROUP):
                    m = n * GROUP + a
                    dve.wait_ge(qk_done, m + 1)
                    nc.vector.tensor_tensor(qkv[:, u, a, 0:2 * D], pQK[:, a % 2], bqkv_bc[:, 0:2 * D],
                                            ALU.add).then_inc(qk_free, 1)
                    dve.wait_ge(v_done, m + 1)
                    ins = nc.vector.tensor_tensor(qkv[:, u, a, 2 * D:3 * D], pV[:, 0:D], bqkv_bc[:, 2 * D:3 * D], ALU.add)
                    ins.then_inc(v_free, 1)

            layernorm(0, 0)
            with dve.Fori(0, GROUPS_PER_SEQ - 1) as t:
                layernorm(t, 1)
                evacuate(t, 0)
                layernorm(t + 1, 0)
                evacuate(t, 1)
            last = GROUPS_PER_SEQ - 1
            layernorm(last, 1)
            evacuate(last, 0)
            evacuate(last, 1)


def route_block(nc, io, dram, keep):
    with ExitStack() as ctx:
        def sb(name, shape, dt=F32):
            return ctx.enter_context(nc.sbuf_tensor(name, shape, dt))

        def ps(name, shape, dt=F32):
            return ctx.enter_context(nc.psum_tensor(name, shape, dt))

        def sem(name):
            return ctx.enter_context(nc.semaphore(name))

        TE = [P, TILES, EXPERTS]
        sel_bias = sb("sel_bias", [P, EXPERTS])
        e_first = sb("e_first", [P, EXPERTS])
        biased = sb("biased", TE)
        top = sb("top", [P, TILES])
        is_top = sb("is_top", TE)
        chosen = [sb(f"chosen{k}", TE) for k in range(TOPK)]
        expw = sb("expw", TE)
        prod = sb("prod", TE)
        picked = sb("picked", [P, TOPK, TILES])
        count = sb("count", TE)
        zero_te = sb("zero_te", [P, TILES])
        upto = sb("upto", TE)
        total = sb("total", [P, EXPERTS])
        below = sb("below", [P, P])
        ones = sb("ones", [P, P])
        rows_i = sb("rows_i", [P, EXPERTS], I32)
        rows = sb("rows", [P, EXPERTS])
        ends = sb("ends", [P, EXPERTS])
        start = sb("start", [P, EXPERTS])
        rank = sb("rank", TE)
        slot = sb("slot", [P, TOPK, TILES])
        tile_row = sb("tile_row", [1, SLOT_TILES])
        tile_exp = sb("tile_exp", [1, SLOT_TILES])

        xrow = sb("xrow", [P, 2, D])
        idx = sb("idx", [P, 2, TOPK], U32)
        dw_w = sb("dw_w", [P, KC, 3])
        dw_b = sb("dw_b", [P, KC])
        pw_w = sb("pw_w", [P, KC, HR])
        pw_b = sb("pw_b", [P, HR])
        anchor = sb("anchor", [P, HEADS, SAMPLES])
        base_i = sb("base_i", [P, SEQ // P], I32)
        base = sb("base", [P, SEQ // P])
        conv = sb("conv", [P, 2, KC, GTOK])
        gel = sb("gel", [P, 2, KC, GTOK])
        off = sb("off", [P, 2, GROUP, HR])
        tanhs = sb("tanhs", [P, 2, GROUP, HR])
        pos = sb("pos", [P, 2, GROUP, HR])

        bias_in = sb("bias_in", [EXPERTS, 2 * HID + D])
        bias_part = sb("bias_part", [EXPERTS, NB, 2 * HID + D], BF16)

        pCount = ps("pCount", [P, 512])
        pOff = ps("pOff", [P, 2, GROUP, 256])

        bias_loaded = sem("bias_loaded")
        bias_ready = sem("bias_ready")
        bias_stored = sem("bias_stored")
        weights_in = sem("weights_in2")
        consts = sem("consts2")
        totals_ready = sem("totals_ready")
        prefix_ready = sem("prefix_ready")
        exp_in = sem("exp_in")
        exp_out = sem("exp_out")
        slots_ready = sem("slots_ready")
        chain_sem = sem("route_chain")
        xrow_loaded = [sem(f"xrow_loaded{u}") for u in range(2)]
        scattered = [sem(f"scattered{u}") for u in range(2)]
        idx_set = sem("idx_set")
        go = sem("go")
        conv_mid = sem("conv_mid")
        conv_done = sem("conv_done")
        gel_ready = sem("gel_ready")
        off_done = sem("off_done")
        off_ready = sem("off_ready")
        tanh_ready = sem("tanh_ready")
        pos_chain = sem("pos_chain")
        pos_ready = sem("pos_ready")
        pos_stored = [sem(f"pos_stored{u}") for u in range(2)]

        block = ctx.enter_context(nc.Block())

        @block.gpsimd
        def _(pool):
            nc.gpsimd.memset(ones[:], 1.0).then_inc(consts, 1)
            pool.wait_ge(consts, 1)
            nc.gpsimd.affine_select(out=below[:], in_=ones[:], compare_op=ALU.is_gt, fill=0.0, base=0,
                                    pattern=[[1, P]], channel_multiplier=-1).then_inc(consts, 1)
            nc.gpsimd.iota(rows_i[:], pattern=[[-1, EXPERTS]], base=EXPERTS, channel_multiplier=0).then_inc(consts, 1)
            nc.gpsimd.iota(base_i[:], pattern=[[P, SEQ // P]], base=0, channel_multiplier=1).then_inc(consts, 1)
            nc.gpsimd.iota(keep["tile_exp"][:], pattern=[[P, SLOT_TILES]], base=0, channel_multiplier=0).then_inc(consts, 1)
            pool.sem_inc(go, 1)
            pool.wait_ge(slots_ready, 1)

            def scatter(t, u):
                pool.wait_ge(xrow_loaded[u], 16 * t + 16)
                pool.sem_inc(go, 1)
                for k in range(TOPK):
                    nc.gpsimd.tensor_copy(idx[:, u, k:k + 1], keep["slot"][:, k, ds(2 * t + u, 1)]).then_inc(idx_set, 1)
                pool.wait_ge(idx_set, (2 * t + u + 1) * TOPK)
                pool.sem_inc(go, 1)
                for k in range(TOPK):
                    nc.gpsimd.indirect_dma_start(
                        out=dram["xs"], out_offset=bass.IndirectOffsetOnAxis(ap=idx[:, u, k:k + 1], axis=0),
                        in_=xrow[:, u], in_offset=None).then_inc(scattered[u], 16)

            scatter(0, 0)
            scatter(0, 1)
            with pool.Fori(1, TILES // 2) as t:
                for u in range(2):
                    pool.wait_ge(scattered[u], 16 * TOPK * t)
                    scatter(t, u)
            for u in range(2):
                pool.wait_ge(scattered[u], 16 * TOPK * (TILES // 2))

        @block.sync
        def _(sp):
            sp.dma_start(bias_in[:, 0:2 * HID], io["b_l1"]).then_inc(bias_loaded, 16)
            sp.dma_start(bias_in[:, 2 * HID:], io["b_l2"]).then_inc(bias_loaded, 16)
            sp.dma_start(sel_bias[:], io["sel_bias"].partition_broadcast(P)).then_inc(weights_in, 16)
            sp.dma_start(dw_w[:], io["dw_w"].rearrange("(k p) n -> p k n", p=P)).then_inc(weights_in, 16)
            sp.dma_start(dw_b[:], io["dw_b"].rearrange("(k p) -> p k", p=P),
                         allow_slow_non_contiguous=True).then_inc(weights_in, 16)
            sp.dma_start(pw_w[:], io["pw_wT"].rearrange("(k p) n -> p k n", p=P)).then_inc(weights_in, 16)
            sp.dma_start(pw_b[:], io["pw_b"].partition_broadcast(P)).then_inc(weights_in, 16)

            sp.wait_ge(bias_ready, 1)
            sp.dma_start(dram["bias"].rearrange("k e n -> e k n"), bias_part[:]).then_inc(bias_stored, 16)
            PAIRS_PER_GROUP = TILES // 2 // GROUPS_PER_SEQ

            def load_row(n, u):
                sp.dma_start(xrow[:, u], dram["xn"][ds((2 * n + u) * P, P), :]).then_inc(xrow_loaded[u], 16)

            def group(t, pairs):
                for m in range(pairs):
                    n = t * PAIRS_PER_GROUP + m
                    for u in range(2):
                        sp.wait_ge(scattered[u], 16 * TOPK * (n + 1))
                        load_row(n + 1, u)
                for u in range(2):
                    sp.wait_ge(pos_ready, 2 * t + u + 1)
                    for hg in range(HG):
                        sp.dma_start(
                            dram["pos"][hg, ds(u * SEQ + t * GTOK, GTOK), :].rearrange("(a p) c -> p a c", p=P),
                            pos[:, u, :, hg * GR:(hg + 1) * GR]).then_inc(pos_stored[u], 16)

            load_row(0, 0)
            load_row(0, 1)
            with sp.Fori(0, GROUPS_PER_SEQ - 1) as t:
                group(t, PAIRS_PER_GROUP)
            group(GROUPS_PER_SEQ - 1, PAIRS_PER_GROUP - 1)
            sp.wait_ge(bias_stored, 16)
            for u in range(2):
                sp.wait_ge(pos_stored[u], 16 * HG * (GROUPS_PER_SEQ + 1))

        @block.scalar
        def _(act):
            act.wait_ge(exp_in, 1)
            nc.scalar.activation(expw[:], prod[:], ACT.Exp).then_inc(exp_out, 1)
            act.wait_ge(weights_in, 80)

            def group(t, u):
                n = 2 * t + u
                col = u * (SEQ + 2) + 1 + t * GTOK
                for c in range(KC):
                    nc.scalar.activation(conv[:, u, c], keep["qT"][:, c, ds(col, GTOK)], ACT.Identity,
                                         bias=dw_b[:, c:c + 1], scale=dw_w[:, c, 1:2]).then_inc(conv_mid, 1)
                act.wait_ge(conv_done, n + 1)
                nc.scalar.activation(gel[:, u], conv[:, u], ACT.Gelu).then_inc(gel_ready, 1)
                act.wait_ge(off_ready, n + 1)
                nc.scalar.activation(tanhs[:, u], off[:, u], ACT.Tanh).then_inc(tanh_ready, 1)

            with act.Fori(0, GROUPS_PER_SEQ) as t:
                group(t, 0)
                group(t, 1)

        @block.tensor
        def _(pe):
            pe.wait_ge(totals_ready, 1)
            pe.wait_ge(consts, 2)
            nc.tensor.matmul(pCount[:, 0:EXPERTS], below[:], total[:], start=True, stop=True)
            nc.tensor.matmul(pCount[:, EXPERTS:2 * EXPERTS], ones[:], total[:], start=True,
                             stop=True).then_inc(prefix_ready, 1)
            pe.wait_ge(weights_in, 80)

            def group(t, u):
                n = 2 * t + u
                pe.wait_ge(gel_ready, n + 1)
                for a in range(GROUP):
                    for c in range(KC):
                        mm = nc.tensor.matmul(pOff[:, u, a, 0:HR], gel[:, u, c, a * P:(a + 1) * P], pw_w[:, c],
                                              start=(c == 0), stop=(c == KC - 1))
                mm.then_inc(off_done, 1)

            with pe.Fori(0, GROUPS_PER_SEQ) as t:
                group(t, 0)
                group(t, 1)

        @block.vector
        def _(dve):
            V = nc.vector

            def per_expert(ap):
                return ap.unsqueeze(2).broadcast_to(TE)

            def per_tile(ap):
                return ap[:, None, :].broadcast_to(TE)

            chain = Chain(dve, chain_sem)
            scores = keep["scores"]
            for u in range(2):
                dve.sem_inc(pos_stored[u], 16 * HG)
            for r, a in enumerate(anchors()):
                V.memset(anchor[:, :, r:r + 1], a)
            V.memset(zero_te[:], 0.0)
            dve.wait_ge(consts, 5)
            V.tensor_copy(e_first[:], rows_i[:])
            V.tensor_copy(tile_row[:], keep["tile_exp"][:])
            chain(V.tensor_copy(base[:], base_i[:]))
            dve.wait_ge(weights_in, 80)
            chain(V.tensor_reduce(top[:], scores[:], AX.X, ALU.max))
            V.tensor_tensor(prod[:], scores[:], per_expert(top[:]), ALU.subtract).then_inc(exp_in, 1)
            chain(V.tensor_tensor(biased[:], scores[:], per_tile(sel_bias[:]), ALU.add))
            for k in range(TOPK):
                chain(V.tensor_reduce(top[:], biased[:], AX.X, ALU.max))
                chain(V.tensor_tensor(is_top[:], biased[:], per_expert(top[:]), ALU.is_equal))
                chain(V.tensor_tensor(is_top[:], is_top[:], per_tile(e_first[:]), ALU.mult))
                chain(V.tensor_reduce(top[:], is_top[:], AX.X, ALU.max))
                chain(V.tensor_tensor(chosen[k][:], per_tile(e_first[:]), per_expert(top[:]), ALU.is_equal))
                if k == 0:
                    chain(V.scalar_tensor_tensor(biased[:].rearrange("p t e -> p (t e)"),
                                                 chosen[0][:].rearrange("p t e -> p (t e)"), -3.0e38,
                                                 biased[:].rearrange("p t e -> p (t e)"), ALU.mult, ALU.add))
            dve.wait_ge(exp_out, 1)
            for k in range(TOPK):
                chain(V.tensor_tensor(prod[:], expw[:], chosen[k][:], ALU.mult))
                chain(V.tensor_reduce(picked[:, k], prod[:], AX.X, ALU.add))
            chain(V.tensor_tensor(top[:], picked[:, 0], picked[:, 1], ALU.add))
            chain(V.reciprocal(top[:], top[:]))
            for k in range(TOPK):
                V.tensor_tensor(keep["gate"][:, k], picked[:, k], top[:], ALU.mult)
            chain(V.tensor_tensor(count[:], chosen[0][:], chosen[1][:], ALU.add))
            for e in range(EXPERTS):
                ins = V.tensor_tensor_scan(upto[:, :, e], count[:, :, e], zero_te[:], 0.0, ALU.add, ALU.add)
            chain(ins)
            V.tensor_copy(total[:], upto[:, TILES - 1, :]).then_inc(totals_ready, 1)
            chain(V.tensor_tensor(rank[:], upto[:], count[:], ALU.subtract))
            dve.wait_ge(prefix_ready, 1)
            chain(V.tensor_scalar(rows_i[:], pCount[:, EXPERTS:2 * EXPERTS], float(P - 1), None, ALU.add))
            shift = P.bit_length() - 1
            chain(V.tensor_scalar(rows_i[:], rows_i[:], shift, shift, ALU.logical_shift_right, ALU.logical_shift_left))
            chain(V.tensor_copy(rows[:], rows_i[:]))
            chain(V.tensor_tensor_scan(ends[:], rows[:], zero_te[:, 0:EXPERTS], 0.0, ALU.add, ALU.add))
            chain(V.tensor_tensor(start[:], ends[:], rows[:], ALU.subtract))
            chain(V.tensor_tensor(start[:], start[:], pCount[:, 0:EXPERTS], ALU.add))
            chain(V.tensor_tensor(rank[:], rank[:], per_tile(start[:]), ALU.add))
            for k in range(TOPK):
                chain(V.tensor_tensor(prod[:], rank[:], chosen[k][:], ALU.mult))
                chain(V.tensor_reduce(slot[:, k], prod[:], AX.X, ALU.add))
            V.tensor_copy(keep["slot"][:], slot[:]).then_inc(slots_ready, 1)
            chain(V.tensor_scalar(tile_exp[:], tile_row[:], ends[0:1, 0:1], None, ALU.is_ge))
            for e in range(1, EXPERTS - 1):
                chain(V.scalar_tensor_tensor(tile_exp[:], tile_row[:], ends[0:1, e:e + 1], tile_exp[:],
                                             ALU.is_ge, ALU.add))
            V.tensor_copy(keep["tile_exp"][:], tile_exp[:])

            dve.wait_ge(bias_loaded, 32)
            for k in range(NB):
                chain(V.tensor_copy(bias_part[:, k], bias_in[:]))
                if k < NB - 1:
                    chain(V.tensor_tensor(bias_in[:], bias_in[:], bias_part[:, k], ALU.subtract))
            dve.sem_inc(bias_ready, 1)
            CHAIN = 5

            def group(t, u):
                n = 2 * t + u
                col = u * (SEQ + 2) + 1 + t * GTOK
                dve.wait_ge(conv_mid, KC * (n + 1))
                pc = Chain(dve, pos_chain, n * CHAIN)
                for c in range(KC):
                    ins = V.scalar_tensor_tensor(conv[:, u, c], keep["qT"][:, c, ds(col - 1, GTOK)], dw_w[:, c, 0:1],
                                                 conv[:, u, c], ALU.mult, ALU.add)
                pc(ins)
                for c in range(KC):
                    ins = V.scalar_tensor_tensor(conv[:, u, c], keep["qT"][:, c, ds(col + 1, GTOK)], dw_w[:, c, 2:3],
                                                 conv[:, u, c], ALU.mult, ALU.add)
                ins.then_inc(conv_done, 1)
                dve.wait_ge(off_done, n + 1)
                V.tensor_tensor(off[:, u], pOff[:, u, :, 0:HR], pw_b[:, None, :].broadcast_to([P, GROUP, HR]),
                                ALU.add).then_inc(off_ready, 1)
                dve.wait_ge(tanh_ready, n + 1)
                dve.wait_ge(pos_stored[u], 16 * HG * t + 16 * HG)
                pc(V.tensor_scalar(off[:, u], tanhs[:, u], MAX_OFFSET, None, ALU.mult))
                for a in range(GROUP):
                    tile = t * GROUP + a
                    ins = V.scalar_tensor_tensor(pos[:, u, a], anchor[:].rearrange("p h r -> p (h r)"),
                                                 base[:, ds(tile, 1)], off[:, u, a], ALU.add, ALU.add)
                pc(ins)
                pc(V.tensor_scalar(pos[:, u], pos[:, u], 0.0, float(SEQ - 1), ALU.max, ALU.min))
                for a in range(GROUP):
                    tile = t * GROUP + a
                    ins = V.tensor_scalar(pos[:, u, a], pos[:, u, a], base[:, ds(tile, 1)], None, ALU.subtract)
                pc(ins)
                dve.sem_inc(pos_ready, 1)

            with dve.Fori(0, GROUPS_PER_SEQ) as t:
                group(t, 0)
                group(t, 1)


def mix_block(nc, io, dram, keep):
    with ExitStack() as ctx:
        def sb(name, shape, dt=F32):
            return ctx.enter_context(nc.sbuf_tensor(name, shape, dt))

        def ps(name, shape, dt=F32):
            return ctx.enter_context(nc.psum_tensor(name, shape, dt))

        def sem(name):
            return ctx.enter_context(nc.semaphore(name))

        w1 = sb("w1", [P, KC, EXPERTS * 2 * HID])
        w2 = sb("w2", [P, HC, EXPERTS * D])
        b1 = sb("b1", [NB, EXPERTS * 2 * HID], BF16)
        b2 = sb("b2", [NB, EXPERTS * D], BF16)
        ones3 = sb("ones3", [NB, P], BF16)
        xs = sb("xs", [P, 2, D])
        xsT = sb("xsT", [P, KC, P])
        act_a = sb("act_a", [P, HID])
        hid = sb("hid", [P, HID])
        hidT = sb("hidT", [P, HC, P])
        ys = sb("ys", [P, 2, D])
        qw = sb("qw", [P, IB * GD])
        kw = sb("kw", [P, WIN * GD])
        vw = sb("vw", [P, WIN * GD])
        pos = sb("posw", [P, PAIRS])
        prods = sb("prods", [P, 2, TH * DH])
        S = sb("S", [P, NJ, TH])
        bend = sb("bend", [P, KNOTS, TH])
        last = sb("last", [P, TH])
        terms = sb("terms", [P, 4, PAIRS])
        shifted = sb("shifted", [P, PAIRS])
        rel = sb("rel", [P, 1])
        rel_eye = sb("rel_eye", [P, P])
        smax = sb("smax", [P, TH])
        prob = sb("prob", [P, PAIRS])
        psum_e = sb("psum_e", [P, TH])
        G = sb("G", [P, KNOTS, TH])
        slope = sb("slope", [P, KNOTS + 2, TH])
        wgt = sb("wgt", [P, NJ, TH])
        outs = sb("outs", [P, TH * DH])

        pX = ps("pX", [P, 512])
        pA = ps("pA", [P, 512])
        pB = ps("pB", [P, 512])
        pH = ps("pH", [P, 512])
        pY = ps("pY", [P, 512])
        pS = ps("pS", [P, 2, 512])
        pG = ps("pG", [P, 512])

        w_loaded = sem("w_loaded")
        b_loaded = sem("b_loaded")
        ones_set = sem("ones_set")
        rel_ready = sem("rel_ready")
        rel_eye_set = sem("rel_eye_set")
        dist_ready = sem("dist_ready")
        xs_loaded = [sem(f"xs_loaded{u}") for u in range(2)]
        xsT_done = sem("xsT_done")
        xsT_ready = sem("xsT_ready")
        h_done = sem("h_done")
        a_ready = sem("a_ready")
        hid_ready = sem("hid_ready")
        hidT_done = sem("hidT_done")
        hidT_ready = sem("hidT_ready")
        y_done = sem("y_done")
        ys_ready = sem("ys_ready")
        ys_stored = [sem(f"ys_stored{u}") for u in range(2)]

        in_loaded = sem("in_loaded")
        in_free = sem("in_free")
        prod_ready = sem("prod_ready")
        prod_free = sem("prod_free")
        term_ready = sem("term_ready")
        term_free = sem("term_free")
        score_done = sem("score_done")
        shift_ready = sem("shift_ready")
        prob_ready = sem("prob_ready")
        g_ready = sem("g_ready")
        out_prod = sem("out_prod")
        out_prod_free = sem("out_prod_free")
        outs_stored = sem("outs_stored")
        chain_sem = sem("attn_chain")
        go = sem("go3")

        block = ctx.enter_context(nc.Block())

        @block.sync
        def _(sp):
            sp.dma_start(b1[:].rearrange("o (e n) -> o e n", e=EXPERTS), dram["bias"][:, :, 0:2 * HID]).then_inc(b_loaded, 16)
            sp.dma_start(b2[:].rearrange("o (e n) -> o e n", e=EXPERTS), dram["bias"][:, :, 2 * HID:]).then_inc(b_loaded, 16)
            sp.dma_start(rel[:], io["rel_scale"].partition_broadcast(P)).then_inc(rel_ready, 16)

            def load_xs(n, u):
                sp.dma_start(xs[:, u], dram["xs"][ds((2 * n + u) * P, P), :]).then_inc(xs_loaded[u], 16)

            def store_ys(n, u):
                sp.wait_ge(ys_ready, 2 * n + u + 1)
                sp.dma_start(dram["ys"][ds((2 * n + u) * P, P), :], ys[:, u]).then_inc(ys_stored[u], 16)

            def moe_io(n, more=True):
                for u in range(2):
                    store_ys(n, u)
                    if more:
                        load_xs(n + 1, u)

            def step_loads(hg, ib, it):
                sp.wait_ge(in_free, it + 1)
                row = ib * IB
                sp.dma_start(qw[:].rearrange("p (i c) -> p i c", i=IB),
                             dram["q"][hg].rearrange("(p i) c -> p i c", p=P)[:, ds(row, IB), :]).then_inc(in_loaded, 16)
                for name, win in (("k", kw), ("v", vw)):
                    sp.dma_start(win[:].rearrange("p (i c) -> p i c", i=WIN),
                                 bass.AP(dram[name].tensor, (hg * (TOKENS + 2 * REACH) + row) * GD,
                                         [[RUN * GD, P], [GD, WIN], [1, GD]])).then_inc(in_loaded, 16)
                sp.dma_start(pos[:].rearrange("p (i c) -> p i c", i=IB),
                             dram["pos"][hg].rearrange("(p i) c -> p i c", p=P)[:, ds(row, IB), :]).then_inc(in_loaded, 16)

            load_xs(0, 0)
            load_xs(0, 1)
            with sp.Fori(0, HG) as hg:
                for ib in range(NIB):
                    it = hg * NIB + ib
                    step_loads(hg, ib, it)
                    for m in range(MOE_PER_STEP // 2):
                        moe_io(it * (MOE_PER_STEP // 2) + m)
                    sp.wait_ge(out_prod_free, (it + 1) * NJ + 2)
                    sp.dma_start(dram["attn"].rearrange("(p i) c -> p i c", p=P)[:, ib * IB:(ib + 1) * IB, ds(hg * GD, GD)],
                                 outs[:].rearrange("p (i c) -> p i c", i=IB)).then_inc(outs_stored, 16)
            for m in range(MOE_PER_STEP // 2):
                moe_io(STEPS * (MOE_PER_STEP // 2) + m, m < MOE_PER_STEP // 2 - 1)
            sp.wait_ge(outs_stored, 16 * (STEPS + 1))
            for u in range(2):
                sp.wait_ge(ys_stored[u], 16 * (SLOT_TILES // 2 + 1))

        @block.gpsimd
        def _(pool):
            for k in range(KC):
                pool.dma_start(w1[:, k].rearrange("p (e n) -> p e n", e=EXPERTS),
                               io["w_l1"].rearrange("e (k p) n -> k p e n", p=P)[k]).then_inc(w_loaded, 16)
            for k in range(HC):
                pool.dma_start(w2[:, k].rearrange("p (e n) -> p e n", e=EXPERTS),
                               io["w_l2"].rearrange("e (k p) n -> k p e n", p=P)[k]).then_inc(w_loaded, 16)

            def step(it):
                pool.wait_ge(in_loaded, 64 * (it + 1))
                for j in range(NJ):
                    pool.wait_ge(prod_free, it * NJ + j + 1)
                    nc.gpsimd.tensor_tensor(prods[:, j % 2], qw[:], kw[:, j * GD:j * GD + IB * GD],
                                            ALU.mult).then_inc(prod_ready, 1)
                pool.wait_ge(outs_stored, 16 * it + 16)
                for j in range(NJ):
                    pool.wait_ge(out_prod, it * NJ + j + 1)
                    if j == 0:
                        pool.sem_inc(go, 1)
                        ins = nc.gpsimd.tensor_copy(outs[:], prods[:, 0])
                    else:
                        pool.wait_ge(out_prod_free, it * NJ + j + 2)
                        ins = nc.gpsimd.tensor_tensor(outs[:], outs[:], prods[:, j % 2], ALU.add)
                    ins.then_inc(out_prod_free, 1)

            with pool.Fori(0, STEPS) as it:
                step(it)

        @block.scalar
        def _(act):
            def moe(n, u):
                act.wait_ge(xsT_done, n + 1)
                nc.scalar.activation(xsT[:].rearrange("p k t -> p (k t)"), pX[:, 0:D], ACT.Identity).then_inc(xsT_ready, 1)
                act.wait_ge(h_done, n + 1)
                nc.scalar.activation(act_a[:], pA[:], ACT.Silu).then_inc(a_ready, 1)
                act.wait_ge(hidT_done, n + 1)
                nc.scalar.activation(hidT[:].rearrange("p k t -> p (k t)"), pH[:], ACT.Identity).then_inc(hidT_ready, 1)
                act.wait_ge(y_done, n + 1)
                nc.scalar.activation(ys[:, u], pY[:, 0:D], ACT.Identity).then_inc(ys_ready, 1)

            def moes(it):
                for m in range(MOE_PER_STEP):
                    n = it * MOE_PER_STEP + m
                    act.wait_ge(ys_stored[m % 2], 16 * (it * (MOE_PER_STEP // 2) + m // 2 + 1))
                    moe(n, m % 2)

            with act.Fori(0, STEPS) as it:
                act.wait_ge(in_loaded, 64 * (it + 1))
                nc.scalar.activation(prob[:], pos[:], ACT.Abs).then_inc(dist_ready, 1)
                moes(it)
                act.wait_ge(shift_ready, it + 1)
                nc.scalar.activation(prob[:], shifted[:], ACT.Exp, scale=SCALE).then_inc(prob_ready, 1)
                for c in range(KNOTS // 4):
                    act.wait_ge(term_free, it * 2 * KNOTS + KNOTS + 4 * (c + 1) + 4)
                    nc.scalar.activation(G[:, 4 * c:4 * c + 4].rearrange("p j t -> p (j t)"), pG[:, 0:4 * TH],
                                         ACT.Identity).then_inc(g_ready, 1)
            moes(STEPS)

        @block.tensor
        def _(pe):
            pe.wait_ge(w_loaded, 16 * (KC + HC))
            pe.wait_ge(b_loaded, 32)
            pe.wait_ge(ones_set, 1)
            pe.wait_ge(rel_eye_set, 1)

            def moe(n, half, u):
                e = pe.value_load(keep["tile_exp"][0:1, ds(n, 1)], min_val=0, max_val=EXPERTS - 1)
                pe.wait_ge(xs_loaded[u], 16 * half + 16)
                for k in range(KC):
                    tr = nc.tensor.transpose(pX[:, k * P:(k + 1) * P], xs[:, u, k * P:(k + 1) * P], keep["ident"][:])
                tr.then_inc(xsT_done, 1)
                pe.wait_ge(xsT_ready, n + 1)
                for o, dst in ((0, pA), (1, pB)):
                    for k in range(KC):
                        nc.tensor.matmul(dst[:], xsT[:, k], w1[:, k, ds(e * 2 * HID + o * HID, HID)],
                                         start=(k == 0), stop=False)
                    mm = nc.tensor.matmul(dst[:], ones3[:], b1[:, ds(e * 2 * HID + o * HID, HID)], start=False, stop=True)
                mm.then_inc(h_done, 1)
                pe.wait_ge(hid_ready, n + 1)
                for k in range(HC):
                    tr = nc.tensor.transpose(pH[:, k * P:(k + 1) * P], hid[:, k * P:(k + 1) * P], keep["ident"][:])
                tr.then_inc(hidT_done, 1)
                pe.wait_ge(hidT_ready, n + 1)
                for k in range(HC):
                    nc.tensor.matmul(pY[:, 0:D], hidT[:, k], w2[:, k, ds(e * D, D)], start=(k == 0), stop=False)
                nc.tensor.matmul(pY[:, 0:D], ones3[:], b2[:, ds(e * D, D)], start=False, stop=True).then_inc(y_done, 1)

            def moes(it):
                for m in range(MOE_PER_STEP):
                    moe(it * MOE_PER_STEP + m, it * (MOE_PER_STEP // 2) + m // 2, m % 2)

            with pe.Fori(0, STEPS) as it:
                moes(it)
                NT = 2 * KNOTS
                for j in range(KNOTS):
                    pe.wait_ge(term_ready, it * NT + j + 1)
                    for half in range(2):
                        cols = slice(half * PAIRS // 2, (half + 1) * PAIRS // 2)
                        mm = nc.tensor.matmul(pS[:, half, 0:PAIRS // 2], keep["ident"][:], terms[:, j % 4, cols],
                                              start=(j == 0), stop=False)
                    mm.then_inc(term_free, 1)
                pe.wait_ge(dist_ready, it + 1)
                for half in range(2):
                    cols = slice(half * PAIRS // 2, (half + 1) * PAIRS // 2)
                    nc.tensor.matmul(pS[:, half, 0:PAIRS // 2], rel_eye[:], prob[:, cols], start=False, stop=False)
                    const = last[:, half * TH // 2:(half + 1) * TH // 2].unsqueeze(2).broadcast_to([P, TH // 2, SAMPLES])
                    mm = nc.tensor.matmul(pS[:, half, 0:PAIRS // 2].rearrange("p (t r) -> p t r", r=SAMPLES),
                                          keep["ident"][:], const, start=False, stop=True)
                mm.then_inc(score_done, 1)
                for c in range(KNOTS // 4):
                    pe.wait_ge(term_ready, it * NT + KNOTS + 4 * (c + 1))
                    pe.wait_ge(g_ready, it * (KNOTS // 4) + c + 1)
                    view = terms[:].rearrange("p j (t r) -> p j t r", r=SAMPLES)
                    for r in range(SAMPLES):
                        mm = nc.tensor.matmul(pG[:, 0:4 * TH].rearrange("p (j t) -> p j t", j=4), keep["ident"][:],
                                              view[:, :, :, r], start=(r == 0), stop=(r == SAMPLES - 1))
                    mm.then_inc(term_free, 4)
            moes(STEPS)

        @block.vector
        def _(dve):
            V = nc.vector
            for u in range(2):
                dve.sem_inc(ys_stored[u], 16)
            dve.sem_inc(in_free, 1)
            dve.sem_inc(prod_free, 2)
            dve.sem_inc(term_free, 4)
            dve.sem_inc(out_prod_free, 2)
            dve.sem_inc(outs_stored, 16)
            dve.sem_inc(g_ready, 1)
            setup = Chain(dve, chain_sem)
            V.memset(ones3[:], 1.0).then_inc(ones_set, 1)
            dve.wait_ge(rel_ready, 16)
            V.tensor_scalar(rel_eye[:], keep["ident"][:], rel[:, 0:1], -1.0 / SCALE, ALU.mult,
                            ALU.mult).then_inc(rel_eye_set, 1)
            SETUP = setup.n
            CHAIN = 10
            NT = 2 * KNOTS

            def gate_hidden(n):
                dve.wait_ge(h_done, n + 1)
                dve.wait_ge(a_ready, n + 1)
                V.tensor_tensor(hid[:], act_a[:], pB[:], ALU.mult).then_inc(hid_ready, 1)

            def moes(it):
                for m in range(MOE_PER_STEP):
                    gate_hidden(it * MOE_PER_STEP + m)

            def pairs(ap):
                return ap.rearrange("p (t r) -> p t r", r=SAMPLES)

            def each_sample(ap):
                return ap.unsqueeze(2).broadcast_to([P, TH, SAMPLES])

            def step(it):
                chain = Chain(dve, chain_sem, it * CHAIN + SETUP)
                for j in range(NJ):
                    dve.wait_ge(prod_ready, it * NJ + j + 1)
                    V.tensor_reduce(S[:, j], prods[:, j % 2].rearrange("p (t d) -> p t d", d=DH), AX.X,
                                    ALU.add).then_inc(prod_free, 1)
                dve.wait_ge(prod_free, (it + 1) * NJ + 2)
                chain(V.tensor_tensor(slope[:, 0:KNOTS], S[:, 1:NJ], S[:, 0:KNOTS], ALU.subtract))
                V.tensor_copy(bend[:, 0], slope[:, 0])
                V.tensor_tensor(bend[:, 1:KNOTS], slope[:, 1:KNOTS], slope[:, 0:KNOTS - 1], ALU.subtract)
                chain(V.tensor_scalar(last[:], S[:, NJ - 1], -float(REACH - 1), None, ALU.mult))
                chain(V.scalar_tensor_tensor(last[:], S[:, NJ - 2], float(REACH), last[:], ALU.mult, ALU.add))
                for j in range(KNOTS):
                    dve.wait_ge(term_free, it * NT + j + 1)
                    V.scalar_tensor_tensor(pairs(terms[:, j % 4]), pairs(pos[:]), float(j - REACH),
                                           each_sample(bend[:, j]), ALU.max, ALU.mult).then_inc(term_ready, 1)
                dve.wait_ge(score_done, it + 1)
                sc = pS[:, :, 0:PAIRS // 2].rearrange("p b (t r) -> p b t r", r=SAMPLES)
                chain(V.tensor_reduce(smax[:].rearrange("p (b t) -> p b t", b=2), sc, AX.X, ALU.max))
                for half in range(2):
                    cols = slice(half * TH // 2, (half + 1) * TH // 2)
                    ins = V.tensor_tensor(pairs(shifted[:])[:, cols], pairs(pS[:, half, 0:PAIRS // 2]),
                                          each_sample(smax[:])[:, cols], ALU.subtract)
                ins.then_inc(shift_ready, 1)
                dve.wait_ge(prob_ready, it + 1)
                chain(V.tensor_reduce(psum_e[:], pairs(prob[:]), AX.X, ALU.add))
                for j in range(KNOTS):
                    dve.wait_ge(term_free, it * NT + KNOTS + j + 1)
                    V.scalar_tensor_tensor(terms[:, j % 4], pos[:], float(j - REACH), prob[:], ALU.max,
                                           ALU.mult).then_inc(term_ready, 1)
                dve.wait_ge(g_ready, (it + 1) * (KNOTS // 4) + 1)
                chain(V.memset(slope[:, 0], 0.0))
                V.tensor_tensor(slope[:, 1:KNOTS], G[:, 1:KNOTS], G[:, 0:KNOTS - 1], ALU.subtract)
                V.scalar_tensor_tensor(slope[:, KNOTS], psum_e[:], float(REACH), G[:, KNOTS - 1], ALU.mult, ALU.subtract)
                chain(V.tensor_copy(slope[:, KNOTS + 1], psum_e[:]))
                chain(V.reciprocal(psum_e[:], psum_e[:]))
                chain(V.tensor_tensor(wgt[:], slope[:, 1:KNOTS + 2], slope[:, 0:KNOTS + 1], ALU.subtract))
                chain(V.tensor_tensor(wgt[:], wgt[:], psum_e[:, None, :].broadcast_to([P, NJ, TH]), ALU.mult))
                for j in range(NJ):
                    dve.wait_ge(out_prod_free, it * NJ + j + 1)
                    V.tensor_tensor(prods[:, j % 2].rearrange("p (t d) -> p t d", d=DH),
                                    vw[:, j * GD:j * GD + IB * GD].rearrange("p (t d) -> p t d", d=DH),
                                    wgt[:, j].unsqueeze(2).broadcast_to([P, TH, DH]), ALU.mult).then_inc(out_prod, 1)
                dve.wait_ge(out_prod, (it + 1) * NJ)
                dve.sem_inc(in_free, 1)
                assert chain.n == CHAIN, chain.n

            with dve.Fori(0, STEPS) as it:
                moes(it)
                step(it)
            moes(STEPS)


def finish_block(nc, io, dram, keep):
    with ExitStack() as ctx:
        def sb(name, shape, dt=F32):
            return ctx.enter_context(nc.sbuf_tensor(name, shape, dt))

        def ps(name, shape, dt=F32):
            return ctx.enter_context(nc.psum_tensor(name, shape, dt))

        def sem(name):
            return ctx.enter_context(nc.semaphore(name))

        wo = sb("wo", [P, KC, D])
        bo = sb("bo", [P, D])
        xr = sb("xr", [P, 2, D])
        at = sb("at", [P, 2, D])
        atT = sb("atT", [P, 2, KC, P])
        yk = sb("yk", [P, 2, TOPK, D])
        idx = sb("idx4", [P, 2, TOPK], U32)
        moe = sb("moe", [P, 2, D])
        gate = sb("gate4", [P, 2, D])
        proj = sb("proj", [P, 2, D])
        pT = ps("pT4", [P, 2, 512])
        pO = ps("pO4", [P, 2, 512])

        weights_in = sem("weights_in4")
        x_loaded = [sem(f"x_loaded4{u}") for u in range(2)]
        y_loaded = [sem(f"y_loaded4{u}") for u in range(2)]
        idx_set = sem("idx_set4")
        go = sem("go4")
        atT_done = sem("atT_done")
        atT_ready = sem("atT_ready")
        proj_done = sem("proj_done")
        moe_ready = sem("moe_ready")
        gate_ready = sem("gate_ready")
        chain_sem = sem("final_chain")
        out_ready = sem("out_ready")
        out_stored = [sem(f"out_stored{u}") for u in range(2)]
        block = ctx.enter_context(nc.Block())

        @block.sync
        def _(sp):
            sp.dma_start(wo[:], io["w_oT"].rearrange("(k p) n -> p k n", p=P)).then_inc(weights_in, 16)
            sp.dma_start(bo[:], io["b_o"].partition_broadcast(P)).then_inc(weights_in, 16)
            with sp.Fori(0, TILES // 2) as t:
                for u in range(2):
                    row = (2 * t + u) * P
                    sp.wait_ge(out_ready, 2 * t + u + 1)
                    sp.dma_start(xr[:, u], io["x"][ds(row, P), :]).then_inc(x_loaded[u], 16)
                    sp.dma_start(at[:, u], dram["attn"][ds(row, P), :]).then_inc(x_loaded[u], 16)

        @block.gpsimd
        def _(pool):
            def fetch(t, u):
                for k in range(TOPK):
                    nc.gpsimd.tensor_copy(idx[:, u, k:k + 1], keep["slot"][:, k, ds(2 * t + u, 1)]).then_inc(idx_set, 1)
                pool.wait_ge(idx_set, (2 * t + u + 1) * TOPK)
                pool.sem_inc(go, 1)
                for k in range(TOPK):
                    nc.gpsimd.indirect_dma_start(
                        out=yk[:, u, k], out_offset=None, in_=dram["ys"],
                        in_offset=bass.IndirectOffsetOnAxis(ap=idx[:, u, k:k + 1], axis=0)).then_inc(y_loaded[u], 16)

            with pool.Fori(0, TILES // 2) as t:
                for u in range(2):
                    pool.wait_ge(moe_ready, 2 * t + u + 1)
                    pool.sem_inc(go, 1)
                    fetch(t, u)

        @block.tensor
        def _(pe):
            pe.wait_ge(weights_in, 32)
            with pe.Fori(0, TILES // 2) as t:
                for u in range(2):
                    n = 2 * t + u
                    pe.wait_ge(x_loaded[u], 32 * t + 32)
                    for k in range(KC):
                        tr = nc.tensor.transpose(pT[:, u, k * P:(k + 1) * P], at[:, u, k * P:(k + 1) * P], keep["ident"][:])
                    tr.then_inc(atT_done, 1)
                    pe.wait_ge(atT_ready, n + 1)
                    for k in range(KC):
                        mm = nc.tensor.matmul(pO[:, u, 0:D], atT[:, u, k], wo[:, k], start=(k == 0), stop=(k == KC - 1))
                    mm.then_inc(proj_done, 1)

        @block.scalar
        def _(act):
            with act.Fori(0, TILES // 2) as t:
                for u in range(2):
                    n = 2 * t + u
                    act.wait_ge(atT_done, n + 1)
                    nc.scalar.activation(atT[:, u].rearrange("p k t -> p (k t)"), pT[:, u, 0:D],
                                         ACT.Identity).then_inc(atT_ready, 1)
                    act.wait_ge(moe_ready, n + 3)
                    nc.scalar.activation(gate[:, u], moe[:, u], ACT.Silu).then_inc(gate_ready, 1)
                    act.wait_ge(out_ready, n + 3)
                    act.dma_start(io["out"][ds(n * P, P), :], proj[:, u]).then_inc(out_stored[u], 16)
            for u in range(2):
                act.wait_ge(out_stored[u], 16 * (TILES // 2 + 1))

        @block.vector
        def _(dve):
            V = nc.vector
            for u in range(2):
                dve.sem_inc(out_stored[u], 16)
            dve.sem_inc(moe_ready, 2)
            dve.sem_inc(out_ready, 2)
            dve.wait_ge(weights_in, 32)
            CHAIN = 3
            with dve.Fori(0, TILES // 2) as t:
                for u in range(2):
                    n = 2 * t + u
                    chain = Chain(dve, chain_sem, n * CHAIN)
                    dve.wait_ge(y_loaded[u], 32 * t + 32)
                    chain(V.tensor_scalar(moe[:, u], yk[:, u, 0], keep["gate"][:, 0, ds(n, 1)], None, ALU.mult))
                    V.scalar_tensor_tensor(moe[:, u], yk[:, u, 1], keep["gate"][:, 1, ds(n, 1)], moe[:, u],
                                           ALU.mult, ALU.add).then_inc(moe_ready, 1)
                    dve.wait_ge(proj_done, n + 1)
                    dve.wait_ge(out_stored[u], 16 * t + 16)
                    chain(V.tensor_tensor(proj[:, u], pO[:, u, 0:D], bo[:], ALU.add))
                    dve.wait_ge(gate_ready, n + 1)
                    chain(V.tensor_tensor(proj[:, u], proj[:, u], gate[:, u], ALU.mult))
                    V.tensor_tensor(proj[:, u], proj[:, u], xr[:, u], ALU.add).then_inc(out_ready, 1)


def build(nc, io):
    dram = {
        "xn": nc.dram_tensor("xn_rows", [TOKENS, D], F32).ap(),
        "q": nc.dram_tensor("q_rows", [HG, TOKENS, GD], F32).ap(),
        "k": nc.dram_tensor("k_rows", [HG, TOKENS + 2 * REACH, GD], F32).ap(),
        "v": nc.dram_tensor("v_rows", [HG, TOKENS + 2 * REACH, GD], F32).ap(),
        "pos": nc.dram_tensor("pos_rows", [HG, TOKENS, GR], F32).ap(),
        "xs": nc.dram_tensor("xs_slots", [SLOTS, D], F32).ap(),
        "ys": nc.dram_tensor("ys_slots", [SLOTS, D], F32).ap(),
        "bias": nc.dram_tensor("bias_parts", [NB, EXPERTS, 2 * HID + D], BF16).ap(),
        "attn": nc.dram_tensor("attn_rows", [TOKENS, D], F32).ap(),
    }
    with ExitStack() as ctx:
        def sb(name, shape, dt=F32):
            return ctx.enter_context(nc.sbuf_tensor(name, shape, dt))

        keep = {
            "ident": sb("ident", [P, P]),
            "scores": sb("scores", [P, TILES, EXPERTS]),
            "gate": sb("gate", [P, TOPK, TILES]),
            "slot": sb("slot_u", [P, TOPK, TILES], U32),
            "tile_exp": sb("tile_exp_i", [1, SLOT_TILES], I32),
        }
        with nc.sbuf_tensor("qT", [P, KC, BATCH * (SEQ + 2)], F32) as qT:
            keep["qT"] = qT
            project_block(nc, io, dram, keep)
            route_block(nc, io, dram, keep)
        mix_block(nc, io, dram, keep)
        finish_block(nc, io, dram, keep)


def kernel(**inputs):
    import concourse.bacc as bacc
    from concourse.bass_utils import run_bass_kernel_spmd

    a = {k: np.asarray(v) for k, v in inputs.items()}
    t = np.ascontiguousarray
    arrays = {
        "x": a["L0_attn_x"].reshape(TOKENS, D),
        "w_qkvT": t(np.concatenate([a["L0_attn_wq"], a["L0_attn_wk"], a["L0_attn_wv"]], 0).T),
        "b_qkv": np.concatenate([a["L0_attn_bq"], a["L0_attn_bk"], a["L0_attn_bv"]]),
        "w_oT": t(a["L0_attn_wo"].T),
        "b_o": a["L0_attn_bo"],
        "dw_w": a["L0_attn_dw_w"].reshape(D, 3),
        "dw_b": a["L0_attn_dw_b"],
        "pw_wT": t(a["L0_attn_pw_w"].T),
        "pw_b": a["L0_attn_pw_b"],
        "rel_scale": a["L0_attn_rel_scale"].reshape(1),
        "w_rT": t(a["L0_ffn_Wr"].T),
        "b_r": a["L0_ffn_br"],
        "w_l1": a["L0_ffn_Wl1"],
        "b_l1": a["L0_ffn_bl1"],
        "w_l2": a["L0_ffn_Wl2"],
        "b_l2": a["L0_ffn_bl2"],
        "sel_bias": a["L0_ffn_biases_N"],
    }
    nc = bacc.Bacc("TRN2", target_bir_lowering=False, num_devices=1)
    io = {k: nc.dram_tensor(f"in_{k}", v.shape, F32, kind="ExternalInput").ap() for k, v in arrays.items()}
    io["out"] = nc.dram_tensor("out", (TOKENS, D), F32, kind="ExternalOutput").ap()
    build(nc, io)
    r = run_bass_kernel_spmd(nc, [{f"in_{k}": t(v) for k, v in arrays.items()}], core_ids=[0])
    return r.results[0]["out"].reshape(BATCH, SEQ, D)
```

```python
from contextlib import ExitStack

import concourse.bass as bass
import numpy as np
from concourse import mybir

P = 128
F32 = mybir.dt.float32
BF16 = mybir.dt.bfloat16
I32 = mybir.dt.int32
U32 = mybir.dt.uint32
ACT = mybir.ActivationFunctionType
ALU = mybir.AluOpType
AX = mybir.AxisListType
ds = bass.ds

BATCH, SEQ, D = 2, 4096, 256
TOKENS = BATCH * SEQ
TILES = TOKENS // P
KC = D // P
HEADS, SAMPLES = 16, 12
DH = D // HEADS
HR = HEADS * SAMPLES
RHO, MAX_OFFSET = 2.0, 6.0
REACH = int(RHO + MAX_OFFSET)
LN_EPS = 1e-5

EXPERTS, HID, TOPK = 8, 512, 2
NB = 3
HC = HID // P
SLOT_TILES = TOKENS * TOPK // P + EXPERTS
SLOTS = SLOT_TILES * P

GROUP = 4
GTOK = GROUP * P
GROUPS_PER_SEQ = SEQ // GTOK

HG = 4
GH = HEADS // HG
GD = GH * DH
GR = GH * SAMPLES
RUN = TOKENS // P
IB = 16
NIB = RUN // IB
WIN = IB + 2 * REACH
TH = IB * GH
PAIRS = TH * SAMPLES
NJ = 2 * REACH + 1
KNOTS = 2 * REACH
STEPS = HG * NIB
SCALE = float(DH) ** -0.5
MOE_PER_STEP = SLOT_TILES // (STEPS + 1)
assert MOE_PER_STEP * (STEPS + 1) == SLOT_TILES


def anchors():
    step = np.arange(SAMPLES, dtype=np.float32) * np.float32(1.0 / (SAMPLES - 1))
    a = np.float32(-RHO) * (np.float32(1) - step) + np.float32(RHO) * step
    a[-1] = RHO
    return [float(v) for v in a]


class Chain:

    def __init__(self, eng, sem, base=0):
        self.eng, self.sem, self.base, self.n = eng, sem, base, 0

    def __call__(self, ins):
        self.n += 1
        ins.then_inc(self.sem, 1)
        self.eng.wait_ge(self.sem, self.base + self.n)


def project_block(nc, io, dram, keep):
    with ExitStack() as ctx:
        def sb(name, shape, dt=F32):
            return ctx.enter_context(nc.sbuf_tensor(name, shape, dt))

        def ps(name, shape, dt=F32):
            return ctx.enter_context(nc.psum_tensor(name, shape, dt))

        def sem(name):
            return ctx.enter_context(nc.semaphore(name))

        x_in = sb("x_in", [P, 2, GROUP, D])
        xn = sb("xn", [P, 2, GROUP, D])
        xnT = sb("xnT", [P, 2, KC, GTOK])
        wqkv = sb("wqkv", [P, KC, 3 * D])
        wr = sb("wr", [P, KC, EXPERTS])
        bqkv_bc = sb("bqkv_bc", [P, 3 * D])
        br_bc = sb("br_bc", [P, EXPERTS])
        bq_col = sb("bq_col", [P, KC])
        qkv = sb("qkv", [P, 2, GROUP, 3 * D])
        zeros = sb("zeros", [P, 4 * D])
        stats = sb("stats", [P, GROUP, 6])
        mv = sb("mv", [P, GROUP, 2])
        var = sb("var", [P, GROUP])
        std = sb("std", [P, GROUP])
        rstd = sb("rstd", [P, GROUP])

        pT = ps("pT", [P, KC, GTOK])
        pQ = ps("pQ", [P, KC, GTOK])
        pQK = ps("pQK", [P, 2, 512])
        pV = ps("pV", [P, 512])
        pR = ps("pR", [P, 512])

        weights_in = sem("weights_in")
        zeros_set = sem("zeros_set")
        ident_set = sem("ident_set")
        pads_set = sem("pads_set")
        x_loaded = [sem(f"x_loaded{u}") for u in range(2)]
        xn_ready = sem("xn_ready")
        xn_stored = [sem(f"xn_stored{u}") for u in range(2)]
        var_ready = sem("var_ready")
        std_ready = sem("std_ready")
        xT_done = sem("xT_done")
        xnT_ready = sem("xnT_ready")
        qT_done = sem("qT_done")
        r_done = sem("r_done")
        r_free = sem("r_free")
        qk_done = sem("qk_done")
        qk_free = sem("qk_free")
        v_done = sem("v_done")
        v_free = sem("v_free")
        qkv_stored = [sem(f"qkv_stored{u}") for u in range(2)]
        filled = sem("filled")
        go = sem("go1")
        ln_chain = sem("ln_chain")
        QKV_STORES = 3 * HG

        block = ctx.enter_context(nc.Block())

        @block.sync
        def _(sp):
            def load_x(t, u):
                sp.dma_start(x_in[:, u], io["x"][ds(u * SEQ + t * GTOK, GTOK), :].rearrange(
                    "(a p) c -> p a c", p=P)).then_inc(x_loaded[u], 16)

            def store_xn(t, u):
                sp.wait_ge(xn_ready, 2 * t + u + 1)
                sp.dma_start(dram["xn"][ds(u * SEQ + t * GTOK, GTOK), :].rearrange("(a p) c -> p a c", p=P),
                             xn[:, u]).then_inc(xn_stored[u], 16)

            def store_qkv(t, u):
                sp.wait_ge(v_free, (2 * t + u + 1) * GROUP + 1)
                for w, name, pad in ((0, "q", 0), (1, "k", REACH), (2, "v", REACH)):
                    for hg in range(HG):
                        dst = dram[name][hg, ds(pad + u * SEQ + t * GTOK, GTOK), :]
                        sp.dma_start(dst.rearrange("(a p) c -> p a c", p=P),
                                     qkv[:, u, :, w * D + hg * GD:w * D + (hg + 1) * GD]).then_inc(qkv_stored[u], 16)

            load_x(0, 0)
            load_x(0, 1)
            with sp.Fori(0, GROUPS_PER_SEQ - 1) as t:
                for u in range(2):
                    store_xn(t, u)
                    load_x(t + 1, u)
                for u in range(2):
                    store_qkv(t, u)
            for u in range(2):
                store_xn(GROUPS_PER_SEQ - 1, u)
            for u in range(2):
                store_qkv(GROUPS_PER_SEQ - 1, u)
            sp.wait_ge(pads_set, 16 * 4 * HG)
            sp.wait_ge(filled, 16 * (SLOTS // (4 * P)))
            for u in range(2):
                sp.wait_ge(xn_stored[u], 16 * GROUPS_PER_SEQ + 16)
                sp.wait_ge(qkv_stored[u], 16 * QKV_STORES * (GROUPS_PER_SEQ + 1))

        @block.gpsimd
        def _(pool):
            nc.gpsimd.memset(zeros[:], 0.0).then_inc(zeros_set, 1)
            nc.gpsimd.memset(keep["ident"][:], 0.0).then_inc(zeros_set, 1)
            pool.wait_ge(zeros_set, 2)
            nc.gpsimd.affine_select(out=keep["ident"][:], in_=keep["ident"][:], compare_op=ALU.not_equal, fill=1.0,
                                    base=0, pattern=[[-1, P]], channel_multiplier=1).then_inc(ident_set, 1)
            for name in ("k", "v"):
                for hg in range(HG):
                    for row in (0, REACH + TOKENS):
                        pool.dma_start(dram[name][hg, row:row + REACH, :], zeros[0:REACH, 0:GD]).then_inc(pads_set, 16)
            with pool.Fori(0, SLOTS // (4 * P)) as n:
                pool.dma_start(dram["xs"][ds(n * 4 * P, 4 * P), :].rearrange("(p a) c -> p (a c)", p=P),
                               zeros[:]).then_inc(filled, 16)

        @block.scalar
        def _(act):
            act.dma_start(wqkv[:], io["w_qkvT"].rearrange("(k p) n -> p k n", p=P)).then_inc(weights_in, 16)
            act.dma_start(wr[:], io["w_rT"].rearrange("(k p) n -> p k n", p=P)).then_inc(weights_in, 16)
            act.dma_start(bqkv_bc[:], io["b_qkv"].partition_broadcast(P)).then_inc(weights_in, 16)
            act.dma_start(br_bc[:], io["b_r"].partition_broadcast(P)).then_inc(weights_in, 16)
            act.dma_start(bq_col[:], io["b_qkv"][0:D].rearrange("(k p) -> p k", p=P),
                          allow_slow_non_contiguous=True).then_inc(weights_in, 16)
            act.wait_ge(weights_in, 80)

            def group(t, u):
                n = 2 * t + u
                act.wait_ge(xT_done, n + 1)
                nc.scalar.activation(xnT[:, u], pT[:], ACT.Identity).then_inc(xnT_ready, 1)
                act.wait_ge(qT_done, n + 1)
                for c in range(KC):
                    nc.scalar.activation(keep["qT"][:, c, ds(u * (SEQ + 2) + 1 + t * GTOK, GTOK)], pQ[:, c],
                                         ACT.Identity, bias=bq_col[:, c:c + 1])

            def root(t, u):
                act.wait_ge(var_ready, 2 * t + u + 1)
                nc.scalar.activation(std[:], var[:], ACT.Sqrt).then_inc(std_ready, 1)

            root(0, 0)
            with act.Fori(0, GROUPS_PER_SEQ - 1) as t:
                root(t, 1)
                group(t, 0)
                root(t + 1, 0)
                group(t, 1)
            last = GROUPS_PER_SEQ - 1
            root(last, 1)
            group(last, 0)
            group(last, 1)

        @block.tensor
        def _(pe):
            pe.wait_ge(weights_in, 80)
            pe.wait_ge(ident_set, 1)

            def group(t, u):
                n = 2 * t + u
                pe.wait_ge(xn_ready, n + 1)
                for a in range(GROUP):
                    for c in range(KC):
                        tr = nc.tensor.transpose(pT[:, c, a * P:(a + 1) * P], xn[:, u, a, c * P:(c + 1) * P],
                                                 keep["ident"][:])
                tr.then_inc(xT_done, 1)
                pe.wait_ge(xnT_ready, n + 1)
                for o in range(KC):
                    for c in range(KC):
                        mm = nc.tensor.matmul(pQ[:, o], wqkv[:, c, o * P:(o + 1) * P], xnT[:, u, c],
                                              start=(c == 0), stop=(c == KC - 1))
                mm.then_inc(qT_done, 1)
                pe.wait_ge(r_free, n + 1)
                for a in range(GROUP):
                    for c in range(KC):
                        mm = nc.tensor.matmul(pR[:, a * EXPERTS:(a + 1) * EXPERTS], xnT[:, u, c, a * P:(a + 1) * P],
                                              wr[:, c], start=(c == 0), stop=(c == KC - 1))
                mm.then_inc(r_done, 1)
                for a in range(GROUP):
                    m = n * GROUP + a
                    pe.wait_ge(qk_free, m + 1)
                    for c in range(KC):
                        mm = nc.tensor.matmul(pQK[:, a % 2], xnT[:, u, c, a * P:(a + 1) * P], wqkv[:, c, 0:2 * D],
                                              start=(c == 0), stop=(c == KC - 1))
                    mm.then_inc(qk_done, 1)
                    pe.wait_ge(v_free, m + 1)
                    for c in range(KC):
                        mm = nc.tensor.matmul(pV[:, 0:D], xnT[:, u, c, a * P:(a + 1) * P], wqkv[:, c, 2 * D:3 * D],
                                              start=(c == 0), stop=(c == KC - 1))
                    mm.then_inc(v_done, 1)

            with pe.Fori(0, GROUPS_PER_SEQ) as t:
                group(t, 0)
                group(t, 1)

        @block.vector
        def _(dve):
            for u in range(2):
                dve.sem_inc(xn_stored[u], 16)
                dve.sem_inc(qkv_stored[u], 16 * QKV_STORES)
            dve.sem_inc(r_free, 1)
            dve.sem_inc(qk_free, 2)
            dve.sem_inc(v_free, 1)
            for b in range(BATCH):
                for col in (b * (SEQ + 2), b * (SEQ + 2) + SEQ + 1):
                    nc.vector.memset(keep["qT"][:, :, col:col + 1], 0.0)
            dve.wait_ge(weights_in, 80)
            CHAIN = 7

            def layernorm(t, u):
                chain = Chain(dve, ln_chain, (2 * t + u) * CHAIN)
                dve.wait_ge(x_loaded[u], 16 * t + 16)
                dve.wait_ge(xn_stored[u], 16 * t + 16)
                for a in range(GROUP):
                    ins = nc.vector.bn_stats(stats[:, a], x_in[:, u, a])
                chain(ins)
                dve.sem_inc(go, 1)
                for a in range(GROUP):
                    ins = nc.vector.bn_aggr(mv[:, a], stats[:, a])
                chain(ins)
                V = nc.vector
                V.tensor_scalar(var[:], mv[:, :, 1], LN_EPS, None, ALU.add).then_inc(var_ready, 1)
                dve.wait_ge(std_ready, 2 * t + u + 1)
                chain(V.reciprocal(rstd[:], std[:]))
                chain(V.tensor_tensor(std[:], rstd[:], rstd[:], ALU.mult))
                chain(V.tensor_tensor(std[:], std[:], var[:], ALU.mult))
                chain(V.tensor_scalar(std[:], std[:], -0.5, 1.5, ALU.mult, ALU.add))
                chain(V.tensor_tensor(rstd[:], rstd[:], std[:], ALU.mult))
                for a in range(GROUP):
                    ins = nc.vector.tensor_scalar(xn[:, u, a], x_in[:, u, a], mv[:, a, 0:1], rstd[:, a:a + 1],
                                                  ALU.subtract, ALU.mult)
                ins.then_inc(xn_ready, 1)

            def evacuate(t, u):
                n = 2 * t + u
                dve.wait_ge(r_done, n + 1)
                nc.vector.tensor_tensor(
                    keep["scores"][:, ds((u * GROUPS_PER_SEQ + t) * GROUP, GROUP), :],
                    pR[:, 0:GROUP * EXPERTS].rearrange("p (a e) -> p a e", a=GROUP),
                    br_bc[:, None, :].broadcast_to([P, GROUP, EXPERTS]), ALU.add).then_inc(r_free, 1)
                dve.wait_ge(qkv_stored[u], 16 * QKV_STORES * t + 16 * QKV_STORES)
                for a in range(GROUP):
                    m = n * GROUP + a
                    dve.wait_ge(qk_done, m + 1)
                    nc.vector.tensor_tensor(qkv[:, u, a, 0:2 * D], pQK[:, a % 2], bqkv_bc[:, 0:2 * D],
                                            ALU.add).then_inc(qk_free, 1)
                    dve.wait_ge(v_done, m + 1)
                    ins = nc.vector.tensor_tensor(qkv[:, u, a, 2 * D:3 * D], pV[:, 0:D], bqkv_bc[:, 2 * D:3 * D], ALU.add)
                    ins.then_inc(v_free, 1)

            layernorm(0, 0)
            with dve.Fori(0, GROUPS_PER_SEQ - 1) as t:
                layernorm(t, 1)
                evacuate(t, 0)
                layernorm(t + 1, 0)
                evacuate(t, 1)
            last = GROUPS_PER_SEQ - 1
            layernorm(last, 1)
            evacuate(last, 0)
            evacuate(last, 1)


def route_block(nc, io, dram, keep):
    with ExitStack() as ctx:
        def sb(name, shape, dt=F32):
            return ctx.enter_context(nc.sbuf_tensor(name, shape, dt))

        def ps(name, shape, dt=F32):
            return ctx.enter_context(nc.psum_tensor(name, shape, dt))

        def sem(name):
            return ctx.enter_context(nc.semaphore(name))

        TE = [P, TILES, EXPERTS]
        sel_bias = sb("sel_bias", [P, EXPERTS])
        e_first = sb("e_first", [P, EXPERTS])
        biased = sb("biased", TE)
        top = sb("top", [P, TILES])
        is_top = sb("is_top", TE)
        chosen = [sb(f"chosen{k}", TE) for k in range(TOPK)]
        expw = sb("expw", TE)
        prod = sb("prod", TE)
        picked = sb("picked", [P, TOPK, TILES])
        count = sb("count", TE)
        zero_te = sb("zero_te", [P, TILES])
        upto = sb("upto", TE)
        total = sb("total", [P, EXPERTS])
        below = sb("below", [P, P])
        ones = sb("ones", [P, P])
        rows_i = sb("rows_i", [P, EXPERTS], I32)
        rows = sb("rows", [P, EXPERTS])
        ends = sb("ends", [P, EXPERTS])
        start = sb("start", [P, EXPERTS])
        rank = sb("rank", TE)
        slot = sb("slot", [P, TOPK, TILES])
        tile_row = sb("tile_row", [1, SLOT_TILES])
        tile_exp = sb("tile_exp", [1, SLOT_TILES])

        xrow = sb("xrow", [P, 2, D])
        idx = sb("idx", [P, 2, TOPK], U32)
        dw_w = sb("dw_w", [P, KC, 3])
        dw_b = sb("dw_b", [P, KC])
        pw_w = sb("pw_w", [P, KC, HR])
        pw_b = sb("pw_b", [P, HR])
        anchor = sb("anchor", [P, HEADS, SAMPLES])
        base_i = sb("base_i", [P, SEQ // P], I32)
        base = sb("base", [P, SEQ // P])
        conv = sb("conv", [P, 2, KC, GTOK])
        gel = sb("gel", [P, 2, KC, GTOK])
        off = sb("off", [P, 2, GROUP, HR])
        tanhs = sb("tanhs", [P, 2, GROUP, HR])
        pos = sb("pos", [P, 2, GROUP, HR])

        bias_in = sb("bias_in", [EXPERTS, 2 * HID + D])
        bias_part = sb("bias_part", [EXPERTS, NB, 2 * HID + D], BF16)

        pCount = ps("pCount", [P, 512])
        pOff = ps("pOff", [P, 2, GROUP, 256])

        bias_loaded = sem("bias_loaded")
        bias_ready = sem("bias_ready")
        bias_stored = sem("bias_stored")
        weights_in = sem("weights_in2")
        consts = sem("consts2")
        totals_ready = sem("totals_ready")
        prefix_ready = sem("prefix_ready")
        exp_in = sem("exp_in")
        exp_out = sem("exp_out")
        slots_ready = sem("slots_ready")
        chain_sem = sem("route_chain")
        xrow_loaded = [sem(f"xrow_loaded{u}") for u in range(2)]
        scattered = [sem(f"scattered{u}") for u in range(2)]
        idx_set = sem("idx_set")
        go = sem("go")
        conv_mid = sem("conv_mid")
        conv_done = sem("conv_done")
        gel_ready = sem("gel_ready")
        off_done = sem("off_done")
        off_ready = sem("off_ready")
        tanh_ready = sem("tanh_ready")
        pos_chain = sem("pos_chain")
        pos_ready = sem("pos_ready")
        pos_stored = [sem(f"pos_stored{u}") for u in range(2)]

        block = ctx.enter_context(nc.Block())

        @block.gpsimd
        def _(pool):
            nc.gpsimd.memset(ones[:], 1.0).then_inc(consts, 1)
            pool.wait_ge(consts, 1)
            nc.gpsimd.affine_select(out=below[:], in_=ones[:], compare_op=ALU.is_gt, fill=0.0, base=0,
                                    pattern=[[1, P]], channel_multiplier=-1).then_inc(consts, 1)
            nc.gpsimd.iota(rows_i[:], pattern=[[-1, EXPERTS]], base=EXPERTS, channel_multiplier=0).then_inc(consts, 1)
            nc.gpsimd.iota(base_i[:], pattern=[[P, SEQ // P]], base=0, channel_multiplier=1).then_inc(consts, 1)
            nc.gpsimd.iota(keep["tile_exp"][:], pattern=[[P, SLOT_TILES]], base=0, channel_multiplier=0).then_inc(consts, 1)
            pool.sem_inc(go, 1)
            pool.wait_ge(slots_ready, 1)

            def scatter(t, u):
                pool.wait_ge(xrow_loaded[u], 16 * t + 16)
                pool.sem_inc(go, 1)
                for k in range(TOPK):
                    nc.gpsimd.tensor_copy(idx[:, u, k:k + 1], keep["slot"][:, k, ds(2 * t + u, 1)]).then_inc(idx_set, 1)
                pool.wait_ge(idx_set, (2 * t + u + 1) * TOPK)
                pool.sem_inc(go, 1)
                for k in range(TOPK):
                    nc.gpsimd.indirect_dma_start(
                        out=dram["xs"], out_offset=bass.IndirectOffsetOnAxis(ap=idx[:, u, k:k + 1], axis=0),
                        in_=xrow[:, u], in_offset=None).then_inc(scattered[u], 16)

            scatter(0, 0)
            scatter(0, 1)
            with pool.Fori(1, TILES // 2) as t:
                for u in range(2):
                    pool.wait_ge(scattered[u], 16 * TOPK * t)
                    scatter(t, u)
            for u in range(2):
                pool.wait_ge(scattered[u], 16 * TOPK * (TILES // 2))

        @block.sync
        def _(sp):
            sp.dma_start(bias_in[:, 0:2 * HID], io["b_l1"]).then_inc(bias_loaded, 16)
            sp.dma_start(bias_in[:, 2 * HID:], io["b_l2"]).then_inc(bias_loaded, 16)
            sp.dma_start(sel_bias[:], io["sel_bias"].partition_broadcast(P)).then_inc(weights_in, 16)
            sp.dma_start(dw_w[:], io["dw_w"].rearrange("(k p) n -> p k n", p=P)).then_inc(weights_in, 16)
            sp.dma_start(dw_b[:], io["dw_b"].rearrange("(k p) -> p k", p=P),
                         allow_slow_non_contiguous=True).then_inc(weights_in, 16)
            sp.dma_start(pw_w[:], io["pw_wT"].rearrange("(k p) n -> p k n", p=P)).then_inc(weights_in, 16)
            sp.dma_start(pw_b[:], io["pw_b"].partition_broadcast(P)).then_inc(weights_in, 16)

            sp.wait_ge(bias_ready, 1)
            sp.dma_start(dram["bias"].rearrange("k e n -> e k n"), bias_part[:]).then_inc(bias_stored, 16)
            PAIRS_PER_GROUP = TILES // 2 // GROUPS_PER_SEQ

            def load_row(n, u):
                sp.dma_start(xrow[:, u], dram["xn"][ds((2 * n + u) * P, P), :]).then_inc(xrow_loaded[u], 16)

            def group(t, pairs):
                for m in range(pairs):
                    n = t * PAIRS_PER_GROUP + m
                    for u in range(2):
                        sp.wait_ge(scattered[u], 16 * TOPK * (n + 1))
                        load_row(n + 1, u)
                for u in range(2):
                    sp.wait_ge(pos_ready, 2 * t + u + 1)
                    for hg in range(HG):
                        sp.dma_start(
                            dram["pos"][hg, ds(u * SEQ + t * GTOK, GTOK), :].rearrange("(a p) c -> p a c", p=P),
                            pos[:, u, :, hg * GR:(hg + 1) * GR]).then_inc(pos_stored[u], 16)

            load_row(0, 0)
            load_row(0, 1)
            with sp.Fori(0, GROUPS_PER_SEQ - 1) as t:
                group(t, PAIRS_PER_GROUP)
            group(GROUPS_PER_SEQ - 1, PAIRS_PER_GROUP - 1)
            sp.wait_ge(bias_stored, 16)
            for u in range(2):
                sp.wait_ge(pos_stored[u], 16 * HG * (GROUPS_PER_SEQ + 1))

        @block.scalar
        def _(act):
            act.wait_ge(exp_in, 1)
            nc.scalar.activation(expw[:], prod[:], ACT.Exp).then_inc(exp_out, 1)
            act.wait_ge(weights_in, 80)

            def group(t, u):
                n = 2 * t + u
                col = u * (SEQ + 2) + 1 + t * GTOK
                for c in range(KC):
                    nc.scalar.activation(conv[:, u, c], keep["qT"][:, c, ds(col, GTOK)], ACT.Identity,
                                         bias=dw_b[:, c:c + 1], scale=dw_w[:, c, 1:2]).then_inc(conv_mid, 1)
                act.wait_ge(conv_done, n + 1)
                nc.scalar.activation(gel[:, u], conv[:, u], ACT.Gelu).then_inc(gel_ready, 1)
                act.wait_ge(off_ready, n + 1)
                nc.scalar.activation(tanhs[:, u], off[:, u], ACT.Tanh).then_inc(tanh_ready, 1)

            with act.Fori(0, GROUPS_PER_SEQ) as t:
                group(t, 0)
                group(t, 1)

        @block.tensor
        def _(pe):
            pe.wait_ge(totals_ready, 1)
            pe.wait_ge(consts, 2)
            nc.tensor.matmul(pCount[:, 0:EXPERTS], below[:], total[:], start=True, stop=True)
            nc.tensor.matmul(pCount[:, EXPERTS:2 * EXPERTS], ones[:], total[:], start=True,
                             stop=True).then_inc(prefix_ready, 1)
            pe.wait_ge(weights_in, 80)

            def group(t, u):
                n = 2 * t + u
                pe.wait_ge(gel_ready, n + 1)
                for a in range(GROUP):
                    for c in range(KC):
                        mm = nc.tensor.matmul(pOff[:, u, a, 0:HR], gel[:, u, c, a * P:(a + 1) * P], pw_w[:, c],
                                              start=(c == 0), stop=(c == KC - 1))
                mm.then_inc(off_done, 1)

            with pe.Fori(0, GROUPS_PER_SEQ) as t:
                group(t, 0)
                group(t, 1)

        @block.vector
        def _(dve):
            V = nc.vector

            def per_expert(ap):
                return ap.unsqueeze(2).broadcast_to(TE)

            def per_tile(ap):
                return ap[:, None, :].broadcast_to(TE)

            chain = Chain(dve, chain_sem)
            scores = keep["scores"]
            for u in range(2):
                dve.sem_inc(pos_stored[u], 16 * HG)
            for r, a in enumerate(anchors()):
                V.memset(anchor[:, :, r:r + 1], a)
            V.memset(zero_te[:], 0.0)
            dve.wait_ge(consts, 5)
            V.tensor_copy(e_first[:], rows_i[:])
            V.tensor_copy(tile_row[:], keep["tile_exp"][:])
            chain(V.tensor_copy(base[:], base_i[:]))
            dve.wait_ge(weights_in, 80)
            chain(V.tensor_reduce(top[:], scores[:], AX.X, ALU.max))
            V.tensor_tensor(prod[:], scores[:], per_expert(top[:]), ALU.subtract).then_inc(exp_in, 1)
            chain(V.tensor_tensor(biased[:], scores[:], per_tile(sel_bias[:]), ALU.add))
            for k in range(TOPK):
                chain(V.tensor_reduce(top[:], biased[:], AX.X, ALU.max))
                chain(V.tensor_tensor(is_top[:], biased[:], per_expert(top[:]), ALU.is_equal))
                chain(V.tensor_tensor(is_top[:], is_top[:], per_tile(e_first[:]), ALU.mult))
                chain(V.tensor_reduce(top[:], is_top[:], AX.X, ALU.max))
                chain(V.tensor_tensor(chosen[k][:], per_tile(e_first[:]), per_expert(top[:]), ALU.is_equal))
                if k == 0:
                    chain(V.scalar_tensor_tensor(biased[:].rearrange("p t e -> p (t e)"),
                                                 chosen[0][:].rearrange("p t e -> p (t e)"), -3.0e38,
                                                 biased[:].rearrange("p t e -> p (t e)"), ALU.mult, ALU.add))
            dve.wait_ge(exp_out, 1)
            for k in range(TOPK):
                chain(V.tensor_tensor(prod[:], expw[:], chosen[k][:], ALU.mult))
                chain(V.tensor_reduce(picked[:, k], prod[:], AX.X, ALU.add))
            chain(V.tensor_tensor(top[:], picked[:, 0], picked[:, 1], ALU.add))
            chain(V.reciprocal(top[:], top[:]))
            for k in range(TOPK):
                V.tensor_tensor(keep["gate"][:, k], picked[:, k], top[:], ALU.mult)
            chain(V.tensor_tensor(count[:], chosen[0][:], chosen[1][:], ALU.add))
            for e in range(EXPERTS):
                ins = V.tensor_tensor_scan(upto[:, :, e], count[:, :, e], zero_te[:], 0.0, ALU.add, ALU.add)
            chain(ins)
            V.tensor_copy(total[:], upto[:, TILES - 1, :]).then_inc(totals_ready, 1)
            chain(V.tensor_tensor(rank[:], upto[:], count[:], ALU.subtract))
            dve.wait_ge(prefix_ready, 1)
            chain(V.tensor_scalar(rows_i[:], pCount[:, EXPERTS:2 * EXPERTS], float(P - 1), None, ALU.add))
            shift = P.bit_length() - 1
            chain(V.tensor_scalar(rows_i[:], rows_i[:], shift, shift, ALU.logical_shift_right, ALU.logical_shift_left))
            chain(V.tensor_copy(rows[:], rows_i[:]))
            chain(V.tensor_tensor_scan(ends[:], rows[:], zero_te[:, 0:EXPERTS], 0.0, ALU.add, ALU.add))
            chain(V.tensor_tensor(start[:], ends[:], rows[:], ALU.subtract))
            chain(V.tensor_tensor(start[:], start[:], pCount[:, 0:EXPERTS], ALU.add))
            chain(V.tensor_tensor(rank[:], rank[:], per_tile(start[:]), ALU.add))
            for k in range(TOPK):
                chain(V.tensor_tensor(prod[:], rank[:], chosen[k][:], ALU.mult))
                chain(V.tensor_reduce(slot[:, k], prod[:], AX.X, ALU.add))
            V.tensor_copy(keep["slot"][:], slot[:]).then_inc(slots_ready, 1)
            chain(V.tensor_scalar(tile_exp[:], tile_row[:], ends[0:1, 0:1], None, ALU.is_ge))
            for e in range(1, EXPERTS - 1):
                chain(V.scalar_tensor_tensor(tile_exp[:], tile_row[:], ends[0:1, e:e + 1], tile_exp[:],
                                             ALU.is_ge, ALU.add))
            V.tensor_copy(keep["tile_exp"][:], tile_exp[:])

            dve.wait_ge(bias_loaded, 32)
            for k in range(NB):
                chain(V.tensor_copy(bias_part[:, k], bias_in[:]))
                if k < NB - 1:
                    chain(V.tensor_tensor(bias_in[:], bias_in[:], bias_part[:, k], ALU.subtract))
            dve.sem_inc(bias_ready, 1)
            CHAIN = 5

            def group(t, u):
                n = 2 * t + u
                col = u * (SEQ + 2) + 1 + t * GTOK
                dve.wait_ge(conv_mid, KC * (n + 1))
                pc = Chain(dve, pos_chain, n * CHAIN)
                for c in range(KC):
                    ins = V.scalar_tensor_tensor(conv[:, u, c], keep["qT"][:, c, ds(col - 1, GTOK)], dw_w[:, c, 0:1],
                                                 conv[:, u, c], ALU.mult, ALU.add)
                pc(ins)
                for c in range(KC):
                    ins = V.scalar_tensor_tensor(conv[:, u, c], keep["qT"][:, c, ds(col + 1, GTOK)], dw_w[:, c, 2:3],
                                                 conv[:, u, c], ALU.mult, ALU.add)
                ins.then_inc(conv_done, 1)
                dve.wait_ge(off_done, n + 1)
                V.tensor_tensor(off[:, u], pOff[:, u, :, 0:HR], pw_b[:, None, :].broadcast_to([P, GROUP, HR]),
                                ALU.add).then_inc(off_ready, 1)
                dve.wait_ge(tanh_ready, n + 1)
                dve.wait_ge(pos_stored[u], 16 * HG * t + 16 * HG)
                pc(V.tensor_scalar(off[:, u], tanhs[:, u], MAX_OFFSET, None, ALU.mult))
                for a in range(GROUP):
                    tile = t * GROUP + a
                    ins = V.scalar_tensor_tensor(pos[:, u, a], anchor[:].rearrange("p h r -> p (h r)"),
                                                 base[:, ds(tile, 1)], off[:, u, a], ALU.add, ALU.add)
                pc(ins)
                pc(V.tensor_scalar(pos[:, u], pos[:, u], 0.0, float(SEQ - 1), ALU.max, ALU.min))
                for a in range(GROUP):
                    tile = t * GROUP + a
                    ins = V.tensor_scalar(pos[:, u, a], pos[:, u, a], base[:, ds(tile, 1)], None, ALU.subtract)
                pc(ins)
                dve.sem_inc(pos_ready, 1)

            with dve.Fori(0, GROUPS_PER_SEQ) as t:
                group(t, 0)
                group(t, 1)


def mix_block(nc, io, dram, keep):
    with ExitStack() as ctx:
        def sb(name, shape, dt=F32):
            return ctx.enter_context(nc.sbuf_tensor(name, shape, dt))

        def ps(name, shape, dt=F32):
            return ctx.enter_context(nc.psum_tensor(name, shape, dt))

        def sem(name):
            return ctx.enter_context(nc.semaphore(name))

        w1 = sb("w1", [P, KC, EXPERTS * 2 * HID])
        w2 = sb("w2", [P, HC, EXPERTS * D])
        bias = sb("bias", [NB, 2, 2 * HID + D], BF16)
        ones3 = sb("ones3", [NB, P], BF16)
        xs = sb("xs", [P, 2, D])
        xsT = sb("xsT", [P, KC, P])
        act_a = sb("act_a", [P, HID])
        hid = sb("hid", [P, HID])
        hidT = sb("hidT", [P, HC, P])
        ys = sb("ys", [P, 2, D])
        qw = sb("qw", [P, IB * GD])
        kw = sb("kw", [P, WIN * GD])
        vw = sb("vw", [P, WIN * GD])
        pos_in = sb("pos_in", [P, PAIRS])
        pos = sb("posw", [P, PAIRS])
        sprod = sb("sprod", [P, 2, TH * DH])
        oprod = sb("oprod", [P, 2, TH * DH])
        S = sb("S", [P, NJ, TH])
        slope = sb("slope", [P, KNOTS + 2, TH])
        bend = sb("bend", [P, KNOTS, TH])
        G = bend
        last = sb("last", [P, TH])
        terms = sb("terms", [P, 4, PAIRS])
        rel = sb("rel", [P, 1])
        rel_eye = sb("rel_eye", [P, P])
        smax = sb("smax", [P, TH])
        prob = sb("prob", [P, PAIRS])
        psum_e = sb("psum_e", [P, TH])
        wgt = sb("wgt", [P, NJ, TH])
        outs = sb("outs", [P, TH * DH])

        pX = ps("pX", [P, 512])
        pA = ps("pA", [P, 512])
        pB = ps("pB", [P, 512])
        pH = ps("pH", [P, 512])
        pY = ps("pY", [P, 512])
        pS = ps("pS", [P, 2, 512])

        w_loaded = sem("w_loaded")
        ones_set = sem("ones_set")
        rel_ready = sem("rel_ready")
        rel_eye_set = sem("rel_eye_set")
        bias_loaded = [sem(f"bias_loaded{u}") for u in range(2)]
        xs_loaded = [sem(f"xs_loaded{u}") for u in range(2)]
        xsT_done = sem("xsT_done")
        xsT_ready = sem("xsT_ready")
        h_done = sem("h_done")
        a_ready = sem("a_ready")
        hid_ready = sem("hid_ready")
        hidT_done = sem("hidT_done")
        hidT_ready = sem("hidT_ready")
        y_done = sem("y_done")
        ys_ready = sem("ys_ready")
        ys_stored = [sem(f"ys_stored{u}") for u in range(2)]

        qk_loaded = sem("qk_loaded")
        v_loaded = sem("v_loaded")
        pos_loaded = sem("pos_loaded")
        pos_free = sem("pos_free")
        pos_set = sem("pos_set")
        dist_ready = sem("dist_ready")
        sprod_ready = sem("sprod_ready")
        sprod_free = sem("sprod_free")
        term_ready = sem("term_ready")
        term_free = sem("term_free")
        score_done = sem("score_done")
        shift_ready = sem("shift_ready")
        prob_ready = sem("prob_ready")
        oprod_ready = sem("oprod_ready")
        oprod_free = sem("oprod_free")
        outs_stored = sem("outs_stored")
        chain_sem = sem("attn_chain")
        go = sem("go3")
        block = ctx.enter_context(nc.Block())

        LAST = STEPS - 1
        TAIL = STEPS * MOE_PER_STEP
        EARLY = 2
        assert MOE_PER_STEP % 2 == 0

        def run_steps(eng, step):
            step(0, True, False)
            with eng.Fori(1, LAST) as it:
                step(it, False, False)
            step(LAST, False, True)

        @block.sync
        def _(sp):
            sp.dma_start(rel[:], io["rel_scale"].partition_broadcast(P)).then_inc(rel_ready, 16)

            def load_xs(n, u):
                sp.dma_start(xs[:, u], dram["xs"][ds(n * P, P), :]).then_inc(xs_loaded[u], 16)

            def load_bias(n, u):
                e = sp.value_load(keep["tile_exp"][0:1, ds(n, 1)], min_val=0, max_val=EXPERTS - 1)
                sp.dma_start(bias[:, u, :], dram["bias"][:, ds(e, 1), :].rearrange("k o n -> k (o n)")).then_inc(
                    bias_loaded[u], 16)

            def tile_io(n, m, first=False, left=2):
                u = m % 2
                if not first:
                    sp.wait_ge(ys_ready, n)
                    sp.dma_start(dram["ys"][ds((n - 1) * P, P), :], ys[:, 1 - u]).then_inc(ys_stored[1 - u], 16)
                if left >= 1:
                    load_bias(n + 1, 1 - u)
                if left >= 2:
                    load_xs(n + 2, u)

            def load_qk(hg, ib):
                row = ib * IB
                sp.dma_start(qw[:].rearrange("p (i c) -> p i c", i=IB),
                             bass.AP(dram["q"].tensor, (hg * TOKENS + row) * GD,
                                     [[RUN * GD, P], [GD, IB], [1, GD]])).then_inc(qk_loaded, 16)
                sp.dma_start(kw[:].rearrange("p (i c) -> p i c", i=WIN),
                             bass.AP(dram["k"].tensor, (hg * (TOKENS + 2 * REACH) + row) * GD,
                                     [[RUN * GD, P], [GD, WIN], [1, GD]])).then_inc(qk_loaded, 16)

            def load_v(hg, ib):
                sp.dma_start(vw[:].rearrange("p (i c) -> p i c", i=WIN),
                             bass.AP(dram["v"].tensor, (hg * (TOKENS + 2 * REACH) + ib * IB) * GD,
                                     [[RUN * GD, P], [GD, WIN], [1, GD]])).then_inc(v_loaded, 16)

            def load_pos(hg, ib):
                sp.dma_start(pos_in[:].rearrange("p (i c) -> p i c", i=IB),
                             bass.AP(dram["pos"].tensor, (hg * TOKENS + ib * IB) * GR,
                                     [[RUN * GR, P], [GR, IB], [1, GR]])).then_inc(pos_loaded, 16)

            def store_outs(hg, ib):
                sp.dma_start(bass.AP(dram["attn"].tensor, ib * IB * D + hg * GD, [[RUN * D, P], [D, IB], [1, GD]]),
                             outs[:].rearrange("p (i c) -> p i c", i=IB)).then_inc(outs_stored, 16)

            def step(ib, hg, first=False, last=False):
                it = ib * HG + hg
                if not last:
                    nib, nhg = (ib, hg + 1) if hg < HG - 1 else (ib + 1, 0)
                    sp.wait_ge(dist_ready, it + 1)
                    load_pos(nhg, nib)
                    sp.wait_ge(sprod_free, (it + 1) * NJ + 2)
                    load_qk(nhg, nib)
                for m in range(EARLY):
                    tile_io(it * MOE_PER_STEP + m, m, first and m == 0)
                if not first:
                    pib, phg = (ib, hg - 1) if hg > 0 else (ib - 1, HG - 1)
                    sp.wait_ge(oprod_free, it * NJ + 2)
                    store_outs(phg, pib)
                    load_v(hg, ib)
                for m in range(EARLY, MOE_PER_STEP):
                    tile_io(it * MOE_PER_STEP + m, m)

            load_xs(0, 0)
            load_xs(1, 1)
            load_bias(0, 0)
            load_qk(0, 0)
            load_pos(0, 0)
            load_v(0, 0)
            for hg in range(HG):
                step(0, hg, first=hg == 0)
            with sp.Fori(1, NIB - 1) as ib:
                for hg in range(HG):
                    step(ib, hg)
            for hg in range(HG):
                step(NIB - 1, hg, last=hg == HG - 1)
            for m in range(MOE_PER_STEP):
                tile_io(TAIL + m, m, left=MOE_PER_STEP - 1 - m)
            sp.wait_ge(ys_ready, SLOT_TILES)
            sp.dma_start(dram["ys"][SLOTS - P:SLOTS, :], ys[:, 1]).then_inc(ys_stored[1], 16)
            sp.wait_ge(oprod_free, STEPS * NJ + 2)
            store_outs(HG - 1, NIB - 1)
            sp.wait_ge(outs_stored, 16 * (STEPS + 1))
            for u in range(2):
                sp.wait_ge(ys_stored[u], 16 * (SLOT_TILES // 2 + 1))

        @block.gpsimd
        def _(pool):
            for k in range(KC):
                pool.dma_start(w1[:, k].rearrange("p (e n) -> p e n", e=EXPERTS),
                               io["w_l1"].rearrange("e (k p) n -> k p e n", p=P)[k]).then_inc(w_loaded, 16)
            for k in range(HC):
                pool.dma_start(w2[:, k].rearrange("p (e n) -> p e n", e=EXPERTS),
                               io["w_l2"].rearrange("e (k p) n -> k p e n", p=P)[k]).then_inc(w_loaded, 16)

            def q_times_k(it):
                pool.wait_ge(qk_loaded, 32 * it + 32)
                for j in range(NJ):
                    pool.wait_ge(sprod_free, it * NJ + j + 1)
                    nc.gpsimd.tensor_tensor(sprod[:, j % 2],
                                            qw[:], kw[:, j * GD:j * GD + IB * GD], ALU.mult).then_inc(sprod_ready, 1)

            def sum_values(it):
                pool.wait_ge(outs_stored, 16 * it + 16)
                for j in range(NJ):
                    pool.wait_ge(oprod_ready, it * NJ + j + 1)
                    if j == 0:
                        pool.sem_inc(go, 1)
                        ins = nc.gpsimd.tensor_copy(outs[:], oprod[:, 0])
                    else:
                        pool.wait_ge(oprod_free, it * NJ + j + 2)
                        ins = nc.gpsimd.tensor_tensor(outs[:], outs[:], oprod[:, j % 2], ALU.add)
                    ins.then_inc(oprod_free, 1)

            def step(it, first, last):
                if not first:
                    sum_values(it - 1)
                if not last:
                    q_times_k(it + 1)

            q_times_k(0)
            run_steps(pool, step)
            sum_values(LAST)

        @block.scalar
        def _(act):
            def evacuate_x(n):
                act.wait_ge(xsT_done, n + 1)
                nc.scalar.activation(xsT[:].rearrange("p k t -> p (k t)"), pX[:, 0:D], ACT.Identity).then_inc(xsT_ready, 1)

            def evacuate_y(n, u, pair):
                act.wait_ge(y_done, n + 1)
                act.wait_ge(ys_stored[u], 16 * pair + 16)
                nc.scalar.activation(ys[:, u], pY[:, 0:D], ACT.Identity).then_inc(ys_ready, 1)

            def tile_slot(n, m, pair, first=False, last=False):
                act.wait_ge(h_done, n + 1)
                nc.scalar.activation(act_a[:], pA[:], ACT.Silu).then_inc(a_ready, 1)
                if not first:
                    evacuate_y(n - 1, (m + 1) % 2, pair - 1 if m % 2 == 0 else pair)
                if not last:
                    evacuate_x(n + 1)
                act.wait_ge(hidT_done, n + 1)
                nc.scalar.activation(hidT[:].rearrange("p k t -> p (k t)"), pH[:], ACT.Identity).then_inc(hidT_ready, 1)

            def step(it, first, last):
                act.wait_ge(pos_loaded, 16 * it + 16)
                act.wait_ge(pos_free, it + 1)
                nc.scalar.activation(pos[:], pos_in[:], ACT.Identity).then_inc(pos_set, 1)
                nc.scalar.activation(prob[:], pos_in[:], ACT.Abs).then_inc(dist_ready, 1)
                for m in range(MOE_PER_STEP):
                    if m == EARLY:
                        act.wait_ge(shift_ready, it + 1)
                        nc.scalar.activation(prob[:], prob[:], ACT.Exp, scale=SCALE).then_inc(prob_ready, 1)
                    tile_slot(it * MOE_PER_STEP + m, m, it * (MOE_PER_STEP // 2) + m // 2, first and m == 0)

            evacuate_x(0)
            run_steps(act, step)
            for m in range(MOE_PER_STEP):
                tile_slot(TAIL + m, m, TAIL // 2 + m // 2, last=m == MOE_PER_STEP - 1)
            evacuate_y(SLOT_TILES - 1, 1, SLOT_TILES // 2 - 1)

        @block.tensor
        def _(pe):
            pe.wait_ge(w_loaded, 16 * (KC + HC))
            pe.wait_ge(ones_set, 1)
            pe.wait_ge(rel_eye_set, 1)
            eye = keep["ident"]

            def expert(n):
                return pe.value_load(keep["tile_exp"][0:1, ds(n, 1)], min_val=0, max_val=EXPERTS - 1)

            def transpose_x(n, u, pair):
                pe.wait_ge(xs_loaded[u], 16 * pair + 16)
                for k in range(KC):
                    tr = nc.tensor.transpose(pX[:, k * P:(k + 1) * P], xs[:, u, k * P:(k + 1) * P], eye[:])
                tr.then_inc(xsT_done, 1)

            def times_w2(n, u):
                e = expert(n)
                pe.wait_ge(hidT_ready, n + 1)
                for k in range(HC):
                    nc.tensor.matmul(pY[:, 0:D], hidT[:, k], w2[:, k, ds(e * D, D)], start=(k == 0), stop=False)
                nc.tensor.matmul(pY[:, 0:D], ones3[:], bias[:, u, 2 * HID:], start=False, stop=True).then_inc(y_done, 1)

            def tile_slot(n, m, pair, first=False, last=False):
                u = m % 2
                e = expert(n)
                pe.wait_ge(bias_loaded[u], 16 * pair + 16)
                pe.wait_ge(xsT_ready, n + 1)
                for o, dst in ((0, pA), (1, pB)):
                    for k in range(KC):
                        nc.tensor.matmul(dst[:], xsT[:, k], w1[:, k, ds(e * 2 * HID + o * HID, HID)],
                                         start=(k == 0), stop=False)
                    mm = nc.tensor.matmul(dst[:], ones3[:], bias[:, u, o * HID:(o + 1) * HID], start=False, stop=True)
                mm.then_inc(h_done, 1)
                if not first:
                    times_w2(n - 1, 1 - u)
                if not last:
                    transpose_x(n + 1, 1 - u, pair if u == 0 else pair + 1)
                pe.wait_ge(hid_ready, n + 1)
                for k in range(HC):
                    tr = nc.tensor.transpose(pH[:, k * P:(k + 1) * P], hid[:, k * P:(k + 1) * P], eye[:])
                tr.then_inc(hidT_done, 1)

            def step(it, first, last):
                def slot(m):
                    tile_slot(it * MOE_PER_STEP + m, m, it * (MOE_PER_STEP // 2) + m // 2, first and m == 0)

                for j in range(KNOTS):
                    pe.wait_ge(term_ready, it * KNOTS + j + 1)
                    for half in range(2):
                        cols = slice(half * PAIRS // 2, (half + 1) * PAIRS // 2)
                        mm = nc.tensor.matmul(pS[:, half, 0:PAIRS // 2], eye[:], terms[:, j % 4, cols],
                                              start=(j == 0), stop=False)
                    mm.then_inc(term_free, 1)
                    if (j + 1) % (KNOTS // EARLY) == KNOTS // EARLY // 2:
                        slot(j // (KNOTS // EARLY))
                pe.wait_ge(dist_ready, it + 1)
                for half in range(2):
                    cols = slice(half * PAIRS // 2, (half + 1) * PAIRS // 2)
                    nc.tensor.matmul(pS[:, half, 0:PAIRS // 2], rel_eye[:], prob[:, cols], start=False, stop=False)
                for half in range(2):
                    const = last_bc[:, half * TH // 2:(half + 1) * TH // 2].unsqueeze(2).broadcast_to(
                        [P, TH // 2, SAMPLES])
                    mm = nc.tensor.matmul(pS[:, half, 0:PAIRS // 2].rearrange("p (t r) -> p t r", r=SAMPLES),
                                          eye[:], const, start=False, stop=True)
                mm.then_inc(score_done, 1)
                for m in range(EARLY, MOE_PER_STEP):
                    slot(m)

            last_bc = last
            transpose_x(0, 0, 0)
            run_steps(pe, step)
            for m in range(MOE_PER_STEP):
                tile_slot(TAIL + m, m, TAIL // 2 + m // 2, last=m == MOE_PER_STEP - 1)
            times_w2(SLOT_TILES - 1, 1)

        @block.vector
        def _(dve):
            V = nc.vector
            for u in range(2):
                dve.sem_inc(ys_stored[u], 16)
            dve.sem_inc(pos_free, 1)
            dve.sem_inc(sprod_free, 2)
            dve.sem_inc(term_free, 4)
            dve.sem_inc(oprod_free, 2)
            dve.sem_inc(outs_stored, 16)
            V.memset(ones3[:], 1.0).then_inc(ones_set, 1)
            dve.wait_ge(rel_ready, 16)
            V.tensor_scalar(rel_eye[:], keep["ident"][:], rel[:, 0:1], -1.0 / SCALE, ALU.mult,
                            ALU.mult).then_inc(rel_eye_set, 1)

            def gate_hidden(n):
                dve.wait_ge(h_done, n + 1)
                dve.wait_ge(a_ready, n + 1)
                V.tensor_tensor(hid[:], act_a[:], pB[:], ALU.mult).then_inc(hid_ready, 1)

            def pairs(ap):
                return ap.rearrange("p (t r) -> p t r", r=SAMPLES)

            def each_sample(ap):
                return ap.unsqueeze(2).broadcast_to([P, TH, SAMPLES])

            def sum_qk(it, j):
                dve.wait_ge(sprod_ready, it * NJ + j + 1)
                V.tensor_reduce(S[:, j], sprod[:, j % 2].rearrange("p (t d) -> p t d", d=DH), AX.X,
                                ALU.add).then_inc(sprod_free, 1)

            BEND_CHAIN = 3

            def bends(it, chain):
                dve.wait_ge(sprod_free, (it + 1) * NJ + 2)
                chain(V.tensor_tensor(slope[:, 0:KNOTS], S[:, 1:NJ], S[:, 0:KNOTS], ALU.subtract))
                V.tensor_copy(bend[:, 0], slope[:, 0])
                V.tensor_tensor(bend[:, 1:KNOTS], slope[:, 1:KNOTS], slope[:, 0:KNOTS - 1], ALU.subtract)
                chain(V.tensor_scalar(last[:], S[:, NJ - 1], -float(REACH - 1), None, ALU.mult))
                chain(V.scalar_tensor_tensor(last[:], S[:, NJ - 2], float(REACH), last[:], ALU.mult, ALU.add))

            def weigh_values(it, j):
                dve.wait_ge(oprod_free, it * NJ + j + 1)
                V.tensor_tensor(oprod[:, j % 2].rearrange("p (t d) -> p t d", d=DH),
                                vw[:, j * GD:j * GD + IB * GD].rearrange("p (t d) -> p t d", d=DH),
                                wgt[:, j].unsqueeze(2).broadcast_to([P, TH, DH]), ALU.mult).then_inc(oprod_ready, 1)

            CHAIN = 16

            def step(it, first, last):
                chain = Chain(dve, chain_sem, it * CHAIN + BEND_CHAIN)

                def gate(m):
                    gate_hidden(it * MOE_PER_STEP + m)

                dve.wait_ge(pos_set, it + 1)
                if not first:
                    dve.wait_ge(v_loaded, 16 * it)
                for j in range(NJ):
                    if j < KNOTS:
                        dve.wait_ge(term_free, it * KNOTS + j + 1)
                        V.scalar_tensor_tensor(pairs(terms[:, j % 4]), pairs(pos[:]), float(j - REACH),
                                               each_sample(bend[:, j]), ALU.max, ALU.mult).then_inc(term_ready, 1)
                    if not first:
                        weigh_values(it - 1, j)
                    if j % (KNOTS // EARLY) == KNOTS // EARLY - 2:
                        gate(j // (KNOTS // EARLY))
                dve.wait_ge(score_done, it + 1)
                sc = pS[:, :, 0:PAIRS // 2].rearrange("p b (t r) -> p b t r", r=SAMPLES)
                chain(V.tensor_reduce(smax[:].rearrange("p (b t) -> p b t", b=2), sc, AX.X, ALU.max))
                for half in range(2):
                    cols = slice(half * TH // 2, (half + 1) * TH // 2)
                    ins = V.tensor_tensor(pairs(prob[:])[:, cols], pairs(pS[:, half, 0:PAIRS // 2]),
                                          each_sample(smax[:])[:, cols], ALU.subtract)
                ins.then_inc(shift_ready, 1)
                done = 0
                for c in range(KNOTS // 4):
                    if c == 0:
                        if not last:
                            sum_qk(it + 1, 0)
                            sum_qk(it + 1, 1)
                            done = 2
                        dve.wait_ge(prob_ready, it + 1)
                        V.tensor_reduce(psum_e[:], pairs(prob[:]), AX.X, ALU.add)
                    for jj in range(4):
                        j = 4 * c + jj
                        ins = V.scalar_tensor_tensor(terms[:, jj], pos[:], float(j - REACH), prob[:], ALU.max, ALU.mult)
                        if jj == 3:
                            chain(ins)
                        if not last and done < NJ:
                            sum_qk(it + 1, done)
                            done += 1
                        if j % 3 == 0:
                            gate(EARLY + j // 3)
                    chain(V.tensor_reduce(G[:, 4 * c:4 * c + 4], terms[:].rearrange("p j (t r) -> p j t r", r=SAMPLES),
                                          AX.X, ALU.add))
                V.memset(slope[:, 0], 0.0).then_inc(pos_free, 1)
                V.tensor_tensor(slope[:, 1:KNOTS], G[:, 1:KNOTS], G[:, 0:KNOTS - 1], ALU.subtract)
                V.scalar_tensor_tensor(slope[:, KNOTS], psum_e[:], float(REACH), G[:, KNOTS - 1], ALU.mult, ALU.subtract)
                chain(V.tensor_copy(slope[:, KNOTS + 1], psum_e[:]))
                chain(V.reciprocal(psum_e[:], psum_e[:]))
                chain(V.tensor_tensor(wgt[:], slope[:, 1:KNOTS + 2], slope[:, 0:KNOTS + 1], ALU.subtract))
                chain(V.tensor_tensor(wgt[:], wgt[:], psum_e[:, None, :].broadcast_to([P, NJ, TH]), ALU.mult))
                if not last:
                    assert done == NJ
                    bends(it + 1, chain)
                    assert chain.n == CHAIN, chain.n

            for j in range(NJ):
                sum_qk(0, j)
            bends(0, Chain(dve, chain_sem))
            run_steps(dve, step)
            dve.wait_ge(v_loaded, 16 * STEPS)
            for j in range(NJ):
                weigh_values(LAST, j)
                if j % 2 == 1:
                    gate_hidden(TAIL + j // 2)


def finish_block(nc, io, dram, keep):
    with ExitStack() as ctx:
        def sb(name, shape, dt=F32):
            return ctx.enter_context(nc.sbuf_tensor(name, shape, dt))

        def ps(name, shape, dt=F32):
            return ctx.enter_context(nc.psum_tensor(name, shape, dt))

        def sem(name):
            return ctx.enter_context(nc.semaphore(name))

        wo = sb("wo", [P, KC, D])
        bo = sb("bo", [P, D])
        xr = sb("xr", [P, 2, D])
        at = sb("at", [P, 2, D])
        atT = sb("atT", [P, 2, KC, P])
        yk = sb("yk", [P, 2, TOPK, D])
        idx = sb("idx4", [P, 2, TOPK], U32)
        moe = sb("moe", [P, 2, D])
        gate = sb("gate4", [P, 2, D])
        proj = sb("proj", [P, 2, D])
        pT = ps("pT4", [P, 2, 512])
        pO = ps("pO4", [P, 2, 512])

        weights_in = sem("weights_in4")
        x_loaded = [sem(f"x_loaded4{u}") for u in range(2)]
        y_loaded = [sem(f"y_loaded4{u}") for u in range(2)]
        idx_set = sem("idx_set4")
        go = sem("go4")
        atT_done = sem("atT_done")
        atT_ready = sem("atT_ready")
        proj_done = sem("proj_done")
        moe_ready = sem("moe_ready")
        gate_ready = sem("gate_ready")
        chain_sem = sem("final_chain")
        out_ready = sem("out_ready")
        out_stored = [sem(f"out_stored{u}") for u in range(2)]
        block = ctx.enter_context(nc.Block())

        @block.sync
        def _(sp):
            sp.dma_start(wo[:], io["w_oT"].rearrange("(k p) n -> p k n", p=P)).then_inc(weights_in, 16)
            sp.dma_start(bo[:], io["b_o"].partition_broadcast(P)).then_inc(weights_in, 16)
            with sp.Fori(0, TILES // 2) as t:
                for u in range(2):
                    row = (2 * t + u) * P
                    sp.wait_ge(out_ready, 2 * t + u + 1)
                    sp.dma_start(xr[:, u], io["x"][ds(row, P), :]).then_inc(x_loaded[u], 16)
                    sp.dma_start(at[:, u], dram["attn"][ds(row, P), :]).then_inc(x_loaded[u], 16)

        @block.gpsimd
        def _(pool):
            def fetch(t, u):
                for k in range(TOPK):
                    nc.gpsimd.tensor_copy(idx[:, u, k:k + 1], keep["slot"][:, k, ds(2 * t + u, 1)]).then_inc(idx_set, 1)
                pool.wait_ge(idx_set, (2 * t + u + 1) * TOPK)
                pool.sem_inc(go, 1)
                for k in range(TOPK):
                    nc.gpsimd.indirect_dma_start(
                        out=yk[:, u, k], out_offset=None, in_=dram["ys"],
                        in_offset=bass.IndirectOffsetOnAxis(ap=idx[:, u, k:k + 1], axis=0)).then_inc(y_loaded[u], 16)

            with pool.Fori(0, TILES // 2) as t:
                for u in range(2):
                    pool.wait_ge(moe_ready, 2 * t + u + 1)
                    pool.sem_inc(go, 1)
                    fetch(t, u)

        @block.tensor
        def _(pe):
            pe.wait_ge(weights_in, 32)
            with pe.Fori(0, TILES // 2) as t:
                for u in range(2):
                    n = 2 * t + u
                    pe.wait_ge(x_loaded[u], 32 * t + 32)
                    for k in range(KC):
                        tr = nc.tensor.transpose(pT[:, u, k * P:(k + 1) * P], at[:, u, k * P:(k + 1) * P], keep["ident"][:])
                    tr.then_inc(atT_done, 1)
                    pe.wait_ge(atT_ready, n + 1)
                    for k in range(KC):
                        mm = nc.tensor.matmul(pO[:, u, 0:D], atT[:, u, k], wo[:, k], start=(k == 0), stop=(k == KC - 1))
                    mm.then_inc(proj_done, 1)

        @block.scalar
        def _(act):
            with act.Fori(0, TILES // 2) as t:
                for u in range(2):
                    n = 2 * t + u
                    act.wait_ge(atT_done, n + 1)
                    nc.scalar.activation(atT[:, u].rearrange("p k t -> p (k t)"), pT[:, u, 0:D],
                                         ACT.Identity).then_inc(atT_ready, 1)
                    act.wait_ge(moe_ready, n + 3)
                    nc.scalar.activation(gate[:, u], moe[:, u], ACT.Silu).then_inc(gate_ready, 1)
                    act.wait_ge(out_ready, n + 3)
                    act.dma_start(io["out"][ds(n * P, P), :], proj[:, u]).then_inc(out_stored[u], 16)
            for u in range(2):
                act.wait_ge(out_stored[u], 16 * (TILES // 2 + 1))

        @block.vector
        def _(dve):
            V = nc.vector
            for u in range(2):
                dve.sem_inc(out_stored[u], 16)
            dve.sem_inc(moe_ready, 2)
            dve.sem_inc(out_ready, 2)
            dve.wait_ge(weights_in, 32)
            CHAIN = 3
            with dve.Fori(0, TILES // 2) as t:
                for u in range(2):
                    n = 2 * t + u
                    chain = Chain(dve, chain_sem, n * CHAIN)
                    dve.wait_ge(y_loaded[u], 32 * t + 32)
                    chain(V.tensor_scalar(moe[:, u], yk[:, u, 0], keep["gate"][:, 0, ds(n, 1)], None, ALU.mult))
                    V.scalar_tensor_tensor(moe[:, u], yk[:, u, 1], keep["gate"][:, 1, ds(n, 1)], moe[:, u],
                                           ALU.mult, ALU.add).then_inc(moe_ready, 1)
                    dve.wait_ge(proj_done, n + 1)
                    dve.wait_ge(out_stored[u], 16 * t + 16)
                    chain(V.tensor_tensor(proj[:, u], pO[:, u, 0:D], bo[:], ALU.add))
                    dve.wait_ge(gate_ready, n + 1)
                    chain(V.tensor_tensor(proj[:, u], proj[:, u], gate[:, u], ALU.mult))
                    V.tensor_tensor(proj[:, u], proj[:, u], xr[:, u], ALU.add).then_inc(out_ready, 1)


def build(nc, io):
    dram = {
        "xn": nc.dram_tensor("xn_rows", [TOKENS, D], F32).ap(),
        "q": nc.dram_tensor("q_rows", [HG, TOKENS, GD], F32).ap(),
        "k": nc.dram_tensor("k_rows", [HG, TOKENS + 2 * REACH, GD], F32).ap(),
        "v": nc.dram_tensor("v_rows", [HG, TOKENS + 2 * REACH, GD], F32).ap(),
        "pos": nc.dram_tensor("pos_rows", [HG, TOKENS, GR], F32).ap(),
        "xs": nc.dram_tensor("xs_slots", [SLOTS, D], F32).ap(),
        "ys": nc.dram_tensor("ys_slots", [SLOTS, D], F32).ap(),
        "bias": nc.dram_tensor("bias_parts", [NB, EXPERTS, 2 * HID + D], BF16).ap(),
        "attn": nc.dram_tensor("attn_rows", [TOKENS, D], F32).ap(),
    }
    with ExitStack() as ctx:
        def sb(name, shape, dt=F32):
            return ctx.enter_context(nc.sbuf_tensor(name, shape, dt))

        keep = {
            "ident": sb("ident", [P, P]),
            "scores": sb("scores", [P, TILES, EXPERTS]),
            "gate": sb("gate", [P, TOPK, TILES]),
            "slot": sb("slot_u", [P, TOPK, TILES], U32),
            "tile_exp": sb("tile_exp_i", [1, SLOT_TILES], I32),
        }
        with nc.sbuf_tensor("qT", [P, KC, BATCH * (SEQ + 2)], F32) as qT:
            keep["qT"] = qT
            project_block(nc, io, dram, keep)
            route_block(nc, io, dram, keep)
        mix_block(nc, io, dram, keep)
        finish_block(nc, io, dram, keep)


def kernel(**inputs):
    import concourse.bacc as bacc
    from concourse.bass_utils import run_bass_kernel_spmd

    a = {k: np.asarray(v) for k, v in inputs.items()}
    t = np.ascontiguousarray
    arrays = {
        "x": a["L0_attn_x"].reshape(TOKENS, D),
        "w_qkvT": t(np.concatenate([a["L0_attn_wq"], a["L0_attn_wk"], a["L0_attn_wv"]], 0).T),
        "b_qkv": np.concatenate([a["L0_attn_bq"], a["L0_attn_bk"], a["L0_attn_bv"]]),
        "w_oT": t(a["L0_attn_wo"].T),
        "b_o": a["L0_attn_bo"],
        "dw_w": a["L0_attn_dw_w"].reshape(D, 3),
        "dw_b": a["L0_attn_dw_b"],
        "pw_wT": t(a["L0_attn_pw_w"].T),
        "pw_b": a["L0_attn_pw_b"],
        "rel_scale": a["L0_attn_rel_scale"].reshape(1),
        "w_rT": t(a["L0_ffn_Wr"].T),
        "b_r": a["L0_ffn_br"],
        "w_l1": a["L0_ffn_Wl1"],
        "b_l1": a["L0_ffn_bl1"],
        "w_l2": a["L0_ffn_Wl2"],
        "b_l2": a["L0_ffn_bl2"],
        "sel_bias": a["L0_ffn_biases_N"],
    }
    nc = bacc.Bacc("TRN2", target_bir_lowering=False, num_devices=1)
    io = {k: nc.dram_tensor(f"in_{k}", v.shape, F32, kind="ExternalInput").ap() for k, v in arrays.items()}
    io["out"] = nc.dram_tensor("out", (TOKENS, D), F32, kind="ExternalOutput").ap()
    build(nc, io)
    r = run_bass_kernel_spmd(nc, [{f"in_{k}": t(v) for k, v in arrays.items()}], core_ids=[0])
    return r.results[0]["out"].reshape(BATCH, SEQ, D)
```

```python
from contextlib import ExitStack

import concourse.bass as bass
import numpy as np
from concourse import mybir

P = 128
F32 = mybir.dt.float32
BF16 = mybir.dt.bfloat16
I32 = mybir.dt.int32
U32 = mybir.dt.uint32
ACT = mybir.ActivationFunctionType
ALU = mybir.AluOpType
AX = mybir.AxisListType
ds = bass.ds

BATCH, SEQ, D = 2, 4096, 256
TOKENS = BATCH * SEQ
TILES = TOKENS // P
KC = D // P
HEADS, SAMPLES = 16, 12
DH = D // HEADS
HR = HEADS * SAMPLES
RHO, MAX_OFFSET = 2.0, 6.0
REACH = int(RHO + MAX_OFFSET)
LN_EPS = 1e-5

EXPERTS, HID, TOPK = 8, 512, 2
NB = 3
HC = HID // P
SLOT_TILES = TOKENS * TOPK // P + EXPERTS
SLOTS = SLOT_TILES * P

GROUP = 4
GTOK = GROUP * P
GROUPS_PER_SEQ = SEQ // GTOK

HG = 4
GH = HEADS // HG
GD = GH * DH
GR = GH * SAMPLES
RUN = TOKENS // P
IB = 16
NIB = RUN // IB
WIN = IB + 2 * REACH
SLOPES = P + 2 * REACH - 1
SROWS = 32
S_ROW = (SROWS + 2 * REACH - 1) * GH
S_PITCH = S_ROW + GH
KSLOTS = 4
XSLOTS = 4
FSLOTS = 8
TH = IB * GH
PAIRS = TH * SAMPLES
NJ = 2 * REACH + 1
KNOTS = 2 * REACH
STEPS = HG * NIB
SCALE = float(DH) ** -0.5
GSUM = 4
MOE_PER_STEP = SLOT_TILES // (STEPS - 1)
FIRST_TILES = 2
assert FIRST_TILES % 2 == 0 and 0 < SLOT_TILES - FIRST_TILES - (STEPS - 2) * MOE_PER_STEP <= MOE_PER_STEP


def anchors():
    step = np.arange(SAMPLES, dtype=np.float32) * np.float32(1.0 / (SAMPLES - 1))
    a = np.float32(-RHO) * (np.float32(1) - step) + np.float32(RHO) * step
    a[-1] = RHO
    return [float(v) for v in a]


class Chain:

    def __init__(self, eng, sem, base=0):
        self.eng, self.sem, self.base, self.n = eng, sem, base, 0

    def count(self, ins):
        self.n += 1
        ins.then_inc(self.sem, 1)

    def wait(self):
        self.eng.wait_ge(self.sem, self.base + self.n)

    def __call__(self, ins):
        self.count(ins)
        self.wait()


def project_block(nc, io, dram, keep):
    with ExitStack() as ctx:
        def sb(name, shape, dt=F32):
            return ctx.enter_context(nc.sbuf_tensor(name, shape, dt))

        def ps(name, shape, dt=F32):
            return ctx.enter_context(nc.psum_tensor(name, shape, dt))

        def sem(name):
            return ctx.enter_context(nc.semaphore(name))

        x_in = sb("x_in", [P, 2, GROUP, D])
        xn = sb("xn", [P, 2, GROUP, D])
        xnT = sb("xnT", [P, 2, KC, GTOK])
        wqkv = sb("wqkv", [P, KC, 3 * D])
        wr = sb("wr", [P, KC, EXPERTS])
        bv_bc = sb("bv_bc", [P, D])
        br_bc = sb("br_bc", [P, EXPERTS])
        bqk_col = sb("bqk_col", [P, 2 * KC])
        v = sb("v", [P, 2, GROUP, D])
        zeros = sb("zeros", [P, 4 * D])
        stats = sb("stats", [P, GROUP, 6])
        mv = sb("mv", [P, GROUP, 2])
        var = sb("var", [P, GROUP])
        std = sb("std", [P, GROUP])
        rstd = sb("rstd", [P, GROUP])
        bias_in = sb("bias_in", [EXPERTS, 2 * HID + D])
        bias_part = sb("bias_part", [EXPERTS, NB, 2 * HID + D], BF16)

        pT = ps("pT", [P, KC, GTOK])
        pQK = ps("pQK", [P, 2, GTOK])
        pV = ps("pV", [P, 2, 2, D])
        pR = ps("pR", [P, 512])

        weights_in = sem("weights_in")
        bias_loaded = sem("bias_loaded")
        bias_chain = sem("bias_chain")
        bias_stored = sem("bias_stored")
        zeros_set = sem("zeros_set")
        ident_set = sem("ident_set")
        pads_set = sem("pads_set")
        x_loaded = [sem(f"x_loaded{u}") for u in range(2)]
        xn_ready = sem("xn_ready")
        xn_stored = [sem(f"xn_stored{u}") for u in range(2)]
        var_ready = sem("var_ready")
        std_ready = sem("std_ready")
        xT_done = sem("xT_done")
        xnT_ready = sem("xnT_ready")
        qk_done = sem("qk_done")
        qk_free = sem("qk_free")
        k_sloped = sem("k_sloped")
        r_done = sem("r_done")
        r_free = sem("r_free")
        v_done = sem("v_done")
        v_free = sem("v_free")
        v_stored = [sem(f"v_stored{u}") for u in range(2)]
        filled = sem("filled")
        go = sem("go1")
        ln_chain = sem("ln_chain")
        NQK = 2 * KC
        NV = GROUP // 2

        block = ctx.enter_context(nc.Block())

        @block.sync
        def _(sp):
            def load_x(t, u):
                sp.dma_start(x_in[:, u], io["x"][ds(u * SEQ + t * GTOK, GTOK), :].rearrange(
                    "(a p) c -> p a c", p=P)).then_inc(x_loaded[u], 16)

            def store_xn(t, u):
                sp.wait_ge(xn_ready, 2 * t + u + 1)
                sp.dma_start(dram["xn"][ds(u * SEQ + t * GTOK, GTOK), :].rearrange("(a p) c -> p a c", p=P),
                             xn[:, u]).then_inc(xn_stored[u], 16)

            def store_v(t, u):
                sp.wait_ge(v_free, (2 * t + u + 1) * NV + 2)
                for hg in range(HG):
                    sp.dma_start(dram["v"][hg, ds(REACH + u * SEQ + t * GTOK, GTOK), :].rearrange("(a p) c -> p a c", p=P),
                                 v[:, u, :, hg * GD:(hg + 1) * GD]).then_inc(v_stored[u], 16)

            load_x(0, 0)
            load_x(0, 1)
            sp.dma_start(bias_in[:, 0:2 * HID], io["b_l1"]).then_inc(bias_loaded, 16)
            sp.dma_start(bias_in[:, 2 * HID:], io["b_l2"]).then_inc(bias_loaded, 16)
            store_xn(0, 0)
            load_x(1, 0)
            with sp.Fori(0, GROUPS_PER_SEQ - 2) as t:
                store_xn(t, 1)
                load_x(t + 1, 1)
                store_v(t, 0)
                store_xn(t + 1, 0)
                load_x(t + 2, 0)
                store_v(t, 1)
            end = GROUPS_PER_SEQ - 1
            store_xn(end - 1, 1)
            load_x(end, 1)
            store_v(end - 1, 0)
            store_xn(end, 0)
            store_v(end - 1, 1)
            store_xn(end, 1)
            store_v(end, 0)
            store_v(end, 1)
            sp.wait_ge(bias_chain, 2 * NB - 1)
            sp.dma_start(dram["bias"].rearrange("k e n -> e k n"), bias_part[:]).then_inc(bias_stored, 16)
            sp.wait_ge(pads_set, 16 * 2 * HG)
            sp.wait_ge(filled, 16 * (SLOTS // (4 * P)))
            sp.wait_ge(bias_stored, 16)
            for u in range(2):
                sp.wait_ge(xn_stored[u], 16 * GROUPS_PER_SEQ + 16)
                sp.wait_ge(v_stored[u], 16 * HG * (GROUPS_PER_SEQ + 1))

        @block.gpsimd
        def _(pool):
            nc.gpsimd.memset(zeros[:], 0.0).then_inc(zeros_set, 1)
            nc.gpsimd.memset(keep["ident"][:], 0.0).then_inc(zeros_set, 1)
            pool.wait_ge(zeros_set, 2)
            nc.gpsimd.affine_select(out=keep["ident"][:], in_=keep["ident"][:], compare_op=ALU.not_equal, fill=1.0,
                                    base=0, pattern=[[-1, P]], channel_multiplier=1).then_inc(ident_set, 1)
            for hg in range(HG):
                for row in (0, REACH + TOKENS):
                    pool.dma_start(dram["v"][hg, row:row + REACH, :], zeros[0:REACH, 0:GD]).then_inc(pads_set, 16)
            def fill(n):
                pool.dma_start(dram["xs"][ds(n * 4 * P, 4 * P), :].rearrange("(p a) c -> p (a c)", p=P),
                               zeros[:]).then_inc(filled, 16)

            def slopes_of_k(t, u):
                n = BATCH * t + u
                pool.wait_ge(k_sloped, n + 1)
                pool.sem_inc(go, 1)
                pool.wait_ge(qk_free, (n + 1) * NQK + 2)
                col = REACH + u * (SEQ + 1) + t * GTOK
                nc.gpsimd.tensor_tensor(keep["kT"][:, :, ds(col - 1, GTOK)], keep["kT"][:, :, ds(col, GTOK)],
                                        keep["kT"][:, :, ds(col - 1, GTOK)], ALU.subtract).then_inc(k_sloped, 1)

            FILLS = SLOTS // (4 * P)
            PER_GROUP = FILLS // (BATCH * GROUPS_PER_SEQ)
            with pool.Fori(0, GROUPS_PER_SEQ) as t:
                for u in range(BATCH):
                    n = BATCH * t + u
                    pool.wait_ge(xn_ready, n + 1)
                    pool.sem_inc(go, 1)
                    for m in range(PER_GROUP):
                        fill(n * PER_GROUP + m)
                    slopes_of_k(t, u)
            for m in range(PER_GROUP * BATCH * GROUPS_PER_SEQ, FILLS):
                fill(m)

        @block.scalar
        def _(act):
            act.dma_start(wqkv[:], io["w_qkvT"].rearrange("(k p) n -> p k n", p=P)).then_inc(weights_in, 16)
            act.dma_start(wr[:], io["w_rT"].rearrange("(k p) n -> p k n", p=P)).then_inc(weights_in, 16)
            act.dma_start(bv_bc[:], io["b_qkv"][2 * D:3 * D].partition_broadcast(P)).then_inc(weights_in, 16)
            act.dma_start(br_bc[:], io["b_r"].partition_broadcast(P)).then_inc(weights_in, 16)
            act.dma_start(bqk_col[:], io["b_qkv"][0:2 * D].rearrange("(k p) -> p k", p=P),
                          allow_slow_non_contiguous=True).then_inc(weights_in, 16)

            def root(t, u):
                act.wait_ge(var_ready, 2 * t + u + 1)
                nc.scalar.activation(std[:], var[:], ACT.Sqrt).then_inc(std_ready, 1)

            def evacuate_x(t, u):
                act.wait_ge(xT_done, 2 * t + u + 1)
                nc.scalar.activation(xnT[:, u], pT[:], ACT.Identity).then_inc(xnT_ready, 1)

            def evacuate_qk(t, u):
                tok = u * SEQ + t * GTOK
                for i in range(NQK):
                    act.wait_ge(qk_done, (2 * t + u) * NQK + i + 1)
                    c = i % KC
                    if i < KC:
                        dst = keep["qT"][:, c, ds(tok + 2 * u + 1, GTOK)]
                    else:
                        dst = keep["kT"][:, c, ds(REACH + tok + u, GTOK)]
                    nc.scalar.activation(dst, pQK[:, i % 2], ACT.Identity, bias=bqk_col[:, i:i + 1]).then_inc(qk_free, 1)

            def group(t, u, ahead=None):
                if ahead:
                    root(*ahead)
                evacuate_qk(t, u)
                if ahead:
                    evacuate_x(*ahead)

            root(0, 0)
            evacuate_x(0, 0)
            act.wait_ge(weights_in, 80)
            with act.Fori(0, GROUPS_PER_SEQ - 1) as t:
                group(t, 0, (t, 1))
                group(t, 1, (t + 1, 0))
            end = GROUPS_PER_SEQ - 1
            group(end, 0, (end, 1))
            group(end, 1)

        @block.tensor
        def _(pe):
            pe.wait_ge(ident_set, 1)

            def transposes(t, u):
                n = 2 * t + u
                pe.wait_ge(xn_ready, n + 1)
                pe.wait_ge(xnT_ready, n + 1)
                for a in range(GROUP):
                    for c in range(KC):
                        tr = nc.tensor.transpose(pT[:, c, a * P:(a + 1) * P], xn[:, u, a, c * P:(c + 1) * P],
                                                 keep["ident"][:])
                tr.then_inc(xT_done, 1)

            def group(t, u, ahead=None):
                n = 2 * t + u
                pe.wait_ge(xnT_ready, n + 2)
                for i in range(NQK):
                    pe.wait_ge(qk_free, n * NQK + i + 1)
                    for c in range(KC):
                        mm = nc.tensor.matmul(pQK[:, i % 2], wqkv[:, c, i * P:(i + 1) * P], xnT[:, u, c],
                                              start=(c == 0), stop=(c == KC - 1))
                    mm.then_inc(qk_done, 1)
                if ahead:
                    transposes(*ahead)
                pe.wait_ge(r_free, n + 1)
                for a in range(GROUP):
                    for c in range(KC):
                        mm = nc.tensor.matmul(pR[:, a * EXPERTS:(a + 1) * EXPERTS], xnT[:, u, c, a * P:(a + 1) * P],
                                              wr[:, c], start=(c == 0), stop=(c == KC - 1))
                mm.then_inc(r_done, 1)
                for b in range(NV):
                    pe.wait_ge(v_free, n * NV + b + 1)
                    for a in range(2):
                        tok = slice((2 * b + a) * P, (2 * b + a + 1) * P)
                        for c in range(KC):
                            mm = nc.tensor.matmul(pV[:, b % 2, a], xnT[:, u, c, tok], wqkv[:, c, 2 * D:3 * D],
                                                  start=(c == 0), stop=(c == KC - 1))
                    mm.then_inc(v_done, 1)

            transposes(0, 0)
            pe.wait_ge(weights_in, 80)
            with pe.Fori(0, GROUPS_PER_SEQ - 1) as t:
                group(t, 0, (t, 1))
                group(t, 1, (t + 1, 0))
            end = GROUPS_PER_SEQ - 1
            group(end, 0, (end, 1))
            group(end, 1)

        @block.vector
        def _(dve):
            V = nc.vector
            for u in range(2):
                dve.sem_inc(xn_stored[u], 16)
                dve.sem_inc(v_stored[u], 16 * HG)
            dve.sem_inc(xnT_ready, 1)
            dve.sem_inc(r_free, 1)
            dve.sem_inc(qk_free, 2)
            dve.sem_inc(k_sloped, 1)
            dve.sem_inc(v_free, 2)
            for b in range(BATCH):
                for col in (b * (SEQ + 2), b * (SEQ + 2) + SEQ + 1):
                    V.memset(keep["qT"][:, :, col:col + 1], 0.0)
            for col, n in ((0, REACH), (REACH + SEQ, 1), (REACH + SEQ + 1 + SEQ, REACH)):
                V.memset(keep["kT"][:, :, col:col + n], 0.0)
            CHAIN = 7

            def layernorm(t, u):
                chain = Chain(dve, ln_chain, (2 * t + u) * CHAIN)
                dve.wait_ge(x_loaded[u], 16 * t + 16)
                dve.wait_ge(xn_stored[u], 16 * t + 16)
                for a in range(GROUP):
                    ins = V.bn_stats(stats[:, a], x_in[:, u, a])
                chain(ins)
                dve.sem_inc(go, 1)
                for a in range(GROUP):
                    ins = V.bn_aggr(mv[:, a], stats[:, a])
                chain(ins)
                V.tensor_scalar(var[:], mv[:, :, 1], LN_EPS, None, ALU.add).then_inc(var_ready, 1)
                dve.wait_ge(std_ready, 2 * t + u + 1)
                chain(V.reciprocal(rstd[:], std[:]))
                chain(V.tensor_tensor(std[:], rstd[:], rstd[:], ALU.mult))
                chain(V.tensor_tensor(std[:], std[:], var[:], ALU.mult))
                chain(V.tensor_scalar(std[:], std[:], -0.5, 1.5, ALU.mult, ALU.add))
                chain(V.tensor_tensor(rstd[:], rstd[:], std[:], ALU.mult))
                for a in range(GROUP):
                    ins = V.tensor_scalar(xn[:, u, a], x_in[:, u, a], mv[:, a, 0:1], rstd[:, a:a + 1],
                                          ALU.subtract, ALU.mult)
                ins.then_inc(xn_ready, 1)

            def evacuate(t, u):
                n = 2 * t + u
                dve.wait_ge(r_done, n + 1)
                V.tensor_tensor(
                    keep["scores"][:, ds((u * GROUPS_PER_SEQ + t) * GROUP, GROUP), :],
                    pR[:, 0:GROUP * EXPERTS].rearrange("p (a e) -> p a e", a=GROUP),
                    br_bc[:, None, :].broadcast_to([P, GROUP, EXPERTS]), ALU.add).then_inc(r_free, 1)
                dve.wait_ge(v_stored[u], 16 * HG * t + 16 * HG)
                for b in range(NV):
                    dve.wait_ge(v_done, n * NV + b + 1)
                    V.tensor_tensor(v[:, u, 2 * b:2 * b + 2], pV[:, b % 2], bv_bc[:, None, :].broadcast_to([P, 2, D]),
                                    ALU.add).then_inc(v_free, 1)

            layernorm(0, 0)
            dve.wait_ge(bias_loaded, 32)
            parts = Chain(dve, bias_chain)
            for k in range(NB):
                parts(V.tensor_copy(bias_part[:, k], bias_in[:]))
                if k < NB - 1:
                    parts(V.tensor_tensor(bias_in[:], bias_in[:], bias_part[:, k], ALU.subtract))
            dve.wait_ge(weights_in, 80)
            with dve.Fori(0, GROUPS_PER_SEQ - 1) as t:
                layernorm(t, 1)
                evacuate(t, 0)
                layernorm(t + 1, 0)
                evacuate(t, 1)
            end = GROUPS_PER_SEQ - 1
            layernorm(end, 1)
            evacuate(end, 0)
            evacuate(end, 1)


def route_block(nc, io, dram, keep):
    with ExitStack() as ctx:
        def sb(name, shape, dt=F32):
            return ctx.enter_context(nc.sbuf_tensor(name, shape, dt))

        def ps(name, shape, dt=F32):
            return ctx.enter_context(nc.psum_tensor(name, shape, dt))

        def sem(name):
            return ctx.enter_context(nc.semaphore(name))

        TE = [P, TILES, EXPERTS]
        sel_bias = sb("sel_bias", [P, EXPERTS])
        e_first = sb("e_first", [P, EXPERTS])
        biased = sb("biased", TE)
        top = sb("top", [P, TILES])
        is_top = sb("is_top", TE)
        chosen = [sb(f"chosen{k}", TE) for k in range(TOPK)]
        expw = sb("expw", TE)
        prod = sb("prod", TE)
        picked = sb("picked", [P, TOPK, TILES])
        count = expw
        zero_te = sb("zero_te", [P, TILES])
        upto = biased
        total = sb("total", [P, EXPERTS])
        below = sb("below", [P, P])
        ones = sb("ones", [P, P])
        rows_i = sb("rows_i", [P, EXPERTS], I32)
        rows = sb("rows", [P, EXPERTS])
        ends = sb("ends", [P, EXPERTS])
        start = sb("start", [P, EXPERTS])
        rank = is_top
        slot = sb("slot", [P, TOPK, TILES])
        tile_row = sb("tile_row", [1, SLOT_TILES])
        tile_exp = sb("tile_exp", [1, SLOT_TILES])

        xrow = sb("xrow", [P, XSLOTS, D])
        idx = sb("idx", [P, XSLOTS, TOPK], U32)
        dw_w = sb("dw_w", [P, KC, 3])
        dw_b = sb("dw_b", [P, KC])
        pw_w = sb("pw_w", [P, KC, HR])
        pw_b = sb("pw_b", [P, HR])
        anchor = sb("anchor", [P, HEADS, SAMPLES])
        base_i = sb("base_i", [P, SEQ // P], I32)
        base = sb("base", [P, SEQ // P])
        conv = sb("conv", [P, 2, KC, GTOK])
        off = sb("off", [P, 2, GROUP, HR])
        pos = sb("pos", [P, 2, GROUP, HR])
        head_i = sb("head_i", [P, 1], I32)
        head_f = sb("head_f", [P, 1])
        head_mask = sb("head_mask", [P, GH])
        qm = sb("qm", [P, 2, GH, KC, P])
        kw = sb("kw", [P, KSLOTS, KC, SLOPES])
        Sx = sb("Sx", [P, 2, HG, SLOPES, GH])

        pOff = ps("pOff", [P, GROUP, 256])
        pCount = ps("pCount", [P, 512])
        pS = ps("pSx", [P, 2, 2, 512])

        kw_loaded = [sem(f"kw_loaded{u}") for u in range(KSLOTS)]
        mask_set = sem("mask_set")
        qm_ready = sem("qm_ready")
        s_done = sem("s_done")
        s_free = sem("s_free")
        s_free_last = sem("s_free_last")
        sx_stored = [[sem(f"sx_stored{u}{half}") for half in range(2)] for u in range(2)]
        weights_in = sem("weights_in2")
        consts = sem("consts2")
        totals_ready = sem("totals_ready")
        prefix_ready = sem("prefix_ready")
        exp_in = sem("exp_in")
        exp_out = sem("exp_out")
        slots_ready = sem("slots_ready")
        chain_sem = sem("route_chain")
        xrow_loaded = [sem(f"xrow_loaded{u}") for u in range(XSLOTS)]
        scattered = [sem(f"scattered{u}") for u in range(XSLOTS)]
        idx_set = sem("idx_set")
        go = sem("go")
        conv_done = sem("conv_done")
        gel_ready = sem("gel_ready")
        off_done = sem("off_done")
        off_ready = sem("off_ready")
        tanh_ready = sem("tanh_ready")
        pos_chain = sem("pos_chain")
        conv_chain = sem("conv_chain")
        pos_ready = sem("pos_ready")
        pos_stored = [sem(f"pos_stored{u}") for u in range(2)]

        def scored(hg):
            return pS[:, hg % 2, :, 0:2 * SLOPES].rearrange("p r (h k) -> p r h k", h=2)

        def copied(a, hg):
            return Sx[:, a % 2, hg].rearrange("p k (r h) -> p r h k", r=2)

        block = ctx.enter_context(nc.Block())

        @block.gpsimd
        def _(pool):
            nc.gpsimd.memset(ones[:], 1.0).then_inc(consts, 1)
            pool.wait_ge(consts, 1)
            nc.gpsimd.affine_select(out=below[:], in_=ones[:], compare_op=ALU.is_gt, fill=0.0, base=0,
                                    pattern=[[1, P]], channel_multiplier=-1).then_inc(consts, 1)
            nc.gpsimd.iota(rows_i[:], pattern=[[-1, EXPERTS]], base=EXPERTS, channel_multiplier=0).then_inc(consts, 1)
            nc.gpsimd.iota(base_i[:], pattern=[[P, SEQ // P]], base=0, channel_multiplier=1).then_inc(consts, 1)
            nc.gpsimd.iota(keep["tile_exp"][:], pattern=[[P, SLOT_TILES]], base=0, channel_multiplier=0).then_inc(consts, 1)
            nc.gpsimd.iota(head_i[:], pattern=[[0, 1]], base=0, channel_multiplier=1).then_inc(consts, 1)
            def load_row(n, u):
                pool.dma_start(xrow[:, u], dram["xn"][ds(n * P, P), :]).then_inc(xrow_loaded[u], 16)

            def scatter(t, u):
                n = XSLOTS * t + u
                for k in range(TOPK):
                    nc.gpsimd.tensor_copy(idx[:, u, k:k + 1], keep["slot"][:, k, ds(n, 1)]).then_inc(idx_set, 1)
                pool.wait_ge(idx_set, (n + 1) * TOPK)
                pool.sem_inc(go, 1)
                pool.wait_ge(xrow_loaded[u], 16 * t + 16)
                pool.sem_inc(go, 1)
                for k in range(TOPK):
                    nc.gpsimd.indirect_dma_start(
                        out=dram["xs"], out_offset=bass.IndirectOffsetOnAxis(ap=idx[:, u, k:k + 1], axis=0),
                        in_=xrow[:, u], in_offset=None).then_inc(scattered[u], 16)

            for u in range(XSLOTS):
                load_row(u, u)
            pool.wait_ge(slots_ready, 1)
            for u in range(XSLOTS):
                scatter(0, u)
            with pool.Fori(1, TILES // XSLOTS) as t:
                for u in range(XSLOTS):
                    pool.wait_ge(scattered[u], 16 * TOPK * t)
                    load_row(XSLOTS * t + u, u)
                for u in range(XSLOTS):
                    scatter(t, u)
            for u in range(XSLOTS):
                pool.wait_ge(scattered[u], 16 * TOPK * (TILES // XSLOTS))

        @block.sync
        def _(sp):
            sp.dma_start(sel_bias[:], io["sel_bias"].partition_broadcast(P)).then_inc(weights_in, 16)
            sp.dma_start(dw_w[:], io["dw_w"].rearrange("(k p) n -> p k n", p=P)).then_inc(weights_in, 16)
            sp.dma_start(dw_b[:], io["dw_b"].rearrange("(k p) -> p k", p=P),
                         allow_slow_non_contiguous=True).then_inc(weights_in, 16)
            sp.dma_start(pw_w[:], io["pw_wT"].rearrange("(k p) n -> p k n", p=P)).then_inc(weights_in, 16)
            sp.dma_start(pw_b[:], io["pw_b"].partition_broadcast(P)).then_inc(weights_in, 16)


            def load_keys(t, u, a):
                sp.dma_start(kw[:, a % KSLOTS], keep["kT"][:, :, ds(u * (SEQ + 1) + t * GTOK + a * P, SLOPES)]).then_inc(
                    kw_loaded[a % KSLOTS], 16)

            def store_half(tok, u, half):
                pair = slice(2 * half, 2 * half + 2)
                for g in range(0, P, SROWS):
                    sp.dma_start(
                        bass.AP(dram["S"].tensor, (tok + g) * S_PITCH + 2 * half * TOKENS * S_PITCH,
                                [[S_ROW, SROWS], [TOKENS * S_PITCH, 2], [1, S_ROW]]),
                        Sx[g:g + SROWS, u, pair, g:g + SROWS + 2 * REACH - 1, :].rearrange("p g k h -> p g (k h)")
                    ).then_inc(sx_stored[u][half], 16)

            def store_s(t, u, after=None, pos_of=None):
                for a in range(GROUP):
                    n = (2 * t + u) * GROUP + a
                    tok = u * SEQ + t * GTOK + a * P
                    sp.wait_ge(s_free, n * (HG - 1) + 3)
                    store_half(tok, a % 2, 0)
                    sp.wait_ge(s_free_last, n + 2)
                    if a + KSLOTS < GROUP:
                        load_keys(t, u, a + KSLOTS)
                    elif after:
                        load_keys(*after, a + KSLOTS - GROUP)
                    sp.wait_ge(s_free, n * (HG - 1) + 4)
                    store_half(tok, a % 2, 1)
                    if pos_of and a == 2 * u:
                        store_pos(*pos_of)

            def store_pos(t, u):
                sp.wait_ge(pos_ready, 2 * t + u + 1)
                sp.dma_start(dram["pos"][ds(u * SEQ + t * GTOK, GTOK), :].rearrange("(a p) c -> p a c", p=P),
                             pos[:, u]).then_inc(pos_stored[u], 16)

            for a in range(KSLOTS):
                load_keys(0, 0, a)
            store_s(0, 0, (0, 1))
            store_s(0, 1, (1, 0))
            store_s(1, 0, (1, 1))
            store_s(1, 1, (2, 0), (0, 0))
            with sp.Fori(2, GROUPS_PER_SEQ - 1) as t:
                store_s(t, 0, (t, 1), (t - 2, 1))
                store_s(t, 1, (t + 1, 0), (t - 1, 0))
            end = GROUPS_PER_SEQ - 1
            store_s(end, 0, (end, 1), (end - 2, 1))
            store_s(end, 1, None, (end - 1, 0))
            store_pos(end - 1, 1)
            store_pos(end, 0)
            store_pos(end, 1)
            for u in range(2):
                sp.wait_ge(pos_stored[u], 16 * (GROUPS_PER_SEQ + 1))
                for half in range(2):
                    sp.wait_ge(sx_stored[u][half], 16 * (P // SROWS) * (TILES // 2 + 1))

        @block.scalar
        def _(act):
            act.wait_ge(mask_set, 1)

            def mask_q(t, u, a, h):
                col = u * (SEQ + 2) + 1 + t * GTOK + a * P
                nc.scalar.activation(qm[:, a % 2, h], keep["qT"][:, :, ds(col, P)], ACT.Identity,
                                     scale=head_mask[:, h:h + 1]).then_inc(qm_ready, 1)

            def copy_s(t, u, a, after=None, first=False):
                n = (2 * t + u) * GROUP + a
                pair = (2 * t + u) * (GROUP // 2) + a // 2
                stores = 16 * (P // SROWS)
                if not first:
                    act.wait_ge(s_done, n * HG)
                masks = iter(range(GH if after else 0))
                for hg in range(HG - 1):
                    for h in masks:
                        mask_q(*after, h)
                        if h > 0:
                            break
                    if hg != 1:
                        act.wait_ge(sx_stored[a % 2][hg // 2], stores * pair + stores)
                    act.wait_ge(s_done, n * HG + hg + 1)
                    nc.scalar.activation(copied(a, hg), scored(hg), ACT.Identity).then_inc(s_free, 1)

            def tanh(t, u):
                act.wait_ge(off_ready, 2 * t + u + 2)
                nc.scalar.activation(off[:, u], off[:, u], ACT.Tanh).then_inc(tanh_ready, 1)

            def gelu(t, u):
                act.wait_ge(conv_done, 2 * t + u + 1)
                nc.scalar.activation(conv[:, u], conv[:, u], ACT.Gelu).then_inc(gel_ready, 1)

            def first_half(t, first=False):
                for a in range(GROUP):
                    copy_s(t, 0, a, (t, 0, a + 1) if a + 1 < GROUP else (t, 1, 0), first=first and a == 0)
                    if first and a == 1:
                        gelu(t, 0)

            def second_half(t, first=False, last=False):
                copy_s(t, 1, 0, (t, 1, 1))
                if not first:
                    gelu(t, 0)
                copy_s(t, 1, 1, (t, 1, 2))
                copy_s(t, 1, 2, (t, 1, 3))
                gelu(t, 1)
                copy_s(t, 1, 3, None if last else (t + 1, 0, 0))
                tanh(t, 0)

            for h in range(GH):
                mask_q(0, 0, 0, h)
            first_half(0, first=True)
            act.wait_ge(exp_in, 1)
            nc.scalar.activation(expw[:], prod[:], ACT.Exp).then_inc(exp_out, 1)
            second_half(0, first=True)
            with act.Fori(1, GROUPS_PER_SEQ - 1) as t:
                first_half(t)
                tanh(t - 1, 1)
                second_half(t)
            end = GROUPS_PER_SEQ - 1
            first_half(end)
            tanh(end - 1, 1)
            second_half(end, last=True)
            tanh(end, 1)

        @block.tensor
        def _(pe):
            def head_scores(t, u, a):
                n = (2 * t + u) * GROUP + a
                pe.wait_ge(qm_ready, (n + 1) * GH)
                pe.wait_ge(kw_loaded[a % KSLOTS], 16 * ((2 * t + u) * (GROUP // KSLOTS) + a // KSLOTS + 1))
                for hg in range(HG):
                    if hg == 1:
                        pe.wait_ge(s_free_last, n + 1)
                    else:
                        pe.wait_ge(s_free, n * (HG - 1) + max(hg, 1))
                    for h in range(GH):
                        c = hg // 2
                        rows = slice(hg % 2 * GD, (hg % 2 + 1) * GD)
                        mm = nc.tensor.matmul(pS[:, hg % 2, h // 2, h % 2 * SLOPES:(h % 2 + 1) * SLOPES],
                                              qm[rows, a % 2, h, c, :], kw[rows, a % KSLOTS, c, :],
                                              start=True, stop=True)
                    mm.then_inc(s_done, 1)

            def offsets(t, u):
                n = 2 * t + u
                pe.wait_ge(gel_ready, n + 1)
                pe.wait_ge(off_ready, n + 1)
                for a in range(GROUP):
                    for c in range(KC):
                        mm = nc.tensor.matmul(pOff[:, a, 0:HR], conv[:, u, c, a * P:(a + 1) * P], pw_w[:, c],
                                              start=(c == 0), stop=(c == KC - 1))
                mm.then_inc(off_done, 1)

            def group(t, u, before=None):
                head_scores(t, u, 0)
                head_scores(t, u, 1)
                if before:
                    offsets(*before)
                head_scores(t, u, 2)
                head_scores(t, u, 3)

            group(0, 0)
            pe.wait_ge(weights_in, 80)
            offsets(0, 0)
            group(0, 1)
            pe.wait_ge(totals_ready, 1)
            pe.wait_ge(consts, 2)
            nc.tensor.matmul(pCount[:, 0:EXPERTS], below[:], total[:], start=True, stop=True)
            nc.tensor.matmul(pCount[:, EXPERTS:2 * EXPERTS], ones[:], total[:], start=True,
                             stop=True).then_inc(prefix_ready, 1)
            with pe.Fori(1, GROUPS_PER_SEQ) as t:
                group(t, 0, (t - 1, 1))
                group(t, 1, (t, 0))
            offsets(GROUPS_PER_SEQ - 1, 1)

        @block.vector
        def _(dve):
            V = nc.vector

            def per_expert(ap):
                return ap.unsqueeze(2).broadcast_to(TE)

            def per_tile(ap):
                return ap[:, None, :].broadcast_to(TE)

            def copy_last(t, u, a):
                n = (2 * t + u) * GROUP + a
                pair = (2 * t + u) * (GROUP // 2) + a // 2
                stores = 16 * (P // SROWS)
                dve.wait_ge(sx_stored[a % 2][1], stores * pair + stores)
                dve.wait_ge(s_done, (n + 1) * HG)
                V.tensor_copy(copied(a, HG - 1), scored(HG - 1)).then_inc(s_free_last, 1)

            def convolve(t, u, c):
                col = u * (SEQ + 2) + 1 + t * GTOK
                cc = Chain(dve, conv_chain, ((2 * t + u) * KC + c) * 2)
                cc(V.tensor_scalar(conv[:, u, c], keep["qT"][:, c, ds(col, GTOK)], dw_w[:, c, 1:2], dw_b[:, c:c + 1],
                                   ALU.mult, ALU.add))
                cc(V.scalar_tensor_tensor(conv[:, u, c], keep["qT"][:, c, ds(col - 1, GTOK)], dw_w[:, c, 0:1],
                                          conv[:, u, c], ALU.mult, ALU.add))
                ins = V.scalar_tensor_tensor(conv[:, u, c], keep["qT"][:, c, ds(col + 1, GTOK)], dw_w[:, c, 2:3],
                                             conv[:, u, c], ALU.mult, ALU.add)
                if c == KC - 1:
                    ins.then_inc(conv_done, 1)

            def offset_bias(t, u):
                dve.wait_ge(off_done, 2 * t + u + 1)
                V.tensor_tensor(off[:, u], pOff[:, :, 0:HR], pw_b[:, None, :].broadcast_to([P, GROUP, HR]),
                                ALU.add).then_inc(off_ready, 1)

            POS_CHAIN = 3

            def sample(t, u):
                n = 2 * t + u
                pc = Chain(dve, pos_chain, n * POS_CHAIN)
                dve.wait_ge(tanh_ready, n + 1)
                dve.wait_ge(pos_stored[u], 16 * t + 16)
                pc(V.tensor_scalar(off[:, u], off[:, u], MAX_OFFSET, None, ALU.mult))
                for a in range(GROUP):
                    ins = V.scalar_tensor_tensor(pos[:, u, a], anchor[:].rearrange("p h r -> p (h r)"),
                                                 base[:, ds(t * GROUP + a, 1)], off[:, u, a], ALU.add, ALU.add)
                pc(ins)

            def relate(t, u):
                n = 2 * t + u
                pc = Chain(dve, pos_chain, n * POS_CHAIN + 2)
                pc(V.tensor_scalar(pos[:, u], pos[:, u], 0.0, float(SEQ - 1), ALU.max, ALU.min))
                for a in range(GROUP):
                    ins = V.tensor_scalar(pos[:, u, a], pos[:, u, a], base[:, ds(t * GROUP + a, 1)], None, ALU.subtract)
                ins.then_inc(pos_ready, 1)

            chain = Chain(dve, chain_sem)
            scores = keep["scores"]
            for u in range(2):
                dve.sem_inc(pos_stored[u], 16)
                for half in range(2):
                    dve.sem_inc(sx_stored[u][half], 16 * (P // SROWS))
            dve.sem_inc(s_free, 1)
            dve.sem_inc(s_free_last, 1)
            dve.sem_inc(off_ready, 1)
            for r, a in enumerate(anchors()):
                V.memset(anchor[:, :, r:r + 1], a)
            V.memset(zero_te[:], 0.0)
            dve.wait_ge(consts, 6)
            chain(V.tensor_scalar(head_i[:], head_i[:], DH.bit_length() - 1, GH - 1, ALU.logical_shift_right, ALU.bitwise_and))
            chain(V.tensor_copy(head_f[:], head_i[:]))
            for h in range(GH):
                ins = V.tensor_scalar(head_mask[:, h:h + 1], head_f[:], float(h), None, ALU.is_equal)
            ins.then_inc(mask_set, 1)
            V.tensor_copy(e_first[:], rows_i[:])
            V.tensor_copy(tile_row[:], keep["tile_exp"][:])
            chain(V.tensor_copy(base[:], base_i[:]))
            dve.wait_ge(weights_in, 80)
            convolve(0, 0, 0)
            convolve(0, 0, 1)
            copy_last(0, 0, 0)
            copy_last(0, 0, 1)
            chain(V.tensor_reduce(top[:], scores[:], AX.X, ALU.max))
            V.tensor_tensor(prod[:], scores[:], per_expert(top[:]), ALU.subtract).then_inc(exp_in, 1)
            chain(V.tensor_tensor(biased[:], scores[:], per_tile(sel_bias[:]), ALU.add))
            for k in range(TOPK):
                chain(V.tensor_reduce(top[:], biased[:], AX.X, ALU.max))
                chain(V.tensor_tensor(is_top[:], biased[:], per_expert(top[:]), ALU.is_equal))
                chain(V.tensor_tensor(is_top[:], is_top[:], per_tile(e_first[:]), ALU.mult))
                copy_last(0, k, 2 - 2 * k)
                chain(V.tensor_reduce(top[:], is_top[:], AX.X, ALU.max))
                chain(V.tensor_tensor(chosen[k][:], per_tile(e_first[:]), per_expert(top[:]), ALU.is_equal))
                if k == 0:
                    chain(V.scalar_tensor_tensor(biased[:].rearrange("p t e -> p (t e)"),
                                                 chosen[0][:].rearrange("p t e -> p (t e)"), -3.0e38,
                                                 biased[:].rearrange("p t e -> p (t e)"), ALU.mult, ALU.add))
                copy_last(0, k, 3 - 2 * k)
            offset_bias(0, 0)
            dve.wait_ge(exp_out, 1)
            for k in range(TOPK):
                chain(V.tensor_tensor(prod[:], expw[:], chosen[k][:], ALU.mult))
                chain(V.tensor_reduce(picked[:, k], prod[:], AX.X, ALU.add))
            chain(V.tensor_tensor(top[:], picked[:, 0], picked[:, 1], ALU.add))
            chain(V.reciprocal(top[:], top[:]))
            for k in range(TOPK):
                V.tensor_tensor(keep["gate"][:, k], picked[:, k], top[:], ALU.mult)
            convolve(0, 1, 0)
            convolve(0, 1, 1)
            copy_last(0, 1, 2)
            chain(V.tensor_tensor(count[:], chosen[0][:], chosen[1][:], ALU.add))
            for e in range(EXPERTS):
                ins = V.tensor_tensor_scan(upto[:, :, e], count[:, :, e], zero_te[:], 0.0, ALU.add, ALU.add)
            chain(ins)
            V.tensor_copy(total[:], upto[:, TILES - 1, :]).then_inc(totals_ready, 1)
            copy_last(0, 1, 3)
            chain(V.tensor_tensor(rank[:], upto[:], count[:], ALU.subtract))
            dve.wait_ge(prefix_ready, 1)
            chain(V.tensor_scalar(rows_i[:], pCount[:, EXPERTS:2 * EXPERTS], float(P - 1), None, ALU.add))
            shift = P.bit_length() - 1
            chain(V.tensor_scalar(rows_i[:], rows_i[:], shift, shift, ALU.logical_shift_right, ALU.logical_shift_left))
            chain(V.tensor_copy(rows[:], rows_i[:]))
            chain(V.tensor_tensor_scan(ends[:], rows[:], zero_te[:, 0:EXPERTS], 0.0, ALU.add, ALU.add))
            chain(V.tensor_tensor(start[:], ends[:], rows[:], ALU.subtract))
            chain(V.tensor_tensor(start[:], start[:], pCount[:, 0:EXPERTS], ALU.add))
            chain(V.tensor_tensor(rank[:], rank[:], per_tile(start[:]), ALU.add))
            for k in range(TOPK):
                chain(V.tensor_tensor(prod[:], rank[:], chosen[k][:], ALU.mult))
                chain(V.tensor_reduce(slot[:, k], prod[:], AX.X, ALU.add))
            V.tensor_copy(keep["slot"][:], slot[:]).then_inc(slots_ready, 1)
            chain(V.tensor_scalar(tile_exp[:], tile_row[:], ends[0:1, 0:1], None, ALU.is_ge))
            for e in range(1, EXPERTS - 1):
                chain(V.scalar_tensor_tensor(tile_exp[:], tile_row[:], ends[0:1, e:e + 1], tile_exp[:],
                                             ALU.is_ge, ALU.add))
            V.tensor_copy(keep["tile_exp"][:], tile_exp[:])

            with dve.Fori(1, GROUPS_PER_SEQ) as t:
                copy_last(t, 0, 0)
                convolve(t, 0, 0)
                copy_last(t, 0, 1)
                convolve(t, 0, 1)
                copy_last(t, 0, 2)
                offset_bias(t - 1, 1)
                sample(t - 1, 0)
                copy_last(t, 0, 3)
                convolve(t, 1, 0)
                copy_last(t, 1, 0)
                convolve(t, 1, 1)
                copy_last(t, 1, 1)
                relate(t - 1, 0)
                copy_last(t, 1, 2)
                offset_bias(t, 0)
                sample(t - 1, 1)
                copy_last(t, 1, 3)
                relate(t - 1, 1)
            end = GROUPS_PER_SEQ - 1
            sample(end, 0)
            relate(end, 0)
            offset_bias(end, 1)
            sample(end, 1)
            relate(end, 1)


def mix_block(nc, io, dram, keep):
    with ExitStack() as ctx:
        def sb(name, shape, dt=F32):
            return ctx.enter_context(nc.sbuf_tensor(name, shape, dt))

        def ps(name, shape, dt=F32):
            return ctx.enter_context(nc.psum_tensor(name, shape, dt))

        def sem(name):
            return ctx.enter_context(nc.semaphore(name))

        w1 = sb("w1", [P, KC, EXPERTS * 2 * HID])
        w2 = sb("w2", [P, HC, EXPERTS * D])
        b1 = sb("b1", [NB, 2, 2 * HID], BF16)
        b2 = sb("b2", [NB, 2, D], BF16)
        ones3 = sb("ones3", [NB, P], BF16)
        xs = sb("xs", [P, 2, D])
        xsT = sb("xsT", [P, KC, P])
        act_a = sb("act_a", [P, 2, HID])
        hid = sb("hid", [P, 2, HID])
        hidT = sb("hidT", [P, 2, HC, P])
        ys = sb("ys", [P, 2, D])
        slope = sb("slope", [P, IB, KNOTS, GH])
        bend = sb("bend", [P, KNOTS, TH])
        pos_in = sb("pos_in", [P, PAIRS])
        pos = sb("posw", [P, 2, PAIRS])
        prob = sb("prob", [P, 2, PAIRS])
        terms = sb("terms", [P, 2, PAIRS])
        gterms = sb("gterms", [P, GSUM, PAIRS])
        smax = sb("smax", [P, TH])
        psum_e = sb("psum_e", [P, TH])
        gslope = sb("gslope", [P, KNOTS + 2, TH])
        G = gslope[:, 1:KNOTS + 1]
        wgt = sb("wgt", [P, NJ, TH])
        vw = sb("vw", [P, 2, WIN * GD])
        oprod = sb("oprod", [P, 2, TH * DH])
        own = sb("own", [P, TH * DH])
        outs = sb("outs", [P, 2, TH * DH])
        rel = sb("rel", [P, 1])
        rel_neg = sb("rel_neg", [P, 1])

        pX = ps("pX", [P, 512])
        pA = ps("pA", [P, 2, 512])
        pB = ps("pB", [P, 2, 512])
        pH = ps("pH", [P, 512])
        pY = ps("pY", [P, 512])

        w1_loaded = sem("w1_loaded")
        w2_loaded = sem("w2_loaded")
        ones_set = sem("ones_set")
        rel_in = sem("rel_in")
        rel_set = sem("rel_set")
        b1_loaded = [sem(f"b1_loaded{u}") for u in range(2)]
        b2_loaded = [sem(f"b2_loaded{u}") for u in range(2)]
        xs_loaded = [sem(f"xs_loaded{u}") for u in range(2)]
        xsT_done = sem("xsT_done")
        xsT_ready = sem("xsT_ready")
        h_done = sem("h_done")
        a_ready = sem("a_ready")
        hid_ready = sem("hid_ready")
        hidT_done = sem("hidT_done")
        hidT_ready = sem("hidT_ready")
        y_done = sem("y_done")
        ys_ready = sem("ys_ready")
        ys_stored = [sem(f"ys_stored{u}") for u in range(2)]

        s_loaded = sem("s_loaded")
        s_used = sem("s_used")
        pos_loaded = sem("pos_loaded")
        dist_set = sem("dist_set")
        dist_ready = sem("dist_ready")
        pos_set = sem("pos_set")
        step_free = sem("step_free")
        term_ready = sem("term_ready")
        term_free = sem("term_free")
        shift_ready = sem("shift_ready")
        prob_ready = sem("prob_ready")
        v_loaded = [sem(f"v_loaded{u}") for u in range(2)]
        oprod_ready = sem("oprod_ready")
        oprod_free = sem("oprod_free")
        own_done = sem("own_done")
        outs_stored = [sem(f"outs_stored{u}") for u in range(2)]
        chain_sem = sem("attn_chain")
        first_chain = sem("first_chain")
        last_chain = sem("last_chain")
        last_sum = sem("last_sum")
        block = ctx.enter_context(nc.Block())

        LAST = STEPS - 1
        CHAIN = 4 + 2 * (KNOTS // GSUM) + 2
        SHARED = 9
        FIRST_SUMS = 7
        OWN = 2
        OWN_STEPS = 3
        NV = NJ - OWN

        def tiles_before(it):
            return FIRST_TILES + (it - 1) * MOE_PER_STEP

        def run_steps(step):
            return (lambda: step(0, 0, 0, first=True),
                    lambda n: (step(2 * n + 1, 1, n), step(2 * n + 2, 0, n + 1)),
                    lambda: step(LAST, 1, LAST // 2, last=True))

        @block.sync
        def _(sp):
            def load_xs(n, u):
                sp.dma_start(xs[:, u], dram["xs"][ds(n * P, P), :]).then_inc(xs_loaded[u], 16)

            def load_bias(n, u, dst, cols, loaded):
                e = sp.value_load(keep["tile_exp"][0:1, ds(n, 1)], min_val=0, max_val=EXPERTS - 1)
                sp.dma_start(dst[:, u, :], dram["bias"][:, ds(e, 1), cols].rearrange("k o n -> k (o n)")).then_inc(
                    loaded[u], 16)

            def load_b1(n, u):
                load_bias(n, u, b1, slice(0, 2 * HID), b1_loaded)

            def load_b2(n, u):
                load_bias(n, u, b2, slice(2 * HID, 2 * HID + D), b2_loaded)

            def tile_io(n, m, left=2, early=False):
                u = m % 2
                if left >= 1 and not (early and n == 0):
                    sp.wait_ge(h_done, n)
                if left >= 1:
                    load_b1(n + 1, 1 - u)
                if left >= 2:
                    sp.wait_ge(xsT_done, n + 1)
                    load_xs(n + 2, u)
                if not early:
                    sp.wait_ge(ys_ready, n - 1)
                    store_y(n - 2, u)
                load_b2(n, u)

            def store_y(n, u):
                sp.dma_start(dram["ys"][ds(n * P, P), :], ys[:, u]).then_inc(ys_stored[u], 16)

            def load_s(hg, ib):
                sp.dma_start(slope[:].rearrange("p i j h -> p i (j h)"),
                             bass.AP(dram["S"].tensor, (hg * TOKENS + ib * IB) * S_PITCH,
                                     [[RUN * S_PITCH, P], [S_PITCH, IB], [1, KNOTS * GH]])).then_inc(s_loaded, 16)

            def load_pos(hg, ib):
                sp.dma_start(pos_in[:].rearrange("p (i c) -> p i c", i=IB),
                             bass.AP(dram["pos"].tensor, ib * IB * HR + hg * GR,
                                     [[RUN * HR, P], [HR, IB], [1, GR]])).then_inc(pos_loaded, 16)

            def load_v(hg, ib):
                sp.dma_start(vw[:, hg % 2].rearrange("p (i c) -> p i c", i=WIN),
                             bass.AP(dram["v"].tensor, (hg * (TOKENS + 2 * REACH) + ib * IB) * GD,
                                     [[RUN * GD, P], [GD, WIN], [1, GD]])).then_inc(v_loaded[hg % 2], 16)

            def store_outs(hg, ib):
                sp.dma_start(bass.AP(dram["attn"].tensor, ib * IB * D + hg * GD, [[RUN * D, P], [D, IB], [1, GD]]),
                             outs[:, hg % 2].rearrange("p (i c) -> p i c", i=IB)).then_inc(outs_stored[hg % 2], 16)

            def place(ib, hg, shift):
                return (hg + shift) % HG, ib + (hg + shift) // HG

            def step(ib, hg, early=False, late=False):
                it = ib * HG + hg
                n, u = tiles_before(it), (hg * MOE_PER_STEP + FIRST_TILES - MOE_PER_STEP) % 2
                tiles = MOE_PER_STEP
                if early and hg == 0:
                    n, u, tiles = 0, 0, FIRST_TILES
                if late and hg == HG - 1:
                    tiles = SLOT_TILES - tiles_before(STEPS - 1)

                def tiles_io(some):
                    for m in some:
                        if m < tiles:
                            tile_io(n + m, u + m, left=tiles - 1 - m if late and hg == HG - 1 else 2,
                                    early=early and hg == 0 and m < 2)

                tiles_io(range(2))
                if not late:
                    sp.wait_ge(pos_set, it + 2)
                    load_pos(*place(ib, hg, 2))
                if not early:
                    sp.wait_ge(oprod_free, (it - 1) * NV + 2)
                    load_v(hg, ib)
                tiles_io(range(2, 4))
                if not late:
                    sp.wait_ge(s_used, it + 2)
                    load_s(*place(ib, hg, 2))
                if not early:
                    sp.wait_ge(oprod_free, (it - 1) * NV + 2)
                    store_outs(*place(ib, hg, -2))
                tiles_io(range(4, MOE_PER_STEP))

            sp.dma_start(rel[:], io["rel_scale"].partition_broadcast(P)).then_inc(rel_in, 16)
            load_pos(0, 0)
            load_s(0, 0)
            load_xs(0, 0)
            load_xs(1, 1)
            load_b1(0, 0)
            load_v(0, 0)
            load_v(1, 0)
            sp.wait_ge(pos_set, 1)
            load_pos(1, 0)
            sp.wait_ge(s_used, 1)
            load_s(1, 0)
            for hg in range(HG):
                step(0, hg, early=hg < 2)
            with sp.Fori(1, NIB - 1) as ib:
                for hg in range(HG):
                    step(ib, hg)
            for hg in range(HG):
                step(NIB - 1, hg, late=hg >= HG - 2)
            for u in range(2):
                sp.wait_ge(ys_ready, SLOT_TILES - 1 + u)
                store_y(SLOT_TILES - 2 + u, u)
            sp.wait_ge(oprod_free, LAST * NV + 2)
            store_outs(HG - 2, NIB - 1)
            sp.wait_ge(last_sum, 1)
            store_outs(HG - 1, NIB - 1)
            for u in range(2):
                sp.wait_ge(outs_stored[u], 16 * (STEPS // 2 + 1))
                sp.wait_ge(ys_stored[u], 16 * (SLOT_TILES // 2 + 1))

        @block.gpsimd
        def _(pool):
            def add_term(it, u, j, first=False):
                if j == (FIRST_SUMS if first else 0):
                    pool.wait_ge(dist_ready, it + 1)
                else:
                    pool.wait_ge(term_free, it * KNOTS + j + 2)
                pool.wait_ge(term_ready, it * KNOTS + j + 1)
                nc.gpsimd.tensor_tensor(prob[:, u], prob[:, u], terms[:, j % 2], ALU.add).then_inc(term_free, 1)

            def weigh_own(it, u, half, written):
                pool.wait_ge(v_loaded[u], 16 * half + 16)
                pool.wait_ge(outs_stored[u], 16 * half + 16)
                pool.wait_ge(chain_sem, written)
                for j in range(OWN):
                    dst = outs[:, u] if j == 0 else own[:]
                    if j > 1:
                        pool.wait_ge(own_done, it * OWN_STEPS + 2 * j - 1)
                    nc.gpsimd.tensor_tensor(dst.rearrange("p (t d) -> p t d", d=DH),
                                            vw[:, u, j * GD:j * GD + IB * GD].rearrange("p (t d) -> p t d", d=DH),
                                            wgt[:, j].unsqueeze(2).broadcast_to([P, TH, DH]), ALU.mult).then_inc(own_done, 1)
                    if j > 0:
                        pool.wait_ge(own_done, it * OWN_STEPS + 2 * j)
                        nc.gpsimd.tensor_tensor(outs[:, u], outs[:, u], own[:], ALU.add).then_inc(own_done, 1)

            def add_value(it, u, j):
                i = j - OWN
                if i == 0:
                    pool.wait_ge(own_done, (it + 1) * OWN_STEPS)
                else:
                    pool.wait_ge(oprod_free, it * NV + i + 2)
                pool.wait_ge(oprod_ready, it * NV + i + 1)
                nc.gpsimd.tensor_tensor(outs[:, u], outs[:, u], oprod[:, (u * NV + i) % 2], ALU.add).then_inc(oprod_free, 1)

            def step(it, u, half, first=False, last=False):
                if not first:
                    weigh_own(it - 1, 1 - u, half - 1 if u == 0 else half, it * CHAIN)
                for j in range(NJ):
                    if not last and j < KNOTS:
                        add_term(it + 1, 1 - u, j)
                    if not first and j >= OWN:
                        add_value(it - 1, 1 - u, j)

            for j in range(FIRST_SUMS, KNOTS):
                add_term(0, 0, j, first=True)
            first_step, two_steps, last_step = run_steps(step)
            first_step()
            with pool.Fori(0, STEPS // 2 - 1) as n:
                two_steps(n)
            last_step()
            weigh_own(LAST, 1, LAST // 2, STEPS * CHAIN)
            for j in range(OWN, SHARED):
                add_value(LAST, 1, j)

        @block.scalar
        def _(act):
            def evacuate_x(n):
                act.wait_ge(xsT_done, n + 1)
                nc.scalar.activation(xsT[:].rearrange("p k t -> p (k t)"), pX[:, 0:D], ACT.Identity).then_inc(xsT_ready, 1)

            def evacuate_y(n, u, pair):
                act.wait_ge(y_done, n + 1)
                act.wait_ge(ys_stored[u], 16 * pair + 16)
                nc.scalar.activation(ys[:, u], pY[:, 0:D], ACT.Identity).then_inc(ys_ready, 1)

            def evacuate_hid(n, u):
                act.wait_ge(hidT_done, n + 1)
                nc.scalar.activation(hidT[:, u].rearrange("p k t -> p (k t)"), pH[:], ACT.Identity).then_inc(hidT_ready, 1)

            def tile_slot(n, m, pair, done=SLOT_TILES):
                u = m % 2
                act.wait_ge(h_done, n + 1)
                nc.scalar.activation(act_a[:, u], pA[:, u], ACT.Silu).then_inc(a_ready, 1)
                if done >= 2:
                    evacuate_y(n - 2, u, pair - 1)
                if done >= 1:
                    evacuate_hid(n - 1, 1 - u)

            def prepare(it, u, early=False):
                act.wait_ge(pos_loaded, 16 * it + 16)
                if not early:
                    act.wait_ge(step_free, it - 1)
                nc.scalar.activation(prob[:, u], pos_in[:], ACT.Abs).then_inc(dist_set, 1)
                act.wait_ge(dist_set, it + 1)
                nc.scalar.activation(prob[:, u], prob[:, u], ACT.Identity, scale=rel_neg[:, 0:1]).then_inc(dist_ready, 1)
                nc.scalar.activation(pos[:, u], pos_in[:], ACT.Identity).then_inc(pos_set, 1)

            def step(it, u, pairs=0, first=False, last=False):
                act.wait_ge(shift_ready, it + 1)
                nc.scalar.activation(prob[:, u], prob[:, u], ACT.Exp, scale=SCALE).then_inc(prob_ready, 1)
                if first:
                    for n in range(FIRST_TILES):
                        tile_slot(n, n, n // 2, done=n)
                        evacuate_x(n + 1)
                    return
                n = tiles_before(it)
                shift = MOE_PER_STEP if u == 0 else 0
                for m in range(SLOT_TILES - n if last else MOE_PER_STEP):
                    tile_slot(n + m, shift + m, pairs + (shift + m) // 2)
                    if not last or n + m < SLOT_TILES - 1:
                        evacuate_x(n + m + 1)

            act.wait_ge(rel_set, 1)
            prepare(0, 0, early=True)
            act.wait_ge(s_loaded, 32)
            for k in range(KC):
                act.dma_start(w1[:, k].rearrange("p (e n) -> p e n", e=EXPERTS),
                              io["w_l1"].rearrange("e (k p) n -> k p e n", p=P)[k]).then_inc(w1_loaded, 16)
            for k in range(HC):
                act.dma_start(w2[:, k].rearrange("p (e n) -> p e n", e=EXPERTS),
                              io["w_l2"].rearrange("e (k p) n -> k p e n", p=P)[k]).then_inc(w2_loaded, 16)
            prepare(1, 1, early=True)
            evacuate_x(0)
            def two_steps(n, last=False):
                pairs = FIRST_TILES // 2 + n * MOE_PER_STEP
                step(2 * n + 1, 1, pairs)
                prepare(2 * n + 3, 1)
                step(2 * n + 2, 0, pairs)
                if not last:
                    prepare(2 * n + 4, 0)

            step(0, 0, first=True)
            prepare(2, 0)
            with act.Fori(0, STEPS // 2 - 2) as n:
                two_steps(n)
            two_steps(STEPS // 2 - 2, last=True)
            step(LAST, 1, tiles_before(LAST) // 2, last=True)
            evacuate_y(SLOT_TILES - 2, 0, SLOT_TILES // 2 - 1)
            evacuate_hid(SLOT_TILES - 1, 1)
            evacuate_y(SLOT_TILES - 1, 1, SLOT_TILES // 2 - 1)

        @block.tensor
        def _(pe):
            eye = keep["ident"]

            def expert(n):
                return pe.value_load(keep["tile_exp"][0:1, ds(n, 1)], min_val=0, max_val=EXPERTS - 1)

            def transpose_x(n, u, pair):
                pe.wait_ge(xs_loaded[u], 16 * pair + 16)
                for k in range(KC):
                    tr = nc.tensor.transpose(pX[:, k * P:(k + 1) * P], xs[:, u, k * P:(k + 1) * P], eye[:])
                tr.then_inc(xsT_done, 1)

            def times_w1(n, u, pair):
                e = expert(n)
                pe.wait_ge(b1_loaded[u], 16 * pair + 16)
                pe.wait_ge(xsT_ready, n + 1)
                for o, dst in ((0, pA), (1, pB)):
                    for k in range(KC):
                        nc.tensor.matmul(dst[:, u], xsT[:, k], w1[:, k, ds(e * 2 * HID + o * HID, HID)],
                                         start=(k == 0), stop=False)
                    mm = nc.tensor.matmul(dst[:, u], ones3[:], b1[:, u, o * HID:(o + 1) * HID], start=False, stop=True)
                mm.then_inc(h_done, 1)

            def times_w2(n, u, pair):
                e = expert(n)
                pe.wait_ge(b2_loaded[u], 16 * pair + 16)
                pe.wait_ge(hidT_ready, n + 1)
                for k in range(HC):
                    nc.tensor.matmul(pY[:, 0:D], hidT[:, u, k], w2[:, k, ds(e * D, D)], start=(k == 0), stop=False)
                nc.tensor.matmul(pY[:, 0:D], ones3[:], b2[:, u], start=False, stop=True).then_inc(y_done, 1)

            def transpose_hid(n, u):
                pe.wait_ge(hid_ready, n + 1)
                for k in range(HC):
                    tr = nc.tensor.transpose(pH[:, k * P:(k + 1) * P], hid[:, u, k * P:(k + 1) * P], eye[:])
                tr.then_inc(hidT_done, 1)

            def tile_slot(n, u, pair, done=SLOT_TILES, last=False):
                times_w1(n, u, pair)
                if done >= 2:
                    times_w2(n - 2, u, pair - 1)
                if done >= 1:
                    transpose_hid(n - 1, 1 - u)
                if not last:
                    transpose_x(n + 1, 1 - u, pair if u == 0 else pair + 1)

            PAIR_TILES = SLOT_TILES // 2
            transpose_x(0, 0, 0)
            pe.wait_ge(w1_loaded, 16 * KC)
            pe.wait_ge(ones_set, 1)
            tile_slot(0, 0, 0, done=0)
            tile_slot(1, 1, 0, done=1)
            pe.wait_ge(w2_loaded, 16 * HC)
            with pe.Fori(1, PAIR_TILES - 1) as pair:
                tile_slot(2 * pair, 0, pair)
                tile_slot(2 * pair + 1, 1, pair)
            tile_slot(SLOT_TILES - 2, 0, PAIR_TILES - 1)
            tile_slot(SLOT_TILES - 1, 1, PAIR_TILES - 1, last=True)
            times_w2(SLOT_TILES - 2, 0, PAIR_TILES - 1)
            transpose_hid(SLOT_TILES - 1, 1)
            times_w2(SLOT_TILES - 1, 1, PAIR_TILES - 1)

        @block.vector
        def _(dve):
            V = nc.vector
            for u in range(2):
                dve.sem_inc(ys_stored[u], 16)
                dve.sem_inc(outs_stored[u], 16)
            dve.sem_inc(term_free, 2 + FIRST_SUMS)
            dve.sem_inc(term_ready, FIRST_SUMS)
            dve.sem_inc(oprod_free, 2)
            V.memset(ones3[:], 1.0).then_inc(ones_set, 1)
            dve.wait_ge(rel_in, 16)
            V.tensor_scalar(rel_neg[:], rel[:], -1.0 / SCALE, None, ALU.mult).then_inc(rel_set, 1)

            def gate_hidden(n, u):
                dve.wait_ge(h_done, n + 1)
                dve.wait_ge(a_ready, n + 1)
                V.tensor_tensor(hid[:, u], act_a[:, u], pB[:, u], ALU.mult).then_inc(hid_ready, 1)

            def pairs(ap):
                return ap.rearrange("p (t r) -> p t r", r=SAMPLES)

            def each_sample(ap):
                return ap.unsqueeze(2).broadcast_to([P, TH, SAMPLES])

            def bends(it):
                dve.wait_ge(s_loaded, 16 * it + 16)
                bend_v = bend[:].rearrange("p j (i h) -> p i j h", h=GH)
                V.tensor_copy(bend_v[:, :, 0], slope[:, :, 0])
                V.tensor_tensor(bend_v[:, :, 1:KNOTS], slope[:, :, 1:KNOTS], slope[:, :, 0:KNOTS - 1],
                                ALU.subtract).then_inc(s_used, 1)

            def term(it, u, j):
                dve.wait_ge(term_free, it * KNOTS + j + 1)
                V.scalar_tensor_tensor(pairs(terms[:, j % 2]), pairs(pos[:, u]), float(j - REACH),
                                       each_sample(bend[:, j]), ALU.max, ALU.mult).then_inc(term_ready, 1)

            def weigh(dst, u, j):
                return V.tensor_tensor(dst.rearrange("p (t d) -> p t d", d=DH),
                                       vw[:, u, j * GD:j * GD + IB * GD].rearrange("p (t d) -> p t d", d=DH),
                                       wgt[:, j].unsqueeze(2).broadcast_to([P, TH, DH]), ALU.mult)

            def weigh_values(it, u, half, j):
                i = j - OWN
                if i == 0:
                    dve.wait_ge(v_loaded[u], 16 * half + 16)
                dve.wait_ge(oprod_free, it * NV + i + 1)
                weigh(oprod[:, (u * NV + i) % 2], u, j).then_inc(oprod_ready, 1)

            def step(it, u, half, first=False, last=False):
                chain = Chain(dve, chain_sem, it * CHAIN)
                tile = 0 if first else tiles_before(it)
                odd = MOE_PER_STEP % 2 if u == 0 and not first else 0
                tiles = FIRST_TILES if first else SLOT_TILES - tile if last else MOE_PER_STEP

                def gate(m):
                    if 0 <= m < tiles:
                        gate_hidden(tile + m, (odd + m) % 2)

                vhalf = half - 1 if u == 0 else half
                dve.wait_ge(term_free, (it + 1) * KNOTS + 2)
                chain.count(V.tensor_reduce(smax[:], pairs(prob[:, u]), AX.X, ALU.max))
                if not last:
                    bends(it + 1)
                chain.wait()
                V.tensor_tensor(pairs(prob[:, u]), pairs(prob[:, u]), each_sample(smax[:]),
                                ALU.subtract).then_inc(shift_ready, 1)
                if not last:
                    dve.wait_ge(s_used, it + 2)
                    dve.wait_ge(pos_set, it + 2)
                for j in range(NJ):
                    if not last and j < KNOTS:
                        term(it + 1, 1 - u, j)
                    if not first and j >= OWN:
                        weigh_values(it - 1, 1 - u, vhalf, j)
                    if j == 0:
                        dve.wait_ge(prob_ready, it + 1)
                        chain(V.tensor_reduce(psum_e[:], pairs(prob[:, u]), AX.X, ALU.add))
                        chain.count(V.reciprocal(psum_e[:], psum_e[:]))
                        continue
                    if j == 1:
                        chain.wait()
                        chain(V.tensor_tensor(pairs(prob[:, u]), pairs(prob[:, u]), each_sample(psum_e[:]), ALU.mult))
                    knot = j - 1
                    jj = knot % GSUM
                    if jj == 0 and knot > 0:
                        chain.wait()
                    ins = V.scalar_tensor_tensor(gterms[:, jj], pos[:, u], float(knot - REACH), prob[:, u], ALU.max, ALU.mult)
                    if jj == GSUM - 1:
                        chain.count(ins)
                    if j % 2 == 0:
                        if first:
                            gate((j - NJ + 1) // 2 + tiles - 1)
                        else:
                            gate(j // 2 - 1)
                    if jj == GSUM - 1:
                        chain.wait()
                        chain.count(V.tensor_reduce(
                            G[:, knot - jj:knot + 1], gterms[:].rearrange("p j (t r) -> p j t r", r=SAMPLES), AX.X, ALU.add))
                if not first:
                    gate(NJ // 2)
                chain.wait()
                V.tensor_tensor(gslope[:, 1:KNOTS], G[:, 1:KNOTS], G[:, 0:KNOTS - 1], ALU.subtract).then_inc(step_free, 1)
                dve.wait_ge(step_free, it + 1)
                chain(V.tensor_scalar(gslope[:, KNOTS], G[:, KNOTS - 1], -1.0, float(REACH), ALU.mult, ALU.add))
                if not first:
                    dve.wait_ge(own_done, it * OWN_STEPS)
                chain(V.tensor_tensor(wgt[:], gslope[:, 1:KNOTS + 2], gslope[:, 0:KNOTS + 1], ALU.subtract))
                if not last:
                    assert chain.n == CHAIN, chain.n

            V.memset(gslope[:, 0], 0.0)
            V.memset(gslope[:, KNOTS + 1], 1.0)
            bends(0)
            dve.wait_ge(s_used, 1)
            dve.wait_ge(pos_set, 1)
            sums = Chain(dve, first_chain)
            for j in range(FIRST_SUMS, KNOTS):
                term(0, 0, j)
                i = j - FIRST_SUMS
                if i < FIRST_SUMS:
                    if i > 1:
                        sums.wait()
                    sums.count(V.scalar_tensor_tensor(pairs(gterms[:, min(i, 1)]), pairs(pos[:, 0]), float(i - REACH),
                                                      each_sample(bend[:, i]), ALU.max, ALU.mult))
                    if i > 0:
                        sums.wait()
                        sums.count(V.tensor_tensor(gterms[:, 0], gterms[:, 0], gterms[:, 1], ALU.add))
            sums.wait()
            dve.wait_ge(term_free, KNOTS + 2)
            sums(V.tensor_tensor(prob[:, 0], prob[:, 0], gterms[:, 0], ALU.add))
            first_step, two_steps, last_step = run_steps(step)
            first_step()
            with dve.Fori(0, STEPS // 2 - 1) as n:
                two_steps(n)
            last_step()
            dve.wait_ge(v_loaded[1], 16 * (STEPS // 2))
            ends = Chain(dve, last_chain)
            part = terms[:].rearrange("p a b -> p (a b)")[:, 0:TH * DH]
            more = gterms[:].rearrange("p a b -> p (a b)")[:, 0:TH * DH]
            for i in range(NJ - SHARED):
                if OWN + i < SHARED:
                    weigh_values(LAST, 1, LAST // 2, OWN + i)
                ends(weigh(part if i == 0 else more, 1, SHARED + i))
                if i > 0:
                    ends(V.tensor_tensor(part, part, more, ALU.add))
            dve.wait_ge(oprod_free, LAST * NV + SHARED - OWN + 2)
            V.tensor_tensor(outs[:, 1], outs[:, 1], part, ALU.add).then_inc(last_sum, 1)


def finish_block(nc, io, dram, keep):
    with ExitStack() as ctx:
        def sb(name, shape, dt=F32):
            return ctx.enter_context(nc.sbuf_tensor(name, shape, dt))

        def ps(name, shape, dt=F32):
            return ctx.enter_context(nc.psum_tensor(name, shape, dt))

        def sem(name):
            return ctx.enter_context(nc.semaphore(name))

        wo = sb("wo", [P, KC, D])
        bo = sb("bo", [P, D])
        xr = sb("xr", [P, FSLOTS, D])
        at = sb("at", [P, FSLOTS, D])
        yk = sb("yk", [P, FSLOTS, TOPK, D])
        idx = sb("idx4", [P, FSLOTS, TOPK], U32)
        proj = sb("proj", [P, FSLOTS, D])
        atT = sb("atT", [P, 2, KC, P])
        moe = sb("moe", [P, 2, D])
        gate = sb("gate4", [P, 2, D])
        pT = ps("pT4", [P, 2, 512])
        pO = ps("pO4", [P, 2, 512])

        weights_in = sem("weights_in4")
        x_loaded = [sem(f"x_loaded4{u}") for u in range(FSLOTS)]
        y_loaded = [sem(f"y_loaded4{u}") for u in range(FSLOTS)]
        idx_set = sem("idx_set4")
        go = sem("go4")
        atT_done = sem("atT_done")
        atT_ready = sem("atT_ready")
        proj_done = sem("proj_done")
        proj_read = sem("proj_read")
        moe_ready = sem("moe_ready")
        gate_ready = sem("gate_ready")
        moe_half = sem("moe_half")
        gated = sem("gated")
        out_ready = sem("out_ready")
        out_stored = [sem(f"out_stored{u}") for u in range(FSLOTS)]
        block = ctx.enter_context(nc.Block())
        ROUNDS = TILES // FSLOTS

        def pipeline(eng, ahead, body):
            def round_of(t, last=False):
                for u in range(FSLOTS):
                    if u < FSLOTS - 1:
                        ahead(t, u + 1)
                    elif not last:
                        ahead(t + 1, 0)
                    body(t, u, last)

            ahead(0, 0)
            with eng.Fori(0, ROUNDS - 1) as t:
                round_of(t)
            round_of(ROUNDS - 1, last=True)

        @block.sync
        def _(sp):
            def load(t, u):
                row = (t * FSLOTS + u) * P
                sp.dma_start(at[:, u], dram["attn"][ds(row, P), :]).then_inc(x_loaded[u], 16)
                sp.dma_start(xr[:, u], io["x"][ds(row, P), :]).then_inc(x_loaded[u], 16)

            def store(t, u):
                sp.wait_ge(out_ready, t * FSLOTS + u + 1)
                sp.dma_start(io["out"][ds((t * FSLOTS + u) * P, P), :], proj[:, u]).then_inc(out_stored[u], 16)

            load(0, 0)
            sp.dma_start(wo[:], io["w_oT"].rearrange("(k p) n -> p k n", p=P)).then_inc(weights_in, 16)
            sp.dma_start(bo[:], io["b_o"].partition_broadcast(P)).then_inc(weights_in, 16)
            for u in range(1, FSLOTS):
                load(0, u)
            with sp.Fori(0, ROUNDS - 1) as t:
                for u in range(FSLOTS):
                    store(t, u)
                    load(t + 1, u)
            for u in range(FSLOTS):
                store(ROUNDS - 1, u)
            for u in range(FSLOTS):
                sp.wait_ge(out_stored[u], 16 * (ROUNDS + 1))

        @block.gpsimd
        def _(pool):
            def fetch(t, u):
                pool.wait_ge(idx_set, t * FSLOTS + u + 1)
                pool.sem_inc(go, 1)
                for k in range(TOPK):
                    nc.gpsimd.indirect_dma_start(
                        out=yk[:, u, k], out_offset=None, in_=dram["ys"],
                        in_offset=bass.IndirectOffsetOnAxis(ap=idx[:, u, k:k + 1], axis=0)).then_inc(y_loaded[u], 16)

            with pool.Fori(0, ROUNDS) as t:
                for u in range(FSLOTS):
                    fetch(t, u)

        @block.tensor
        def _(pe):
            def transpose(t, u):
                n = t * FSLOTS + u
                pe.wait_ge(x_loaded[u], 32 * t + 32)
                pe.wait_ge(atT_ready, n + 1)
                for k in range(KC):
                    tr = nc.tensor.transpose(pT[:, u % 2, k * P:(k + 1) * P], at[:, u, k * P:(k + 1) * P], keep["ident"][:])
                tr.then_inc(atT_done, 1)

            def project(t, u, last):
                n = t * FSLOTS + u
                pe.wait_ge(atT_ready, n + 3)
                pe.wait_ge(proj_read, n + 1)
                for k in range(KC):
                    mm = nc.tensor.matmul(pO[:, u % 2, 0:D], atT[:, u % 2, k], wo[:, k], start=(k == 0), stop=(k == KC - 1))
                mm.then_inc(proj_done, 1)

            pe.wait_ge(weights_in, 32)
            pipeline(pe, transpose, project)

        @block.scalar
        def _(act):
            def evacuate(t, u):
                act.wait_ge(atT_done, t * FSLOTS + u + 1)
                nc.scalar.activation(atT[:, u % 2].rearrange("p k t -> p (k t)"), pT[:, u % 2, 0:D],
                                     ACT.Identity).then_inc(atT_ready, 1)

            def silu(t, u, last):
                act.wait_ge(moe_ready, t * FSLOTS + u + 1)
                nc.scalar.activation(gate[:, u % 2], moe[:, u % 2], ACT.Silu).then_inc(gate_ready, 1)

            pipeline(act, evacuate, silu)

        @block.vector
        def _(dve):
            V = nc.vector
            for u in range(FSLOTS):
                dve.sem_inc(out_stored[u], 16)
            dve.sem_inc(atT_ready, 2)
            dve.sem_inc(proj_read, 2)

            def mix_experts(t, u):
                n = t * FSLOTS + u
                dve.wait_ge(y_loaded[u], 16 * TOPK * (t + 1))
                V.tensor_scalar(moe[:, u % 2], yk[:, u, 0], keep["gate"][:, 0, ds(n, 1)], None, ALU.mult).then_inc(moe_half, 1)
                dve.wait_ge(moe_half, n + 1)
                V.scalar_tensor_tensor(moe[:, u % 2], yk[:, u, 1], keep["gate"][:, 1, ds(n, 1)], moe[:, u % 2],
                                       ALU.mult, ALU.add).then_inc(moe_ready, 1)

            def index(t, u):
                V.tensor_copy(idx[:, u], keep["slot"][:, :, ds(t * FSLOTS + u, 1)].rearrange("p k o -> p (k o)")).then_inc(idx_set, 1)

            def finish(t, u, last):
                n = t * FSLOTS + u
                if not last:
                    index(t + 1, u)
                dve.wait_ge(proj_done, n + 1)
                dve.wait_ge(out_stored[u], 16 * t + 16)
                V.tensor_tensor(proj[:, u], pO[:, u % 2, 0:D], bo[:], ALU.add).then_inc(proj_read, 1)
                dve.wait_ge(proj_read, n + 3)
                dve.wait_ge(gate_ready, n + 1)
                V.tensor_tensor(proj[:, u], proj[:, u], gate[:, u % 2], ALU.mult).then_inc(gated, 1)
                dve.wait_ge(gated, n + 1)
                V.tensor_tensor(proj[:, u], proj[:, u], xr[:, u], ALU.add).then_inc(out_ready, 1)

            for u in range(FSLOTS):
                index(0, u)
            dve.wait_ge(weights_in, 32)
            pipeline(dve, mix_experts, finish)


def build(nc, io):
    dram = {
        "xn": nc.dram_tensor("xn_rows", [TOKENS, D], F32).ap(),
        "S": nc.dram_tensor("S_rows", [HG, TOKENS, S_PITCH], F32).ap(),
        "v": nc.dram_tensor("v_rows", [HG, TOKENS + 2 * REACH, GD], F32).ap(),
        "pos": nc.dram_tensor("pos_rows", [TOKENS, HR], F32).ap(),
        "xs": nc.dram_tensor("xs_slots", [SLOTS, D], F32).ap(),
        "ys": nc.dram_tensor("ys_slots", [SLOTS, D], F32).ap(),
        "bias": nc.dram_tensor("bias_parts", [NB, EXPERTS, 2 * HID + D], BF16).ap(),
        "attn": nc.dram_tensor("attn_rows", [TOKENS, D], F32).ap(),
    }
    with ExitStack() as ctx:
        def sb(name, shape, dt=F32):
            return ctx.enter_context(nc.sbuf_tensor(name, shape, dt))

        keep = {
            "ident": sb("ident", [P, P]),
            "gate": sb("gate", [P, TOPK, TILES]),
            "slot": sb("slot_u", [P, TOPK, TILES], U32),
            "tile_exp": sb("tile_exp_i", [1, SLOT_TILES], I32),
        }
        with nc.sbuf_tensor("scores", [P, TILES, EXPERTS], F32) as scores, \
                nc.sbuf_tensor("qT", [P, KC, BATCH * (SEQ + 2)], F32) as qT, \
                nc.sbuf_tensor("kT", [P, KC, TOKENS + 1 + 2 * REACH], F32) as kT:
            keep.update(scores=scores, qT=qT, kT=kT)
            project_block(nc, io, dram, keep)
            route_block(nc, io, dram, keep)
        mix_block(nc, io, dram, keep)
        finish_block(nc, io, dram, keep)


def kernel(**inputs):
    import concourse.bacc as bacc
    from concourse.bass_utils import run_bass_kernel_spmd

    a = {k: np.asarray(v) for k, v in inputs.items()}
    t = np.ascontiguousarray
    arrays = {
        "x": a["L0_attn_x"].reshape(TOKENS, D),
        "w_qkvT": t(np.concatenate([a["L0_attn_wq"], a["L0_attn_wk"], a["L0_attn_wv"]], 0).T),
        "b_qkv": np.concatenate([a["L0_attn_bq"], a["L0_attn_bk"], a["L0_attn_bv"]]),
        "w_oT": t(a["L0_attn_wo"].T),
        "b_o": a["L0_attn_bo"],
        "dw_w": a["L0_attn_dw_w"].reshape(D, 3),
        "dw_b": a["L0_attn_dw_b"],
        "pw_wT": t(a["L0_attn_pw_w"].T),
        "pw_b": a["L0_attn_pw_b"],
        "rel_scale": a["L0_attn_rel_scale"].reshape(1),
        "w_rT": t(a["L0_ffn_Wr"].T),
        "b_r": a["L0_ffn_br"],
        "w_l1": a["L0_ffn_Wl1"],
        "b_l1": a["L0_ffn_bl1"],
        "w_l2": a["L0_ffn_Wl2"],
        "b_l2": a["L0_ffn_bl2"],
        "sel_bias": a["L0_ffn_biases_N"],
    }
    nc = bacc.Bacc("TRN2", target_bir_lowering=False, num_devices=1)
    io = {k: nc.dram_tensor(f"in_{k}", v.shape, F32, kind="ExternalInput").ap() for k, v in arrays.items()}
    io["out"] = nc.dram_tensor("out", (TOKENS, D), F32, kind="ExternalOutput").ap()
    build(nc, io)
    r = run_bass_kernel_spmd(nc, [{f"in_{k}": t(v) for k, v in arrays.items()}], core_ids=[0])
    return r.results[0]["out"].reshape(BATCH, SEQ, D)
```
